# Optimizing a Trainium2 kernel written in Bass

```python
import numpy as np
import jax
import jax.numpy as jnp

def _softmax(x, axis=-1):
    return jax.nn.softmax(x, axis=axis)

def _gelu(x):
    return jax.nn.gelu(x, approximate=True)

def _silu(x):
    return jax.nn.silu(x)

def _sigmoid(x):
    return jax.nn.sigmoid(x)

def _layernorm(x, axis=-1, eps=1e-05):
    m = jnp.mean(x, axis=axis, keepdims=True)
    v = jnp.var(x, axis=axis, keepdims=True)
    return (x - m) / jnp.sqrt(v + eps)

def _scatter_add(tgt, idx, src, axis=0):
    return tgt.at[idx].add(src)

def _segment_sum(src, seg, n):
    return jax.ops.segment_sum(src, seg, n)
kernel_name = 'mk_early_fusion_d1_tok_img768_r4_8f9491'

def setup_inputs(seed: int=0):
    np.random.seed(seed)
    _w = jnp.asarray

    def _rec_inputs():
        import jax
        import jax.numpy as jnp
        _rk = jax.random.key(seed)
        x = -9.30917e-05 + 1.0002 * jax.random.normal(jax.random.fold_in(_rk, 1), (32, 3, 224, 224), jnp.float32)
        txt = -0.000192023 + 1.00029 * jax.random.normal(jax.random.fold_in(_rk, 2), (32, 128, 192), jnp.float32)
        return (x, txt)
    x, txt = _rec_inputs()

    def _L0_tok_setup():
        import jax, jax.numpy as jnp
        import numpy as np
        PATCH = 16
        EPS = 1e-05

        def _shift(x, pad_spec):
            l, r, t, b = pad_spec
            H, W = (x.shape[2], x.shape[3])
            xp = jnp.pad(x, ((0, 0), (0, 0), (max(t, 0), max(b, 0)), (max(l, 0), max(r, 0))))
            h0 = -t if t < 0 else 0
            w0 = -l if l < 0 else 0
            return xp[:, :, h0:h0 + H, w0:w0 + W]
        key = jax.random.key(seed)
        k1, k2 = jax.random.split(key)
        B, C, H, Wd = (32, 3, 224, 224)
        patch_dim = PATCH * PATCH * 5 * C
        dim = 192
        x = jax.random.normal(k1, (B, C, H, Wd), dtype=jnp.float32)
        ln_gamma = jnp.ones((patch_dim,), dtype=jnp.float32)
        ln_beta = jnp.zeros((patch_dim,), dtype=jnp.float32)
        W = jax.random.normal(k2, (patch_dim, dim), dtype=jnp.float32) * patch_dim ** (-0.5)
        b = jnp.zeros((dim,), dtype=jnp.float32)
        return {'x': x, 'ln_gamma': ln_gamma, 'ln_beta': ln_beta, 'W': W, 'b': b}
    _L0_tok_all = _L0_tok_setup()
    _L0_tok_in = {k: v for k, v in _L0_tok_all.items() if k in ('ln_gamma', 'ln_beta', 'W', 'b')}
    del _L0_tok_all

    def _L0_attn_setup():
        import jax, jax.numpy as jnp
        import numpy as np
        N_HEAD = 12
        WINDOW = 64
        key = jax.random.key(seed)
        k1, k2, k3 = jax.random.split(key, 3)
        B, T, C = (4, 512, 192)
        x = jax.random.normal(k1, (B, T, C), dtype=jnp.float32)
        W_attn = jax.random.normal(k2, (C, 3 * C), dtype=jnp.float32) * 0.02
        b_attn = jnp.zeros((3 * C,), dtype=jnp.float32)
        W_proj = jax.random.normal(k3, (C, C), dtype=jnp.float32) * 0.02
        b_proj = jnp.zeros((C,), dtype=jnp.float32)
        return {'x': x, 'W_attn': W_attn, 'b_attn': b_attn, 'W_proj': W_proj, 'b_proj': b_proj}
    _L0_attn_all = _L0_attn_setup()
    _L0_attn_in = {k: v for k, v in _L0_attn_all.items() if k in ('W_attn', 'b_attn', 'W_proj', 'b_proj')}
    del _L0_attn_all

    def _L0_ffn_setup():
        import jax, jax.numpy as jnp
        import numpy as np
        CAPACITY_FACTOR = 1.25
        key = jax.random.key(seed)
        ks = jax.random.split(key, 5)
        B, S, D, F, E = (8, 512, 192, 768, 8)
        return {'x': jax.random.normal(ks[0], (B, S, D), jnp.float32), 'switch_w': jax.random.normal(ks[1], (D, E), jnp.float32) * 0.02, 'switch_b': jnp.zeros((E,), jnp.float32), 'w1': jax.random.normal(ks[2], (E, D, F), jnp.float32) * 0.02, 'b1': jnp.zeros((E, F), jnp.float32), 'w2': jax.random.normal(ks[3], (E, F, D), jnp.float32) * 0.02, 'b2': jnp.zeros((E, D), jnp.float32)}
    _L0_ffn_all = _L0_ffn_setup()
    _L0_ffn_in = {k: v for k, v in _L0_ffn_all.items() if k in ('switch_w', 'switch_b', 'w1', 'b1', 'w2', 'b2')}
    del _L0_ffn_all
    return {'x': x, 'txt': txt, 'L0_tok_ln_gamma': _L0_tok_in['ln_gamma'], 'L0_tok_ln_beta': _L0_tok_in['ln_beta'], 'L0_tok_W': _L0_tok_in['W'], 'L0_tok_b': _L0_tok_in['b'], 'L0_attn_W_attn': _L0_attn_in['W_attn'], 'L0_attn_b_attn': _L0_attn_in['b_attn'], 'L0_attn_W_proj': _L0_attn_in['W_proj'], 'L0_attn_b_proj': _L0_attn_in['b_proj'], 'L0_ffn_switch_w': _L0_ffn_in['switch_w'], 'L0_ffn_switch_b': _L0_ffn_in['switch_b'], 'L0_ffn_w1': _L0_ffn_in['w1'], 'L0_ffn_b1': _L0_ffn_in['b1'], 'L0_ffn_w2': _L0_ffn_in['w2'], 'L0_ffn_b2': _L0_ffn_in['b2']}

def reference(x, txt, L0_tok_ln_gamma, L0_tok_ln_beta, L0_tok_W, L0_tok_b, L0_attn_W_attn, L0_attn_b_attn, L0_attn_W_proj, L0_attn_b_proj, L0_ffn_switch_w, L0_ffn_switch_b, L0_ffn_w1, L0_ffn_b1, L0_ffn_w2, L0_ffn_b2):
    import jax
    import jax.numpy as jnp

    def _L0_tok_ref(x, ln_gamma, ln_beta, W, b):
        import jax, jax.numpy as jnp
        import numpy as np
        PATCH = 16
        EPS = 1e-05

        def _shift(x, pad_spec):
            l, r, t, b = pad_spec
            H, W = (x.shape[2], x.shape[3])
            xp = jnp.pad(x, ((0, 0), (0, 0), (max(t, 0), max(b, 0)), (max(l, 0), max(r, 0))))
            h0 = -t if t < 0 else 0
            w0 = -l if l < 0 else 0
            return xp[:, :, h0:h0 + H, w0:w0 + W]
        shifts = [(1, -1, 0, 0), (-1, 1, 0, 0), (0, 0, 1, -1), (0, 0, -1, 1)]
        xs = jnp.concatenate([x] + [_shift(x, s) for s in shifts], axis=1)
        B, C5, H, Wd = xs.shape
        h, w = (H // PATCH, Wd // PATCH)
        t = xs.reshape(B, C5, h, PATCH, w, PATCH)
        t = t.transpose(0, 2, 4, 3, 5, 1)
        t = t.reshape(B, h * w, PATCH * PATCH * C5)
        mu = jnp.mean(t, axis=-1, keepdims=True)
        var = jnp.var(t, axis=-1, keepdims=True)
        tn = (t - mu) * jax.lax.rsqrt(var + EPS) * ln_gamma + ln_beta
        return jnp.einsum('bnp,pd->bnd', tn, W) + b

    def _L0_attn_ref(x, W_attn, b_attn, W_proj, b_proj):
        import jax, jax.numpy as jnp
        import numpy as np
        N_HEAD = 12
        WINDOW = 64
        B, T, C = x.shape
        H = N_HEAD
        hd = C // H
        qkv = x @ W_attn + b_attn
        q, k, v = jnp.split(qkv, 3, axis=-1)
        q = q.reshape(B, T, H, hd).transpose(0, 2, 1, 3)
        k = k.reshape(B, T, H, hd).transpose(0, 2, 1, 3)
        v = v.reshape(B, T, H, hd).transpose(0, 2, 1, 3)
        att = jnp.einsum('bhqd,bhkd->bhqk', q, k) * (1.0 / np.sqrt(hd).astype(np.float32))
        i = jnp.arange(T)[:, None]
        j = jnp.arange(T)[None, :]
        keep = (j <= i) & (j > i - WINDOW)
        att = jnp.where(keep[None, None], att, -jnp.inf)
        att = jax.nn.softmax(att, axis=-1)
        y = jnp.einsum('bhqk,bhkd->bhqd', att, v)
        y = y.transpose(0, 2, 1, 3).reshape(B, T, C)
        return y @ W_proj + b_proj

    def _L0_ffn_ref(x, switch_w, switch_b, w1, b1, w2, b2):
        import jax, jax.numpy as jnp
        import numpy as np
        CAPACITY_FACTOR = 1.25
        B, S, D = x.shape
        E = w1.shape[0]
        xf = x.reshape(-1, D)
        N = xf.shape[0]
        capacity = int(CAPACITY_FACTOR * N / E)
        probs = jax.nn.softmax(xf @ switch_w + switch_b, axis=-1)
        prob_max = jnp.max(probs, axis=-1)
        routes = jnp.argmax(probs, axis=-1)
        sort_idx = jnp.lexsort((-prob_max, routes))
        counts = jnp.bincount(routes, length=E)
        starts = jnp.concatenate([jnp.zeros((1,), counts.dtype), jnp.cumsum(counts)[:-1]])
        rank_sorted = jnp.arange(N) - starts[routes[sort_idx]]
        rank = jnp.zeros((N,), jnp.int32).at[sort_idx].set(rank_sorted.astype(jnp.int32))
        keep = rank < capacity
        dest_e = jnp.where(keep, routes, E)
        dest_c = jnp.where(keep, rank, 0)
        buf = jnp.zeros((E + 1, capacity, D), xf.dtype).at[dest_e, dest_c].set(xf)
        h = jax.nn.gelu(jnp.einsum('ecd,edf->ecf', buf[:E], w1) + b1[:, None, :], approximate=False)
        o = jnp.einsum('ecf,efd->ecd', h, w2) + b2[:, None, :]
        y_exp = o[routes, dest_c]
        y = jnp.where(keep[:, None], y_exp, xf)
        out = y * prob_max[:, None]
        return out.reshape(B, S, D)
    h = _L0_tok_ref(x, L0_tok_ln_gamma, L0_tok_ln_beta, L0_tok_W, L0_tok_b)
    h = jnp.concatenate([h, txt], axis=1)
    h = h + _L0_attn_ref(_layernorm(h, axis=-1), L0_attn_W_attn, L0_attn_b_attn, L0_attn_W_proj, L0_attn_b_proj)
    h = h + _L0_ffn_ref(_layernorm(h, axis=-1), L0_ffn_switch_w, L0_ffn_switch_b, L0_ffn_w1, L0_ffn_b1, L0_ffn_w2, L0_ffn_b2)
    return h

_drawn_inputs = setup_inputs


def setup_inputs(seed=0):
    import zlib

    import numpy as np

    out = dict(_drawn_inputs(seed))
    spreads = {'L0_tok_ln_gamma': (1.0, 0.2),
     'L0_tok_ln_beta': (0.0, 0.1),
     'L0_tok_b': (0.0, 0.1),
     'L0_attn_b_attn': (0.0, 0.1),
     'L0_attn_b_proj': (0.0, 0.1),
     'L0_ffn_switch_b': (0.0, 0.1),
     'L0_ffn_b1': (0.0, 0.8),
     'L0_ffn_b2': (0.0, 0.487)}
    factors = {'L0_attn_W_attn': 3.077, 'L0_ffn_w1': 4.227, 'L0_ffn_w2': 3.917}
    for name, (base, spread) in spreads.items():
        noise = np.random.default_rng([zlib.crc32(name.encode()), seed]).standard_normal(out[name].shape)
        drawn = base * np.exp(spread * noise) if base else spread * noise
        out[name] = jnp.asarray(drawn.astype(out[name].dtype))
    for name, factor in factors.items():
        out[name] = (out[name] * factor).astype(out[name].dtype)
    return out
```

```python
from contextlib import ExitStack

import concourse.bass as bass
from concourse import mybir

F32 = mybir.dt.float32
BF16 = mybir.dt.bfloat16
I32 = mybir.dt.int32
ALU = mybir.AluOpType
ACT = mybir.ActivationFunctionType
AX_X = mybir.AxisListType.X

D = 192
HC = D // 2
HEADS, HD = 12, 16
HG = HEADS // 2
EXPERTS, FF = 8, 768
FCH = FF // 128
PIX, PCH = 120, 8
NPATCH, NTXT = 196, 128
T = NPATCH + NTXT
ROWS = [NPATCH // 2, NPATCH // 2, NTXT]
OFF = [0, ROWS[0], 2 * ROWS[0]]
HT = ROWS[0]
WIN = 64
QB = 54
NBLK = T // QB
KW = QB + WIN - 1
PAD = WIN - 1
ORDER = [0, 3, 1, 4, 2, 5]
PATCH_DIM = 16 * 16 * 15
EPS = 1e-5
NEG = -1e30
RW = D + 4
SKIP = 1000000
TAU_STEPS, IDX_STEPS = 27, 14

C_ID, C_UT, C_MQ = 0, 128, 256
C_MT = C_MQ + 3 * KW
C_VALID = C_MT + 3 * QB
C_TOK = C_VALID + 3
C_EOFF = C_TOK + 3
C_W8 = C_EOFF + EXPERTS
C_EI = C_W8 + EXPERTS
C_CNT = C_EI + EXPERTS
C_KI = C_CNT + PCH


def tiles_of(tokens):
    full = (tokens + EXPERTS * 127) // 128
    return -(-full // 4) * 4


def build(nc, x, txt, wtok, gam, bet, btok, wattn, battn, wproj, bproj, wsw, bsw, w1, b1, w2, b2, const, out):
    NB = x.shape[0]
    N = NB * T
    CAP = int(1.25 * N / EXPERTS)
    CAPR = N + 128
    DUMMY = EXPERTS * CAPR
    NT = tiles_of(N)
    NTP = NT + 4
    TILES = 3 * NB
    CW = C_KI + NTP

    with ExitStack() as ctx:
        def sb(name, shape, dt=F32):
            return ctx.enter_context(nc.sbuf_tensor(name, shape, dt))

        def sem(name):
            return ctx.enter_context(nc.semaphore(name))

        cst = sb("cst", [128, CW])
        ident = cst[:, C_ID:C_ID + 128]
        identb = sb("identb", [128, 128], BF16)
        utrib = sb("utrib", [128, 128], BF16)
        mqb = sb("mqb", [128, 3, KW], BF16)
        mtb = sb("mtb", [128, 3, QB], BF16)
        ones = sb("ones", [128, 128])
        onesb = sb("onesb", [128, 128], BF16)
        neghalf = sb("neghalf", [128, 3])
        epsc = sb("epsc", [128, 3])
        pause = sb("pause", [128, 1])
        gpause = sb("gpause", [128, 1])
        W1 = sb("W1", [HC + 1, 2, EXPERTS, FF])
        W2 = sb("W2", [128, EXPERTS, FCH, D])
        B2 = sb("B2", [128, EXPERTS, D])
        WS = W2[:, :, :, :].rearrange("p e f d -> p (e f d)")[0:PIX, 0:5 * PCH * D].rearrange(
            "p (s k d) -> p s k d", s=5, k=PCH)
        GM = sb("GM", [PIX, 5, PCH])
        BT = sb("BT", [PIX, 5, PCH])
        scratch = sb("scratch", [128, PCH * D])
        WTMP = scratch[0:PIX, :].rearrange("p (k d) -> p k d", k=PCH)
        WE = sb("WE", [PIX, PCH, D + 2])
        btrow = sb("btrow", [1, D])
        csum = sb("csum", [HT, D])
        tbias = sb("tbias", [HT, D])
        WA = sb("WA", [HC + 1, 2, 3 * D])
        WP = sb("WP", [HC + 1, 2, D])
        SW = sb("SW", [HC + 1, 2, EXPERTS])

        img = sb("img", [PIX, PCH, NPATCH])
        sq = sb("sq", [PIX, PCH, NPATCH])
        H = sb("H", [128, 3, D])
        R = sb("R", [128, 3, D])
        TMP = sb("TMP", [HT, 2, D])
        negmu = sb("negmu", [HT, 2, 1])
        msq = sb("msq", [HT, 2, 1])
        tvar = sb("tvar", [HT, 2, 1])
        tve = sb("tve", [HT, 2, 1])
        trstd = sb("trstd", [HT, 2, 1])
        BN = sb("BN", [128, 3, 6])
        MV = sb("MV", [128, 3, 2])
        ve1 = sb("ve1", [128, 3])
        rstd1 = sb("rstd1", [128, 3])
        XN = sb("XN", [128, 3, D])
        XT = sb("XT", [HC + 1, 2, PAD + T])
        QS = sb("QS", [HC, 2, T])
        QSb = sb("QSb", [HC, 2, T], BF16)
        KT = sb("KT", [HC + 1, 2, PAD + T])
        KTb = sb("KTb", [HC, 2, PAD + T], BF16)
        arena = sb("arena", [128, HEADS * (T + 10)])
        QD = arena[0:HC + 1, :].rearrange("p (h t) -> p h t", h=HEADS)
        QDb = sb("QDb", [HC, HEADS, T + 10], BF16)
        V = sb("V", [KW, NBLK, HEADS, HD + 1])
        M = sb("M", [128, 3, HEADS])
        mT = sb("mT", [HEADS, T])

        PR = sb("PR", [KW, 2, 2, HG * QB])
        rec = sb("rec", [128, HEADS])
        ysb = sb("ysb", [128, D])
        YT = sb("YT", [HC + 1, 2, T])
        ROW = sb("ROW", [128, 3, RW])
        BN2 = sb("BN2", [128, 3, 6])
        ve2 = sb("ve2", [128, 3])
        XN2 = sb("XN2", [128, 3, D])
        XT2 = sb("XT2", [HC + 1, 2, T])
        LM = sb("LM", [128, 3])
        LS = sb("LS", [128, 3, EXPERTS])
        EL = sb("EL", [128, 3, EXPERTS])
        ES = sb("ES", [128, 3])
        EQ = sb("EQ", [128, 3, EXPERTS])
        SC = sb("SC", [128, 3, EXPERTS])
        MX = sb("MX", [128, 3])
        OH = sb("OH", [128, 3, EXPERTS])
        OHb = sb("OHb", [128, 3, EXPERTS], BF16)
        POS = sb("POS", [128, 3, EXPERTS])
        SLF = sb("SLF", [128, 3])
        SLI = sb("SLI", [128, 3], I32)
        BASE = sb("BASE", [128, EXPERTS])
        TK = sb("TK", [128, 3])
        PME = sb("PME", [128, TILES, EXPERTS])

        GE = sb("GE", [128, max(TILES, NTP), EXPERTS])[:, 0:TILES, :]
        KEY = sb("KEY", [128, max(TILES, NTP), EXPERTS])[:, 0:TILES, :]
        TIDX = sb("TIDX", [128, TILES])
        MID = sb("MID", [128, EXPERTS])
        STEP = sb("STEP", [128, EXPERTS])
        CN = sb("CN", [128, EXPERTS])
        CNb = sb("CNb", [128, EXPERTS], BF16)
        INC = sb("INC", [128, EXPERTS])
        TAU = sb("TAU", [128, EXPERTS])
        IDX = sb("IDX", [128, EXPERTS])
        CI = sb("CI", [128, EXPERTS], I32)
        CI2 = sb("CI2", [128, EXPERTS], I32)
        CNTI = sb("CNTI", [128, EXPERTS], I32)
        NTE = sb("NTE", [128, EXPERTS])
        FI = sb("FI", [1, EXPERTS])
        FE = sb("FE", [1, EXPERTS])
        AE = sb("AE", [1, EXPERTS])
        IN1 = sb("IN1", [1, NTP, EXPERTS]) if NTP > TILES else GE[0:1, 0:NTP, :]
        IN2 = sb("IN2", [1, NTP, EXPERTS]) if NTP > TILES else KEY[0:1, 0:NTP, :]
        IN3 = scratch[0:1, 0:NTP * EXPERTS].rearrange("p (n e) -> p n e", e=EXPERTS)
        TBF = sb("TBF", [1, 2, NTP])
        TBI = sb("TBI", [1, 2, NTP], I32)
        ZR = sb("ZR", [128, RW])

        RT = scratch[:, 0:4 * RW].rearrange("p (u d) -> p u d", u=4)
        XM = arena[:, 0:4 * D].rearrange("p (u d) -> p u d", u=4)
        OT = arena[:, 4 * D:8 * D].rearrange("p (u d) -> p u d", u=4)
        HS = arena[:, 8 * D:8 * D + FF]
        HTs = arena[:, 8 * D + FF:8 * D + 2 * FF].rearrange("p (f n) -> p f n", f=FCH)
        XMT = XT2[:, :, :].rearrange("p c t -> p (c t)")[:, 0:512].rearrange("p (v c n) -> p v c n", v=2, c=2)
        Y1 = scratch[:, 4 * RW:4 * RW + D]
        Y2 = scratch[:, 4 * RW + D:4 * RW + 2 * D]
        ceq = sb("ceq", [128, 1])
        clt = sb("clt", [128, 1])
        ckp = sb("ckp", [128, 1])
        c1 = sb("c1", [128, 1])
        c2 = sb("c2", [128, 1])
        OI = sb("OI", [128, 4], I32)

        ST = ctx.enter_context(nc.psum_tensor("ST", [128, 4, 512], F32))
        Y = ctx.enter_context(nc.psum_tensor("Y", [128, 512], F32))
        G = ctx.enter_context(nc.psum_tensor("G", [128, 3, 512], F32))

        XS = nc.dram_tensor("dispatched", [DUMMY + 128, RW], F32, kind="Internal").ap()

        s_set = sem("s_set")
        s_tokw = sem("s_tokw")
        s_exp = sem("s_exp")
        s_img = sem("s_img")
        s_txt = sem("s_txt")
        s_qd = sem("s_qd")
        s_qdb = sem("s_qdb")
        s_mrow = sem("s_mrow")
        s_scat = sem("s_scat")
        p_set = sem("p_set")
        p_tok = sem("p_tok")
        p_xt = sem("p_xt")
        p_qkv = sem("p_qkv")
        p_st = sem("p_st")
        p_pv = sem("p_pv")
        p_yt = sem("p_yt")
        p_proj = sem("p_proj")
        p_smax = sem("p_smax")
        p_lt = sem("p_lt")
        p_log = sem("p_log")
        p_mt = sem("p_mt")
        p_pref = sem("p_pref")
        p_cnt = sem("p_cnt")
        p_mx = sem("p_mx")
        p_l1 = sem("p_l1")
        p_ht = sem("p_ht")
        p_l2 = sem("p_l2")
        a_sq = sem("a_sq")
        a_xt = sem("a_xt")
        a_qk = sem("a_qk")
        a_v = sem("a_v")
        a_exp = sem("a_exp")
        a_yt = sem("a_yt")
        a_r = sem("a_r")
        a_lt = sem("a_lt")
        a_el = sem("a_el")
        a_mx = sem("a_mx")
        a_gelu = sem("a_gelu")
        d_set = sem("d_set")
        d_we = sem("d_we")
        d_tvar = sem("d_tvar")
        d_tok = sem("d_tok")
        d_mv = sem("d_mv")
        d_xn = sem("d_xn")
        d_norm = sem("d_norm")
        d_h2 = sem("d_h2")
        d_mv2 = sem("d_mv2")
        d_xn2 = sem("d_xn2")
        d_max = sem("d_max")
        d_ls = sem("d_ls")
        d_log = sem("d_log")
        d_oh = sem("d_oh")
        d_mt = sem("d_mt")
        d_pref = sem("d_pref")
        d_row = sem("d_row")
        d_cn = sem("d_cn")
        d_tab = sem("d_tab")
        d_xm = sem("d_xm")
        d_ht = sem("d_ht")
        d_out = sem("d_out")
        d_y = sem("d_y")
        c_set = sem("c_set")
        c_front = sem("c_front")
        c_back = sem("c_back")
        c_srch = sem("c_srch")
        c_moe = sem("c_moe")
        g_set = sem("g_set")
        g_te = sem("g_te")
        g_trstd = sem("g_trstd")
        g_e1 = sem("g_e1")
        g_r1 = sem("g_r1")
        g_e2 = sem("g_e2")
        g_r2 = sem("g_r2")
        g_hold = sem("g_hold")
        s_pad = sem("s_pad")
        s_row = [sem(f"s_row{u}") for u in range(4)]
        s_out = [sem(f"s_out{u}") for u in range(4)]

        block = ctx.enter_context(nc.Block())

        SET_LOADS = 9
        EXP_LOADS = 5

        @block.sync
        def _(sp):
            def load_txt(i):
                sp.dma_start(H[:, 2, :], txt[bass.ds(i, 1), :, :].rearrange("o t d -> t (o d)")).then_inc(s_txt, 16)

            def load_img(i):
                sp.dma_start(img[:, :, :], x[bass.ds(i, 1), :, :, :].rearrange("o p k n -> p (o k) n")).then_inc(
                    s_img, 16)

            sp.dma_start(cst[:, :], const).then_inc(s_set, 16)
            load_img(0)
            sp.dma_start(WS[:, :, :, :], wtok).then_inc(s_tokw, 16)
            sp.dma_start(GM[:, :, :], gam).then_inc(s_tokw, 16)
            sp.dma_start(BT[:, :, :], bet).then_inc(s_tokw, 16)
            sp.dma_start(btrow[:, :], btok.rearrange("(o d) -> o d", o=1)).then_inc(s_tokw, 16)
            sp.dma_start(WA[0:HC, :, :], wattn.rearrange("(c k) n -> k c n", c=2)).then_inc(s_set, 16)
            sp.dma_start(WA[HC:HC + 1, 1, :], battn.rearrange("(o d) -> o d", o=1)).then_inc(s_set, 16)
            sp.dma_start(WP[0:HC, :, :], wproj.rearrange("(c k) n -> k c n", c=2)).then_inc(s_set, 16)
            sp.dma_start(WP[HC:HC + 1, 1, :], bproj.rearrange("(o d) -> o d", o=1)).then_inc(s_set, 16)
            sp.dma_start(SW[0:HC, :, :], wsw.rearrange("(c k) n -> k c n", c=2)).then_inc(s_set, 16)
            sp.dma_start(SW[HC:HC + 1, 1, :], bsw.rearrange("(o d) -> o d", o=1)).then_inc(s_set, 16)
            sp.dma_start(B2[:, :, :], b2.partition_broadcast(128)).then_inc(s_set, 16)
            sp.wait_ge(d_set, 1)
            load_txt(0)
            sp.dma_start(W1[HC:HC + 1, 1, :, :], b1.rearrange("(o e) f -> o e f", o=1)).then_inc(s_set, 16)
            for e in range(0, EXPERTS, 4):
                for c in range(2):
                    sp.dma_start(W1[0:HC, c, e:e + 4, :],
                                 w1[e:e + 4, c * HC:(c + 1) * HC, :].rearrange("e k f -> k e f")).then_inc(s_exp, 16)
            sp.wait_ge(p_set, 2)
            sp.wait_ge(d_we, 1)
            sp.dma_start(W2[:, :, :, :].rearrange("p e f d -> p (e f) d"),
                         w2.rearrange("e (f p) d -> p (e f) d", p=128)).then_inc(s_exp, 16)

            def front(i, more):
                sp.wait_ge(p_tok, i + 1)
                if more:
                    sp.wait_ge(a_sq, i + 1)
                    load_img(i + 1)
                sp.wait_ge(a_qk, 4 * i + 2)
                for a in range(HG):
                    sp.dma_start(QDb[HD * a:HD * a + HD, :, 0:T].rearrange("p (g a) t -> p g a t", g=2)[:, :, a, :],
                                 QSb[HD * a:HD * a + HD, :, :]).then_inc(s_qdb, 16)
                if not (isinstance(i, int) and i == 0):
                    sp.wait_ge(p_st, 6 * i)
                for a in range(HG):
                    sp.dma_start(QD[HD * a:HD * a + HD, :, 0:T].rearrange("p (g a) t -> p g a t", g=2)[:, :, a, :],
                                 QS[HD * a:HD * a + HD, :, :]).then_inc(s_qd, 16)
                if more:
                    sp.wait_ge(a_r, i + 1)
                    load_txt(i + 1)
                sp.wait_ge(d_mt, i + 1)
                sp.dma_start(QD[HC:HC + 1, :, 0:T],
                             mT[:, :]).then_inc(s_mrow, 16)

            front(0, NB > 1)
            if NB > 2:
                with sp.Fori(1, NB - 1) as i:
                    front(i, True)
            if NB > 1:
                front(NB - 1, False)

            sp.wait_ge(d_tab, 1)
            for e in range(EXPERTS):
                r = sp.value_load(CNTI[0:1, e:e + 1], min_val=0, max_val=N)
                sp.dma_start(XS[bass.ds(r + e * CAPR, 128), :], ZR[:, :]).then_inc(s_pad, 16)
            sp.dma_start(XS[DUMMY:DUMMY + 128, :], ZR[:, :]).then_inc(s_pad, 16)
            sp.wait_ge(s_pad, 16 * (EXPERTS + 1))
            sp.wait_ge(s_scat, 48 * NB)

            def load_rows(k, u, free):
                r = sp.value_load(TBI[0:1, 0, bass.ds(k, 1)], min_val=0, max_val=DUMMY)
                if free is not None:
                    sp.wait_ge(d_out, free)
                sp.dma_start(RT[:, u, :], XS[bass.ds(r, 128), :]).then_inc(s_row[u], 16)

            for k in range(4):
                load_rows(k, k, None)
            with sp.Fori(0, NT // 4) as it:
                for u in range(4):
                    k = it * 4 + u
                    load_rows(k + 4, u, k + 1)
            for u in range(4):
                sp.wait_ge(s_row[u], 16 * (NT // 4 + 1))

        @block.gpsimd
        def _(gp):
            nc.gpsimd.memset(neghalf[:, :], -0.5).then_inc(g_set, 1)
            nc.gpsimd.memset(epsc[:, :], EPS).then_inc(g_set, 1)
            nc.gpsimd.memset(QD[:, :, :], 0.0).then_inc(g_set, 1)
            nc.gpsimd.memset(QDb[:, :, :], 0.0).then_inc(g_set, 1)
            nc.gpsimd.memset(XT[:, :, :], 0.0).then_inc(g_set, 1)
            nc.gpsimd.memset(KT[:, :, :], 0.0).then_inc(g_set, 1)
            nc.gpsimd.memset(KTb[:, :, :], 0.0).then_inc(g_set, 1)
            nc.gpsimd.memset(V[:, :, :, :], 1.0).then_inc(g_set, 1)
            gp.wait_ge(g_set, 8)
            nc.gpsimd.memset(XT[HC:HC + 1, :, :], 1.0).then_inc(g_set, 1)
            nc.gpsimd.memset(KT[HC:HC + 1, :, :], 1.0).then_inc(g_set, 1)
            nc.gpsimd.memset(YT[HC:HC + 1, :, :], 1.0).then_inc(g_set, 1)
            nc.gpsimd.memset(XT2[HC:HC + 1, :, :], 1.0).then_inc(g_set, 1)
            gp.wait_ge(g_set, 12)

            def hold():
                return nc.gpsimd.tensor_tensor(gpause[:, :], neghalf[:, 0:1], neghalf[:, 0:1], ALU.add)

            def front(i):
                gp.wait_ge(d_tvar, i + 1)
                nc.gpsimd.tensor_tensor(tve[:, :, 0], tvar[:, :, 0], epsc[0:HT, 0:2], ALU.add).then_inc(g_te, 1)
                gp.wait_ge(g_te, i + 1)
                nc.gpsimd.tensor_tensor(trstd[:, :, 0], tve[:, :, 0], neghalf[0:HT, 0:2], ALU.pow).then_inc(g_trstd, 1)
                gp.wait_ge(d_mv, i + 1)
                nc.gpsimd.tensor_tensor(ve1[:, :], MV[:, :, 1], epsc[:, :], ALU.add).then_inc(g_e1, 1)
                gp.wait_ge(g_e1, i + 1)
                nc.gpsimd.tensor_tensor(rstd1[:, :], ve1[:, :], neghalf[:, :], ALU.pow).then_inc(g_r1, 1)

            def back(a):
                gp.wait_ge(d_mv2, a + 1)
                nc.gpsimd.tensor_tensor(ve2[:, :], ROW[:, :, D + 1], epsc[:, :], ALU.add).then_inc(g_e2, 1)
                gp.wait_ge(g_e2, a + 1)
                nc.gpsimd.tensor_tensor(ROW[:, :, D + 1], ve2[:, :], neghalf[:, :], ALU.pow).then_inc(g_r2, 1)
                gp.wait_ge(d_row, a + 1)
                hold()
                for j in range(3):
                    gp.indirect_dma_start(XS[:, :], bass.IndirectOffsetOnAxis(ap=SLI[0:ROWS[j], j:j + 1], axis=0),
                                          ROW[0:ROWS[j], j, :], None, bounds_check=DUMMY - 1,
                                          oob_is_err=False).then_inc(s_scat, 16)

            front(0)
            with gp.Fori(1, NB) as i:
                front(i)
                back(i - 1)
            back(NB - 1)

            gp.wait_ge(g_r2, NB)
            nc.gpsimd.tensor_tensor(ve2[:, :], epsc[:, :], epsc[:, :], ALU.add).then_inc(g_hold, 1)
            with gp.Fori(0, NT // 4) as it:
                for u in range(4):
                    k = it * 4 + u
                    gp.wait_ge(g_hold, k + 1)
                    gp.wait_ge(d_out, k + 1)
                    hold().then_inc(g_hold, 1)
                    gp.indirect_dma_start(out, bass.IndirectOffsetOnAxis(ap=OI[:, u:u + 1], axis=0),
                                          OT[:, u, :], None, bounds_check=N - 1,
                                          oob_is_err=False).then_inc(s_out[u], 16)
            for u in range(4):
                gp.wait_ge(s_out[u], 16 * (NT // 4))

        @block.scalar
        def _(act):
            copy = nc.scalar.copy

            def square(i):
                act.wait_ge(s_img, 16 * (i + 1))
                if not (isinstance(i, int) and i == 0):
                    act.wait_ge(p_tok, i)
                nc.scalar.activation(sq[:, :, :], img[:, :, :], ACT.Square).then_inc(a_sq, 1)

            def exps(a, n):
                act.wait_ge(p_st, 6 * a + n + 1)
                if n >= 2 or not (isinstance(a, int) and a == 0):
                    act.wait_ge(p_pv, 6 * a + n - 1)
                nc.scalar.activation(PR[:, n % 2, :, :], ST[0:KW, 2 * (n % 2):2 * (n % 2) + 2, 0:HG * QB],
                                     ACT.Exp).then_inc(a_exp, 1)

            def y_turned(a, j, bank):
                act.wait_ge(p_yt, 3 * a + j + 1)
                if j == 0 and not (isinstance(a, int) and a == 0):
                    act.wait_ge(p_proj, 3 * a)
                for c in range(2):
                    last = copy(YT[0:HC, c, :].rearrange("p (s j q) -> p s j q", s=2, j=3)[:, :, j, :],
                                G[0:HC, bank, 128 * c:128 * c + 128].rearrange("p (s q) -> p s q", s=2)[:, :, 0:QB])
                last.then_inc(a_yt, 1)

            def x_turned(i):
                if not (isinstance(i, int) and i == 0):
                    act.wait_ge(p_qkv, 7 * i)
                for c in range(2):
                    act.wait_ge(p_xt, 2 * i + c + 1)
                    copy(XT[0:HC, c, PAD:PAD + T], G[0:HC, c, 0:T]).then_inc(a_xt, 1)

            def queries_keys(i):
                first = isinstance(i, int) and i == 0
                if not first:
                    act.wait_ge(s_qd, 16 * HG * i)
                    act.wait_ge(s_qdb, 16 * HG * i)
                for g in range(2):
                    act.wait_ge(p_qkv, 7 * i + g + 1)
                    bank = 1 + g
                    act.mul(QS[:, g, :], G[0:HC, bank, 0:T], HD ** -0.5)
                    act.mul(QSb[:, g, :], G[0:HC, bank, 0:T], HD ** -0.5).then_inc(a_qk, 1)
                for g in range(2):
                    act.wait_ge(p_qkv, 7 * i + g + 3)
                    if g == 0 and not first:
                        act.wait_ge(p_st, 6 * i)
                        act.wait_ge(p_smax, 9 * i)
                    copy(KT[0:HC, g, PAD:PAD + T], G[0:HC, g, 0:T])
                    copy(KTb[:, g, PAD:PAD + T], G[0:HC, g, 0:T]).then_inc(a_qk, 1)

            def values(i):
                if not (isinstance(i, int) and i == 0):
                    act.wait_ge(p_pv, 6 * i)
                for n in range(3):
                    act.wait_ge(p_qkv, 7 * i + n + 5)
                    copy(V[:, 2 * n:2 * n + 2, :, 0:HD].rearrange("p t h d -> p (t h) d"),
                         G[0:KW, n, 0:2 * D].rearrange("p (h d) -> p h d", d=HD)).then_inc(a_v, 1)

            def residual(i, back):
                if back:
                    act.wait_ge(d_h2, 3 * i)
                act.wait_ge(d_xn, i + 1)
                copy(R[:, :, :], H[:, :, :]).then_inc(a_r, 1)

            def router(a):
                if not (isinstance(a, int) and a == 0):
                    act.wait_ge(p_log, a)
                for c in range(2):
                    act.wait_ge(p_lt, 2 * a + c + 1)
                    copy(XT2[0:HC, c, :], G[0:HC, c, 0:T]).then_inc(a_lt, 1)
                act.wait_ge(d_ls, a + 1)
                nc.scalar.activation(EL[:, :, :], LS[:, :, :], ACT.Exp).then_inc(a_el, 1)

            def body(i, front, back, more):
                a = i - 1
                if back:
                    exps(a, 0)
                    exps(a, 1)
                    exps(a, 2)
                    exps(a, 3)
                    y_turned(a, 0, 2)
                    exps(a, 4)
                if front:
                    x_turned(i)
                if back:
                    exps(a, 5)
                    y_turned(a, 1, 0)
                if front:
                    queries_keys(i)
                if back:
                    y_turned(a, 2, 2)
                if front:
                    values(i)
                    residual(i, back)
                if more:
                    square(i + 1)
                if back:
                    router(a)

            act.wait_ge(g_set, 12)
            act.wait_ge(d_set, 1)
            square(0)
            body(0, True, False, True)
            body(1, True, True, True)
            with act.Fori(2, NB - 1) as i:
                body(i, True, True, True)
            body(NB - 1, True, True, False)
            body(NB, False, True, False)

            def turned(k, v):
                act.wait_ge(p_mx, k + 1)
                if not (isinstance(k, int) and k < 2):
                    act.wait_ge(p_l1, k - 1)
                copy(XMT[0:HC, v, :, :], G[0:HC, 2, 0:256].rearrange("p (c n) -> p c n", c=2)).then_inc(a_mx, 1)

            def gelu(k, v):
                act.wait_ge(p_l1, k + 1)
                if not (isinstance(k, int) and k == 0):
                    act.wait_ge(p_ht, k)
                nc.scalar.activation(HS[:, :].rearrange("p (b n) -> p b n", b=2), ST[:, 2 * v:2 * v + 2, 0:FF // 2],
                                     ACT.Gelu).then_inc(a_gelu, 1)

            turned(0, 0)
            turned(1, 1)
            gelu(0, 0)

            def two(it):
                for v in range(2):
                    k = it * 2 + v
                    turned(k + 2, v)
                    gelu(k + 1, 1 - v)

            two(0)
            with act.Fori(1, NT // 2) as it:
                two(it)

        @block.tensor
        def _(pe):
            mm = nc.tensor.matmul

            def halves(o, lhs, rhs):
                mm(o, lhs(0, HC), rhs(0, HC), start=True, stop=False)
                return mm(o, lhs(1, HC + 1), rhs(1, HC + 1), start=False, stop=True)

            def tokens(i, wait_mt, wait_pref):
                pe.wait_ge(s_img, 16 * (i + 1))
                pe.wait_ge(a_sq, i + 1)
                if wait_mt:
                    pe.wait_ge(d_mt, i)
                if wait_pref is not None:
                    pe.wait_ge(d_pref, wait_pref)
                for j in range(2):
                    for k in range(PCH):
                        mm(G[0:HT, j, 0:D + 1], img[:, k, HT * j:HT * j + HT], WE[:, k, 0:D + 1],
                           start=(k == 0), stop=(k == PCH - 1))
                    for k in range(PCH):
                        last = mm(G[0:HT, j, D + 2:D + 3], sq[:, k, HT * j:HT * j + HT],
                                  cst[0:PIX, C_CNT + k:C_CNT + k + 1], start=(k == 0), stop=(k == PCH - 1))
                last.then_inc(p_tok, 1)

            def x_turn(i):
                pe.wait_ge(d_tok, i + 1)
                pe.wait_ge(d_xn, i + 1)
                for c in range(2):
                    for j in range(3):
                        last = nc.tensor.transpose(G[0:HC, c, OFF[j]:OFF[j] + ROWS[j]],
                                                   XN[0:ROWS[j], j, c * HC:(c + 1) * HC],
                                                   ident[0:ROWS[j], 0:ROWS[j]])
                    last.then_inc(p_xt, 1)

            def project_qk(i, back):
                pe.wait_ge(a_xt, 2 * i + 2)
                for n in range(4):
                    bank = (1 + n) % 3
                    if n == 1 and back:
                        pe.wait_ge(a_yt, 3 * (i - 1) + 1)
                    if n == 2 and back:
                        pe.wait_ge(a_yt, 3 * (i - 1) + 2)
                    if n == 3:
                        pe.wait_ge(a_qk, 4 * i + 1)
                    halves(G[0:HC, bank, 0:T], lambda c, r: WA[0:r, c, HC * n:HC * n + HC],
                           lambda c, r: XT[0:r, c, PAD:PAD + T]).then_inc(p_qkv, 1)

            def project_v(i, back):
                for n in range(3):
                    if n == 0:
                        pe.wait_ge(a_qk, 4 * i + 3)
                    if n == 1:
                        pe.wait_ge(a_qk, 4 * i + 4)
                    if n == 2:
                        if back:
                            pe.wait_ge(a_yt, 3 * (i - 1) + 3)
                        else:
                            pe.wait_ge(a_qk, 4 * i + 2)
                    for t in (2 * n, 2 * n + 1):
                        last = halves(G[0:KW, n, D * (t % 2):D * (t % 2) + D],
                                      lambda c, r: XT[0:r, c, QB * t:QB * t + KW],
                                      lambda c, r: WA[0:r, c, 2 * D:3 * D])
                    last.then_inc(p_qkv, 1)

            def maxima(i, back):
                pe.wait_ge(s_qdb, 16 * HG * (i + 1))
                pe.wait_ge(a_qk, 4 * i + 4)
                if back:
                    pe.wait_ge(a_exp, 6 * i)
                for n in range(9):
                    j, h0 = n // 3, 4 * (n % 3)
                    if n >= 4:
                        pe.wait_ge(d_max, 9 * i + n - 3)
                    mm(ST[:, n % 4, 0:4 * KW], identb[:, :],
                       mqb[:, j, :].unsqueeze(1).broadcast_to([128, 4, KW]), start=True, stop=True,
                       skip_group_check=True)
                    for h in range(h0, h0 + 4):
                        for s in range(2):
                            t = 3 * s + j
                            last = mm(ST[64 * s:64 * s + 64, n % 4, KW * (h - h0):KW * (h - h0) + KW],
                                      QDb[:, h, QB * t:QB * t + 64], KTb[:, h // HG, QB * t:QB * t + KW],
                                      start=False, stop=True, skip_group_check=True)
                    last.then_inc(p_smax, 1)

            def max_turn(i, back):
                pe.wait_ge(d_max, 9 * i + 9)
                if back:
                    pe.wait_ge(a_lt, 2 * (i - 1) + 1)
                else:
                    pe.wait_ge(a_v, 3 * i + 1)
                for j in range(3):
                    last = nc.tensor.transpose(G[0:HEADS, 0, 128 * j:128 * j + 128], M[:, j, :], ident[:, :])
                last.then_inc(p_mt, 1)

            def scores(a, n):
                t = ORDER[n]
                if n == 0:
                    pe.wait_ge(s_qd, 16 * HG * (a + 1))
                    pe.wait_ge(s_mrow, 16 * (a + 1))
                    pe.wait_ge(d_max, 9 * a + 9)
                if n >= 2:
                    pe.wait_ge(a_exp, 6 * a + n - 1)
                for g in range(2):
                    bank = 2 * (n % 2) + g
                    mm(ST[0:KW, bank, 0:HG * QB], identb[0:KW, 0:KW],
                       mtb[0:KW, min(t, 2), :].unsqueeze(1).broadcast_to([KW, HG, QB]), start=True, stop=False)
                    last = mm(ST[0:KW, bank, 0:HG * QB], KT[:, g, QB * t:QB * t + KW],
                              QD[:, HG * g:HG * g + HG, QB * t:QB * t + QB], start=False, stop=True)
                last.then_inc(p_st, 1)

            def weighted(a, n):
                t, s = ORDER[n], n % 2
                pe.wait_ge(a_exp, 6 * a + n + 1)
                if n == 0:
                    pe.wait_ge(a_v, 3 * a + 3)
                if s == 0 and not (n == 0 and isinstance(a, int) and a == 0):
                    pe.wait_ge(d_norm, 3 * a + n // 2)
                for h in range(HEADS):
                    last = mm(Y[64 * s:64 * s + QB, (HD + 1) * h:(HD + 1) * (h + 1)],
                              PR[:, n % 2, h // HG, QB * (h % HG):QB * (h % HG) + QB], V[:, t, h, :],
                              start=True, stop=True)
                last.then_inc(p_pv, 1)

            def y_turn(a, j, bank):
                pe.wait_ge(d_norm, 3 * a + j + 1)
                for c in range(2):
                    last = nc.tensor.transpose(G[0:HC, bank, 128 * c:128 * c + 118], ysb[0:118, c * HC:(c + 1) * HC],
                                               ident[0:118, 0:118])
                last.then_inc(p_yt, 1)

            def project_out(a, front):
                pe.wait_ge(a_yt, 3 * a + 3)
                if front:
                    pe.wait_ge(a_v, 3 * (a + 1) + 3)
                else:
                    pe.wait_ge(d_pref, a)
                for j in range(3):
                    halves(G[0:ROWS[j], j, 0:D], lambda c, r: YT[0:r, c, OFF[j]:OFF[j] + ROWS[j]],
                           lambda c, r: WP[0:r, c, :]).then_inc(p_proj, 1)

            def logits(a):
                pe.wait_ge(d_h2, 3 * a + 3)
                pe.wait_ge(d_xn2, a + 1)
                for c in range(2):
                    for j in range(3):
                        last = nc.tensor.transpose(G[0:HC, c, OFF[j]:OFF[j] + ROWS[j]],
                                                   XN2[0:ROWS[j], j, c * HC:(c + 1) * HC],
                                                   ident[0:ROWS[j], 0:ROWS[j]])
                    last.then_inc(p_lt, 1)
                pe.wait_ge(a_lt, 2 * a + 2)
                for j in range(3):
                    last = halves(G[0:ROWS[j], 2, 8 * j:8 * j + 8], lambda c, r: XT2[0:r, c, OFF[j]:OFF[j] + ROWS[j]],
                                  lambda c, r: SW[0:r, c, :])
                last.then_inc(p_log, 1)

            def prefixes(a):
                pe.wait_ge(d_oh, a + 1)
                for j in range(3):
                    for m in range(j):
                        mm(G[:, 1, 8 * j:8 * j + 8], onesb[0:ROWS[m], :], OHb[0:ROWS[m], m, :],
                           start=(m == 0), stop=False)
                    mm(G[:, 1, 8 * j:8 * j + 8], utrib[0:ROWS[j], :], OHb[0:ROWS[j], j, :], start=(j == 0), stop=True)
                for j in range(3):
                    last = mm(G[:, 1, 24:32], onesb[0:ROWS[j], :], OHb[0:ROWS[j], j, :], start=(j == 0), stop=(j == 2))
                last.then_inc(p_pref, 1)

            def body(i, front, back, pref):
                a = i - 1
                if front:
                    tokens(i, back, pref)
                if back:
                    scores(a, 0)
                    scores(a, 1)
                    weighted(a, 0)
                    scores(a, 2)
                    weighted(a, 1)
                    scores(a, 3)
                    if pref is not None or not front:
                        pe.wait_ge(d_log, a)
                    y_turn(a, 0, 2)
                    weighted(a, 2)
                    scores(a, 4)
                    weighted(a, 3)
                if front:
                    x_turn(i)
                if back:
                    scores(a, 5)
                    if front:
                        pe.wait_ge(a_xt, 2 * i + 1)
                    else:
                        pe.wait_ge(d_mt, i)
                    y_turn(a, 1, 0)
                    weighted(a, 4)
                    weighted(a, 5)
                if front:
                    project_qk(i, back)
                if back:
                    if front:
                        pe.wait_ge(a_qk, 4 * i + 2)
                    else:
                        pe.wait_ge(a_yt, 3 * a + 1)
                    y_turn(a, 2, 2)
                if front:
                    project_v(i, back)
                if back:
                    project_out(a, front)
                if front:
                    maxima(i, back)
                if back:
                    logits(a)
                if front:
                    max_turn(i, back)
                if back:
                    prefixes(a)

            pe.wait_ge(s_tokw, 64)
            pe.wait_ge(d_set, 1)
            n = 0
            for s in range(5):
                for k in range(PCH):
                    mm(G[0:HT, 0, 0:D], BT[:, s, k:k + 1].broadcast_to([PIX, HT]), WS[:, s, k, :],
                       start=(n == 0), stop=False)
                    n += 1
            mm(G[0:HT, 0, 0:D], ones[0:1, 0:HT], btrow[:, :], start=False, stop=True).then_inc(p_set, 1)
            pe.wait_ge(d_we, 1)
            for k in range(PCH):
                last = mm(G[0:HT, 1, 0:D], ones[0:PIX, 0:HT], WE[:, k, 0:D], start=(k == 0), stop=(k == PCH - 1))
            last.then_inc(p_set, 1)

            pe.wait_ge(s_set, 16 * SET_LOADS)
            pe.wait_ge(g_set, 12)
            pe.wait_ge(d_set, 2)
            body(0, True, False, None)
            body(1, True, True, None)
            with pe.Fori(2, NB) as i:
                body(i, True, True, i - 1)
            body(NB, False, True, None)

            with pe.Fori(0, TAU_STEPS + IDX_STEPS) as n:
                pe.wait_ge(d_cn, n + 1)
                mm(G[:, 0, 0:8], onesb[:, :], CNb[:, :], start=True, stop=True).then_inc(p_cnt, 1)

            def turn(k, u):
                pe.wait_ge(d_xm, k + 1)
                if not (isinstance(k, int) and k == 0):
                    pe.wait_ge(a_mx, k)
                for c in range(2):
                    last = nc.tensor.transpose(G[0:HC, 2, 128 * c:128 * c + 128],
                                               XM[:, u, c * HC:(c + 1) * HC], ident[:, :])
                last.then_inc(p_mx, 1)

            def layer1(k, v):
                e = pe.value_load(TBI[0:1, 1, bass.ds(k, 1)], min_val=0, max_val=EXPERTS - 1)
                pe.wait_ge(a_mx, k + 1)
                if not (isinstance(k, int) and k < 2):
                    pe.wait_ge(a_gelu, k - 1)
                for half in range(2):
                    last = halves(ST[:, 2 * v + half, 0:FF // 2], lambda c, r: XMT[0:r, v, c, :],
                                  lambda c, r: W1[0:r, c, bass.ds(e, 1), half * (FF // 2):(half + 1) * (FF // 2)])
                last.then_inc(p_l1, 1)

            def hidden_turn(k):
                pe.wait_ge(a_gelu, k + 1)
                if not (isinstance(k, int) and k == 0):
                    pe.wait_ge(d_ht, k)
                for f in range(FCH):
                    last = nc.tensor.transpose(G[:, f // 3, 128 * (f % 3):128 * (f % 3) + 128],
                                               HS[:, 128 * f:128 * f + 128], ident[:, :])
                last.then_inc(p_ht, 1)

            def layer2(k):
                e = pe.value_load(TBI[0:1, 1, bass.ds(k, 1)], min_val=0, max_val=EXPERTS - 1)
                pe.wait_ge(d_ht, k + 1)
                pe.wait_ge(d_y, k + 1)
                for f in range(FCH):
                    last = mm(Y[:, 0:D], HTs[:, f, :], W2[:, bass.ds(e, 1), f, :], start=(f == 0), stop=(f == FCH - 1))
                last.then_inc(p_l2, 1)

            pe.wait_ge(s_exp, 16 * EXP_LOADS)
            pe.wait_ge(d_tab, 1)
            turn(0, 0)
            turn(1, 1)
            layer1(0, 0)

            def four(it):
                for u in range(4):
                    k = it * 4 + u
                    hidden_turn(k)
                    layer1(k + 1, (u + 1) % 2)
                    turn(k + 2, (u + 2) % 4)
                    layer2(k)

            four(0)
            with pe.Fori(1, NT // 4) as it:
                four(it)

        @block.vector
        def _(dve):
            class Chain:

                def __init__(self, s, base=0):
                    self.s, self.base, self.n = s, base, 0

                def __call__(self, ins):
                    self.n += 1
                    ins.then_inc(self.s, 1)
                    dve.wait_ge(self.s, self.base + self.n)

            v = nc.vector
            FRONT, BACK = 4, 15

            v.memset(H[:, :, :], 0.0)
            v.memset(ones[:, :], 1.0)
            v.memset(ROW[:, :, :], 0.0)
            v.memset(Y[:, :], 1.0)
            v.memset(BASE[:, :], 0.0)
            v.memset(G[:, :, :], 0.0)
            v.memset(onesb[:, :], 1.0)
            v.memset(WE[:, :, D:D + 2], 0.0)
            v.memset(PME[:, :, :], 0.0).then_inc(d_set, 1)
            dve.wait_ge(d_set, 1)
            link = Chain(c_set)
            dve.wait_ge(s_set, 16 * SET_LOADS)
            v.tensor_copy(identb[:, :], ident)
            v.tensor_copy(utrib[:, :], cst[:, C_UT:C_UT + 128])
            v.tensor_copy(mqb[:, :, :], cst[:, C_MQ:C_MT].rearrange("p (v k) -> p v k", v=3))
            v.tensor_copy(mtb[:, :, :], cst[:, C_MT:C_VALID].rearrange("p (v k) -> p v k", v=3))
            v.tensor_copy(TK[:, :], cst[:, C_TOK:C_TOK + 3])
            v.memset(ZR[:, :], 0.0)
            link(v.tensor_copy(WE[:, :, D], cst[0:PIX, C_CNT:C_CNT + PCH]))
            link(v.memset(ZR[:, D + 3:D + 4], float(SKIP)))
            dve.wait_ge(s_tokw, 64)
            link(v.tensor_tensor(WE[:, :, 0:D], WS[:, 0, :, :], GM[:, 0, :].unsqueeze(2).broadcast_to([PIX, PCH, D]),
                                 ALU.mult))
            for s in range(1, 5):
                link(v.tensor_tensor(WTMP[:, :, :], WS[:, s, :, :],
                                     GM[:, s, :].unsqueeze(2).broadcast_to([PIX, PCH, D]), ALU.mult))
                link(v.tensor_tensor(WE[:, :, 0:D], WE[:, :, 0:D], WTMP[:, :, :], ALU.add))
            v.memset(MV[:, :, :], 0.0).then_inc(d_we, 1)
            SETUP = link.n
            dve.wait_ge(p_set, 1)
            v.tensor_copy(tbias[:, :], G[0:HT, 0, 0:D])
            dve.wait_ge(p_set, 2)
            v.tensor_copy(csum[:, :], G[0:HT, 1, 0:D]).then_inc(d_set, 1)
            dve.wait_ge(d_set, 2)

            def front(i):
                link = Chain(c_front, i * FRONT)
                first = isinstance(i, int) and i == 0
                dve.wait_ge(p_tok, i + 1)
                link(v.tensor_scalar(negmu[:, :, :], G[0:HT, 0:2, D:D + 1], -1.0 / PATCH_DIM, None, ALU.mult))
                link(v.tensor_tensor(msq[:, :, :], negmu[:, :, :], negmu[:, :, :], ALU.mult))
                v.scalar_tensor_tensor(tvar[:, :, :], G[0:HT, 0:2, D + 2:D + 3], 1.0 / PATCH_DIM, msq[:, :, :],
                                       ALU.mult, ALU.subtract).then_inc(d_tvar, 1)
                for j in range(2):
                    last = v.scalar_tensor_tensor(TMP[:, j, :], csum[:, :], negmu[:, j, :], G[0:HT, j, 0:D],
                                                  ALU.mult, ALU.add)
                last.then_inc(d_tok, 1)
                dve.wait_ge(d_tok, i + 1)
                dve.wait_ge(g_trstd, i + 1)
                if not first:
                    dve.wait_ge(a_r, i)
                for j in range(2):
                    last = v.scalar_tensor_tensor(H[0:HT, j, :], TMP[:, j, :], trstd[:, j, :], tbias[:, :],
                                                  ALU.mult, ALU.add)
                link(last)
                dve.wait_ge(s_txt, 16 * (i + 1))
                for j in range(3):
                    last = v.bn_stats(BN[:, j, :], H[:, j, :])
                link(last)
                v.memset(pause[:, :], 0.0)
                for j in range(3):
                    last = v.bn_aggr(MV[:, j, :], BN[:, j, :])
                last.then_inc(d_mv, 1)
                dve.wait_ge(d_mv, i + 1)
                dve.wait_ge(g_r1, i + 1)
                if not first:
                    dve.wait_ge(p_xt, 2 * i)
                for j in range(3):
                    last = v.tensor_scalar(XN[:, j, :], H[:, j, :], MV[:, j, 0:1], rstd1[:, j:j + 1],
                                           ALU.subtract, ALU.mult)
                last.then_inc(d_xn, 1)
                assert link.n == FRONT

            def maxima(i):
                first = isinstance(i, int) and i == 0
                if not first:
                    dve.wait_ge(p_mt, i)
                for n in range(9):
                    j, h0 = n // 3, 4 * (n % 3)
                    dve.wait_ge(p_smax, 9 * i + n + 1)
                    v.tensor_reduce(M[:, j, h0:h0 + 4], ST[:, n % 4, 0:4 * KW].rearrange("p (h k) -> p h k", h=4),
                                    AX_X, ALU.max, negate=True).then_inc(d_max, 1)

            def max_rows(i):
                dve.wait_ge(p_mt, i + 1)
                if not (isinstance(i, int) and i == 0):
                    dve.wait_ge(s_mrow, 16 * i)
                for s in range(2):
                    last = v.tensor_copy(mT[:, 3 * QB * s:3 * QB * (s + 1)].rearrange("p (j q) -> p j q", j=3),
                                         G[0:HEADS, 0, 0:384].rearrange("p (j q) -> p j q", j=3)[
                                             :, :, 64 * s:64 * s + QB])
                last.then_inc(d_mt, 1)

            def normalise(a, j, link):
                dve.wait_ge(p_pv, 6 * a + 2 * j + 2)
                if not (j == 0 and isinstance(a, int) and a == 0):
                    dve.wait_ge(p_yt, 3 * a + j)
                yv = Y[:, 0:HEADS * (HD + 1)].rearrange("p (h d) -> p h d", h=HEADS)
                link(v.reciprocal(rec[:, :], yv[:, :, HD]))
                v.tensor_tensor(ysb[:, :].rearrange("p (h d) -> p h d", h=HEADS), yv[:, :, 0:HD],
                                rec[:, :].unsqueeze(2).broadcast_to([128, HEADS, HD]), ALU.mult).then_inc(d_norm, 1)

            def second(a, link):
                first = isinstance(a, int) and a == 0
                if not first:
                    dve.wait_ge(s_scat, 48 * a)
                dve.wait_ge(a_r, a + 1)
                for j in range(3):
                    dve.wait_ge(p_proj, 3 * a + j + 1)
                    v.tensor_tensor(ROW[0:ROWS[j], j, 0:D], G[0:ROWS[j], j, 0:D], R[0:ROWS[j], j, :],
                                    ALU.add).then_inc(d_h2, 1)
                dve.wait_ge(d_h2, 3 * a + 3)
                for j in range(3):
                    last = v.bn_stats(BN2[:, j, :], ROW[:, j, 0:D])
                link(last)
                v.memset(pause[:, :], 0.0)
                for j in range(3):
                    last = v.bn_aggr(ROW[:, j, D:D + 2], BN2[:, j, :])
                last.then_inc(d_mv2, 1)
                dve.wait_ge(d_mv2, a + 1)
                dve.wait_ge(g_r2, a + 1)
                if not first:
                    dve.wait_ge(p_lt, 2 * a)
                for j in range(3):
                    last = v.tensor_scalar(XN2[:, j, :], ROW[:, j, 0:D], ROW[:, j, D:D + 1], ROW[:, j, D + 1:D + 2],
                                           ALU.subtract, ALU.mult)
                last.then_inc(d_xn2, 1)

            def wide(ap):
                return ap.unsqueeze(2).broadcast_to([128, 3, EXPERTS])

            def per_expert(ap):
                return ap.unsqueeze(1).broadcast_to([128, 3, EXPERTS])

            def route(a, link):
                dve.wait_ge(p_log, a + 1)
                lg = G[:, 2, 0:24].rearrange("p (j e) -> p j e", j=3)
                link(v.tensor_reduce(LM[:, :], lg, AX_X, ALU.max))
                if not (isinstance(a, int) and a == 0):
                    dve.wait_ge(a_el, a)
                v.tensor_tensor(LS[:, :, :], lg, wide(LM[:, :]), ALU.subtract).then_inc(d_ls, 1)
                v.tensor_tensor(EQ[:, :, :], lg, wide(LM[:, :]), ALU.is_equal).then_inc(d_log, 1)
                dve.wait_ge(d_log, a + 1)
                link(v.tensor_tensor(SC[:, :, :], EQ[:, :, :], per_expert(cst[:, C_W8:C_W8 + 8]), ALU.mult))
                link(v.tensor_reduce(MX[:, :], SC[:, :, :], AX_X, ALU.max))
                link(v.tensor_tensor(EQ[:, :, :], SC[:, :, :], wide(MX[:, :]), ALU.is_equal))
                if not (isinstance(a, int) and a == 0):
                    dve.wait_ge(p_pref, a)
                v.tensor_tensor(OH[:, :, :], EQ[:, :, :], wide(cst[:, C_VALID:C_VALID + 3]), ALU.mult)
                v.tensor_tensor(OHb[:, :, :], EQ[:, :, :], wide(cst[:, C_VALID:C_VALID + 3]), ALU.mult).then_inc(
                    d_oh, 1)
                dve.wait_ge(a_el, a + 1)
                link(v.tensor_reduce(ES[:, :], EL[:, :, :], AX_X, ALU.add))
                link(v.reciprocal(ROW[:, :, D + 2], ES[:, :]))

            def place(a, link):
                dve.wait_ge(p_pref, a + 1)
                dve.wait_ge(d_oh, a + 1)
                link(v.tensor_tensor(POS[:, :, :], G[:, 1, 0:24].rearrange("p (j e) -> p j e", j=3),
                                     per_expert(BASE[:, :]), ALU.add))
                v.tensor_tensor(BASE[:, :], BASE[:, :], G[:, 1, 24:32], ALU.add).then_inc(d_pref, 1)
                dve.wait_ge(d_pref, a + 1)
                link(v.tensor_tensor(POS[:, :, :], POS[:, :, :], per_expert(cst[:, C_EOFF:C_EOFF + 8]), ALU.add))
                link(v.tensor_tensor(POS[:, :, :], POS[:, :, :], OH[:, :, :], ALU.mult))
                link(v.tensor_reduce(SLF[:, :], POS[:, :, :], AX_X, ALU.add))
                v.tensor_copy(SLI[:, :], SLF[:, :])
                v.tensor_tensor(PME[:, bass.ds(3 * a, 3), :], OH[:, :, :], wide(ROW[:, :, D + 2]), ALU.mult)
                link(v.tensor_copy(ROW[:, :, D + 3], TK[:, :]))
                v.tensor_scalar(TK[:, :], TK[:, :], float(T), None, ALU.add).then_inc(d_row, 1)
                dve.wait_ge(d_row, a + 1)

            def body(i, do_front, do_back):
                a = i - 1
                if do_front:
                    front(i)
                if do_back:
                    link = Chain(c_back, a * BACK)
                    for j in range(3):
                        normalise(a, j, link)
                    second(a, link)
                if do_front:
                    maxima(i)
                if do_back:
                    route(a, link)
                if do_front:
                    max_rows(i)
                if do_back:
                    place(a, link)
                    assert link.n == BACK, link.n

            body(0, True, False)
            body(1, True, True)
            with dve.Fori(2, NB) as i:
                body(i, True, True)
            body(NB, False, True)

            link = Chain(c_set, SETUP)
            link(v.tensor_scalar(NTE[:, :], BASE[:, :], 127.0, None, ALU.add))
            link(v.tensor_copy(CI[:, :], NTE[:, :]))
            v.tensor_copy(CNTI[:, :], BASE[:, :])
            link(v.tensor_scalar(CI2[:, :], CI[:, :], 7, None, ALU.arith_shift_right))
            link(v.tensor_copy(NTE[:, :], CI2[:, :]))
            link(v.tensor_tensor_scan(FI[:, :], ones[0:1, 0:8], NTE[0:1, :], 0.0, ALU.mult, ALU.add))
            link(v.tensor_tensor(FE[:, :], FI[:, :], NTE[0:1, :], ALU.subtract))
            link(v.tensor_scalar(AE[:, :], FE[:, :], -128.0, -float(DUMMY), ALU.mult, ALU.add))
            link(v.tensor_tensor(AE[:, :], AE[:, :], cst[0:1, C_EOFF:C_EOFF + 8], ALU.add))
            shape = [1, NTP, EXPERTS]
            kio = cst[0:1, C_KI:C_KI + NTP].unsqueeze(2).broadcast_to(shape)

            def each(ap):
                return ap.unsqueeze(1).broadcast_to(shape)

            v.tensor_tensor(IN1[:, :, :], kio, each(FE[:, :]), ALU.is_ge)
            link(v.tensor_tensor(IN2[:, :, :], kio, each(FI[:, :]), ALU.is_ge))
            link(v.tensor_tensor(IN1[:, :, :], IN1[:, :, :], IN2[:, :, :], ALU.subtract))
            link(v.scalar_tensor_tensor(IN2[:, :, :], kio, 128.0, each(AE[:, :]), ALU.mult, ALU.add))
            link(v.tensor_tensor(IN2[:, :, :], IN2[:, :, :], IN1[:, :, :], ALU.mult))
            link(v.tensor_tensor(IN3[:, :, :], IN1[:, :, :], each(cst[0:1, C_EI:C_EI + 8]), ALU.mult))
            link(v.tensor_reduce(TBF[:, 0, :], IN2[:, :, :], AX_X, ALU.add))
            link(v.tensor_reduce(TBF[:, 1, :], IN3[:, :, :], AX_X, ALU.add))
            link(v.tensor_scalar(TBF[:, 0, :], TBF[:, 0, :], float(DUMMY), None, ALU.add))
            v.tensor_copy(TBI[:, :, :], TBF[:, :, :]).then_inc(d_tab, 1)
            dve.wait_ge(d_tab, 1)

            link(v.memset(TIDX[:, :], 0.0))
            for j in range(3):
                link(v.tensor_tensor(TIDX[:, :].rearrange("p (b j) -> p b j", j=3)[:, :, j],
                                     cst[:, C_KI:C_KI + NB],
                                     TIDX[:, :].rearrange("p (b j) -> p b j", j=3)[:, :, j], ALU.add))
            link(v.tensor_scalar(TIDX[:, :], TIDX[:, :], float(T), None, ALU.mult))
            link(v.tensor_tensor(TIDX[:, :].rearrange("p (b j) -> p b j", j=3),
                                 TIDX[:, :].rearrange("p (b j) -> p b j", j=3),
                                 cst[:, C_TOK:C_TOK + 3].unsqueeze(1).broadcast_to([128, NB, 3]), ALU.add))

            tshape = [128, TILES, EXPERTS]

            def over(ap):
                return ap.unsqueeze(1).broadcast_to(tshape)

            SRCH = 6
            link(v.memset(TAU[:, :], 0.0625))
            link(v.memset(STEP[:, :], 0.5))

            def count_step(n, key, keep_op, bound, bound_op, value):
                s = Chain(c_srch, n * SRCH)
                s(v.tensor_tensor(MID[:, :], value[:, :], STEP[:, :], ALU.add))
                s(v.tensor_tensor(GE[:, :, :], key, over(MID[:, :]), keep_op))
                last = v.tensor_reduce(CN[:, :], GE[:, :, :].rearrange("p g e -> p e g"), AX_X, ALU.add)
                s(last)
                v.tensor_copy(CNb[:, :], CN[:, :]).then_inc(d_cn, 1)
                dve.wait_ge(p_cnt, n + 1)
                s(v.scalar_tensor_tensor(INC[:, :], G[:, 0, 0:8], bound, STEP[:, :], bound_op, ALU.mult))
                s(v.tensor_tensor(value[:, :], value[:, :], INC[:, :], ALU.add))
                s(v.tensor_scalar(STEP[:, :], STEP[:, :], 0.5, None, ALU.mult))
                assert s.n == SRCH

            with dve.Fori(0, TAU_STEPS) as n:
                count_step(n, PME[:, :, :], ALU.is_ge, float(CAP), ALU.is_ge, TAU)

            link(v.tensor_tensor(KEY[:, :, :], PME[:, :, :], over(TAU[:, :]), ALU.is_equal))
            link(v.tensor_scalar(GE[:, :, 0], TIDX[:, :], -float(SKIP), None, ALU.add))
            link(v.tensor_tensor(KEY[:, :, :], KEY[:, :, :], GE[:, :, 0].unsqueeze(2).broadcast_to(tshape), ALU.mult))
            link(v.tensor_tensor(GE[:, :, :], PME[:, :, :], over(TAU[:, :]), ALU.is_gt))
            link(v.scalar_tensor_tensor(KEY[:, :, :], GE[:, :, :], -float(SKIP) - 1.0, KEY[:, :, :],
                                        ALU.mult, ALU.add))
            link(v.tensor_scalar(KEY[:, :, :], KEY[:, :, :], float(SKIP), None, ALU.add))
            link(v.memset(IDX[:, :], 0.0))
            link(v.memset(STEP[:, :], float(1 << (IDX_STEPS - 1))))
            with dve.Fori(TAU_STEPS, TAU_STEPS + IDX_STEPS) as n:
                count_step(n, KEY[:, :, :], ALU.is_lt, float(CAP), ALU.is_le, IDX)

            MOE = 6

            def normal(k, u, r):
                dve.wait_ge(s_row[u], 16 * (r + 1))
                if not (isinstance(k, int) and k < 4):
                    dve.wait_ge(p_mx, k - 3)
                v.tensor_scalar(XM[:, u, :], RT[:, u, 0:D], RT[:, u, D:D + 1], RT[:, u, D + 1:D + 2],
                                ALU.subtract, ALU.mult).then_inc(d_xm, 1)

            def combine(k, u, it):
                s = Chain(c_moe, k * MOE)
                e = dve.value_load(TBI[0:1, 1, bass.ds(k, 1)], min_val=0, max_val=EXPERTS - 1)
                pm, tok = RT[:, u, D + 2:D + 3], RT[:, u, D + 3:D + 4]
                tau, idx = TAU[:, bass.ds(e, 1)], IDX[:, bass.ds(e, 1)]
                s(v.tensor_tensor(ceq[:, :], pm, tau, ALU.is_equal))
                s(v.tensor_tensor(clt[:, :], tok, idx, ALU.is_lt))
                s(v.tensor_tensor(ceq[:, :], ceq[:, :], clt[:, :], ALU.mult))
                s(v.tensor_tensor(ckp[:, :], pm, tau, ALU.is_gt))
                s(v.scalar_tensor_tensor(c1[:, :], ckp[:, :], ceq[:, 0:1], pm, ALU.add, ALU.mult))
                v.tensor_tensor(c2[:, :], pm, c1[:, :], ALU.subtract)
                dve.wait_ge(p_l2, k + 1)
                s(v.tensor_tensor(Y1[:, :], Y[:, 0:D], B2[:, bass.ds(e, 1), :].rearrange("p o d -> p (o d)"), ALU.add))
                v.scalar_tensor_tensor(Y2[:, :], XM[:, u, :], c2[:, 0:1], RT[:, u, 0:D], ALU.mult,
                                       ALU.add).then_inc(d_y, 1)
                dve.wait_ge(d_y, k + 2)
                if not isinstance(it, int):
                    dve.wait_ge(s_out[u], 16 * it)
                v.tensor_copy(OI[:, u:u + 1], tok)
                v.scalar_tensor_tensor(OT[:, u, :], Y1[:, :], c1[:, 0:1], Y2[:, :], ALU.mult, ALU.add).then_inc(
                    d_out, 1)
                assert s.n == MOE

            link(v.memset(ceq[:, :], 0.0))
            v.memset(c2[:, :], 0.0).then_inc(d_y, 1)
            for k in range(3):
                normal(k, k, 0)

            def four(it):
                for u in range(4):
                    k = it * 4 + u
                    dve.wait_ge(p_ht, k + 1)
                    if not (isinstance(k, int) and k == 0):
                        dve.wait_ge(p_l2, k)
                    v.tensor_copy(HTs[:, :, :].rearrange("p (b f) n -> p b (f n)", b=2),
                                  G[:, 0:2, 0:384]).then_inc(d_ht, 1)
                    normal(k + 3, (u + 3) % 4, it if u == 0 else it + 1)
                    combine(k, u, it)

            four(0)
            with dve.Fori(1, NT // 4) as it:
                four(it)


_INS = ["x", "txt", "wtok", "gam", "bet", "btok", "wattn", "battn", "wproj", "bproj", "wsw", "bsw",
        "w1", "b1", "w2", "b2", "const"]


def _layout(np):
    pix = [(c, y, x) for c in range(3) for y in range(18) for x in range(18)
           if not (y in (0, 17) and x in (0, 17))]
    moves = [(1, 1), (1, 0), (1, 2), (0, 1), (2, 1)]
    rows = np.full((5, len(pix)), PATCH_DIM, np.int64)
    for s, (dy, dx) in enumerate(moves):
        for n, (c, y, x) in enumerate(pix):
            py, px = y - dy, x - dx
            if 0 <= py < 16 and 0 <= px < 16:
                rows[s, n] = (py * 16 + px) * 15 + 3 * s + c
    return pix, rows


def _constants(np, nb, pix, rows):
    n_tiles = tiles_of(nb * T) + 4
    c = np.zeros((128, C_KI + n_tiles), np.float32)
    p = np.arange(128)[:, None]
    c[:, C_ID:C_ID + 128] = np.eye(128)
    c[:, C_UT:C_UT + 128] = p < np.arange(128)[None, :]
    key = np.arange(KW)[None, :]
    for v in range(3):
        q = p % 64
        keep = (key >= q) & (key <= q + PAD)
        keep &= (key >= PAD - QB * v) | (p >= 64)
        c[:, C_MQ + KW * v:C_MQ + KW * (v + 1)] = np.where(keep, 0, NEG)
        k, q = p, np.arange(QB)[None, :]
        keep = (k >= q) & (k <= q + PAD) & (k >= PAD - QB * v)
        c[:, C_MT + QB * v:C_MT + QB * (v + 1)] = np.where(keep, 0, NEG)
    for j in range(3):
        c[:, C_VALID + j] = p[:, 0] < ROWS[j]
        c[:, C_TOK + j] = p[:, 0] + OFF[j]
    e = np.arange(EXPERTS)
    c[:, C_EOFF:C_EOFF + EXPERTS] = e * (nb * T + 128)
    c[:, C_W8:C_W8 + EXPERTS] = EXPERTS - e
    c[:, C_EI:C_EI + EXPERTS] = e
    c[0:PIX, C_CNT:C_CNT + PCH] = (rows < PATCH_DIM).sum(0).reshape(PIX, PCH)
    c[:, C_KI:] = np.arange(n_tiles)
    return c


def kernel(**inputs):
    import numpy as np
    import concourse.bacc as bacc
    from concourse.bass_utils import run_bass_kernel_spmd

    a = {k: np.ascontiguousarray(v) for k, v in inputs.items()}
    nb = a["x"].shape[0]
    pix, rows = _layout(np)
    padded = np.pad(a["x"], ((0, 0), (0, 0), (1, 1), (1, 1)))
    side = 14
    cc = np.array([c for c, _, _ in pix])[:, None, None]
    yy = np.array([y for _, y, _ in pix])[:, None, None] + 16 * np.arange(side)[None, :, None]
    xx = np.array([x for _, _, x in pix])[:, None, None] + 16 * np.arange(side)[None, None, :]
    patches = padded[:, cc, yy, xx].reshape(nb, PIX, PCH, NPATCH)

    def shifted(w):
        w = np.concatenate([w, np.zeros((1,) + w.shape[1:], w.dtype)])
        return np.ascontiguousarray(np.moveaxis(w[rows].reshape((5, PIX, PCH) + w.shape[1:]), 0, 1))

    arrays = {
        "x": patches, "txt": a["txt"],
        "wtok": shifted(a["L0_tok_W"]), "gam": shifted(a["L0_tok_ln_gamma"]), "bet": shifted(a["L0_tok_ln_beta"]),
        "btok": a["L0_tok_b"], "wattn": a["L0_attn_W_attn"], "battn": a["L0_attn_b_attn"],
        "wproj": a["L0_attn_W_proj"], "bproj": a["L0_attn_b_proj"], "wsw": a["L0_ffn_switch_w"],
        "bsw": a["L0_ffn_switch_b"], "w1": a["L0_ffn_w1"], "b1": a["L0_ffn_b1"], "w2": a["L0_ffn_w2"],
        "b2": a["L0_ffn_b2"], "const": _constants(np, nb, pix, rows),
    }
    nc = bacc.Bacc("TRN2", target_bir_lowering=False, num_devices=1)
    args = [nc.dram_tensor("in_" + n, arrays[n].shape, mybir.dt.from_np(arrays[n].dtype), kind="ExternalInput").ap()
            for n in _INS]
    out = nc.dram_tensor("out_0_dram", (nb * T, D), F32, kind="ExternalOutput").ap()
    build(nc, *args, out)
    r = run_bass_kernel_spmd(nc, [{"in_" + n: arrays[n] for n in _INS}], core_ids=[0])
    return r.results[0]["out_0_dram"].reshape(nb, T, D)
```

```python
from contextlib import ExitStack

import concourse.bass as bass
from concourse import mybir

F32 = mybir.dt.float32
F32R = mybir.dt.float32r
BF16 = mybir.dt.bfloat16
I32 = mybir.dt.int32
ALU = mybir.AluOpType
ACT = mybir.ActivationFunctionType
AX_X = mybir.AxisListType.X

D = 192
HC = D // 2
HEADS, HD = 12, 16
HG = HEADS // 2
EXPERTS, FF = 8, 768
FCH = FF // 128
PIX, PCH = 121, 8
NPATCH, NTXT = 196, 128
T = NPATCH + NTXT
ROWS = [NPATCH // 2, NPATCH // 2, NTXT]
OFF = [0, ROWS[0], 2 * ROWS[0]]
HT = ROWS[0]
WIN = 64
QB = 54
NBLK = T // QB
KW = QB + WIN - 1
PAD = WIN - 1
VTOK = 2 * QB
VD = HEADS * (HD + 1)
ORDER = [0, 3, 1, 4, 2, 5]
UNITS = HG * NBLK // 4
PATCH_DIM = 16 * 16 * 15
EPS = 1e-5
NEG = -1e30
RW = D + 4
SKIP = 1000000
TAU_STEPS, IDX_STEPS = 27, 14

C_ID = 0
C_VALID = C_ID + 128
C_TOK = C_VALID + 3
C_EOFF = C_TOK + 3
C_W8 = C_EOFF + EXPERTS
C_EI = C_W8 + EXPERTS
C_CNT = C_EI + EXPERTS
C_KI = C_CNT + 1
M_UT = 0
M_MQ = M_UT + 128
M_MT = M_MQ + 3 * KW
MASKS = M_MT + 3 * QB


def cut(ap):
    return ap.bitcast(F32R)


def tiles_of(tokens):
    full = (tokens + EXPERTS * 127) // 128
    return -(-full // 4) * 4


def build(nc, x, txt, wtok, gam, bet, btok, wattn, battn, wproj, bproj, wsw, bsw, w1, b1, w2, b2, const, out):
    NB = x.shape[0]
    N = NB * T
    CAP = int(1.25 * N / EXPERTS)
    CAPR = N + 128
    DUMMY = EXPERTS * CAPR
    NT = tiles_of(N)
    NTP = NT + 4
    TILES = 3 * NB
    CW = C_KI + NTP

    with ExitStack() as ctx:
        def sb(name, shape, dt=F32):
            return ctx.enter_context(nc.sbuf_tensor(name, shape, dt))

        first_part = ExitStack()

        def early(name, shape, dt=F32):
            return first_part.enter_context(nc.sbuf_tensor(name, shape, dt))

        def sem(name):
            return ctx.enter_context(nc.semaphore(name))

        cst = sb("cst", [128, CW])
        ident = cst[:, C_ID:C_ID + 128]
        ones = sb("ones", [128, 128])
        onesb = sb("onesb", [128, 128], BF16)
        neghalf = sb("neghalf", [128, 3])
        epsc = sb("epsc", [128, 3])
        pause = sb("pause", [128, 1])
        gpause = sb("gpause", [128, 1])
        B2 = sb("B2", [128, EXPERTS, D])
        scratch = sb("scratch", [128, 4 * RW + 2 * D])
        btrow = sb("btrow", [1, D])
        SW = sb("SW", [HC + 1, 2, EXPERTS])

        negmu = sb("negmu", [HT, 2, 1])
        msq = sb("msq", [HT, 2, 1])
        tvar = sb("tvar", [HT, 2, 1])
        tve = sb("tve", [HT, 2, 1])
        trstd = sb("trstd", [HT, 2, 1])
        BN = sb("BN", [128, 3, 6])
        MV = sb("MV", [128, 3, 2])
        ve1 = sb("ve1", [128, 3])
        rstd1 = sb("rstd1", [128, 3])

        rec = sb("rec", [128, HEADS])
        BN2 = sb("BN2", [128, 3, 6])
        ve2 = sb("ve2", [128, 3])
        LM = sb("LM", [128, 3])
        LS = sb("LS", [128, 3, EXPERTS])
        EL = sb("EL", [128, 3, EXPERTS])
        ES = sb("ES", [128, 3])
        EQ = sb("EQ", [128, 3, EXPERTS])
        SC = sb("SC", [128, 3, EXPERTS])
        MX = sb("MX", [128, 3])
        OH = sb("OH", [128, 3, EXPERTS])
        OHb = sb("OHb", [128, 3, EXPERTS], BF16)
        POS = sb("POS", [128, 3, EXPERTS])
        SLF = sb("SLF", [128, 3])
        SLI = sb("SLI", [128, 3], I32)
        BASE = sb("BASE", [128, EXPERTS])
        TK = sb("TK", [128, 3])
        PME = sb("PME", [128, TILES, EXPERTS])

        TIDX = sb("TIDX", [128, TILES])
        MID = sb("MID", [128, EXPERTS])
        STEP = sb("STEP", [128, EXPERTS])
        CN = sb("CN", [128, EXPERTS])
        CNb = sb("CNb", [128, EXPERTS], BF16)
        INC = sb("INC", [128, EXPERTS])
        TAU = sb("TAU", [128, EXPERTS])
        IDX = sb("IDX", [128, EXPERTS])
        CI = sb("CI", [128, EXPERTS], I32)
        CI2 = sb("CI2", [128, EXPERTS], I32)
        CNTI = sb("CNTI", [128, EXPERTS], I32)
        NTE = sb("NTE", [128, EXPERTS])
        FI = sb("FI", [1, EXPERTS])
        FE = sb("FE", [1, EXPERTS])
        AE = sb("AE", [1, EXPERTS])
        IN3 = scratch[0:1, 0:NTP * EXPERTS].rearrange("p (n e) -> p n e", e=EXPERTS)
        TBF = sb("TBF", [1, 2, NTP])
        TBI = sb("TBI", [1, 2, NTP], I32)

        RT = scratch[:, 0:4 * RW].rearrange("p (u d) -> p u d", u=4)
        Y1 = scratch[:, 4 * RW:4 * RW + D]
        Y2 = scratch[:, 4 * RW + D:4 * RW + 2 * D]
        ceq = sb("ceq", [128, 1])
        clt = sb("clt", [128, 1])
        ckp = sb("ckp", [128, 1])
        c1 = sb("c1", [128, 1])
        c2 = sb("c2", [128, 1])
        OI = sb("OI", [128, 4], I32)

        W1 = early("W1", [HC + 1, 2, EXPERTS, FF])
        W2 = early("W2", [128, EXPERTS, FCH, D])
        WS = W2[:, :, :, :].rearrange("p e f d -> p (e f d)")[0:PIX, 0:5 * PCH * D].rearrange(
            "p (s k d) -> p s k d", s=5, k=PCH)
        XT2 = early("XT2", [HC + 1, 2, T])
        arena = early("arena", [128, HEADS * T])
        QD = arena[0:HC + 1, :].rearrange("p (h t) -> p h t", h=HEADS)
        KEYS = max(TILES, NTP) * EXPERTS
        GE = arena[:, 0:TILES * EXPERTS].rearrange("p (g e) -> p g e", e=EXPERTS)
        KEY = arena[:, KEYS:KEYS + TILES * EXPERTS].rearrange("p (g e) -> p g e", e=EXPERTS)
        IN1 = arena[0:1, 0:NTP * EXPERTS].rearrange("p (n e) -> p n e", e=EXPERTS)
        IN2 = arena[0:1, KEYS:KEYS + NTP * EXPERTS].rearrange("p (n e) -> p n e", e=EXPERTS)
        ZR = early("ZR", [128, RW])
        masks = early("masks", [128, MASKS])
        identb = early("identb", [128, 128], BF16)
        utrib = early("utrib", [128, 128], BF16)
        mqb = early("mqb", [2 * QB, NBLK + 2, KW], BF16)
        mtb = early("mtb", [128, 3, QB], BF16)
        GM = early("GM", [PIX, 5, PCH])
        BT = early("BT", [PIX, 5, PCH])
        WE = early("WE", [PIX, PCH, D + 2])
        csum = early("csum", [HT, D])
        tbias = early("tbias", [HT, D])
        WA = early("WA", [HC + 1, 2, 2 * D])
        WV = early("WV", [HC + 1, 2, HEADS, HD + 1])
        WP = early("WP", [HC + 1, 2, D])
        img = early("img", [PIX, PCH, NPATCH])
        sq = early("sq", [PIX, PCH, NPATCH])
        WTMP = sq[:, :, 0:D]
        ssq = early("ssq", [PIX, NPATCH])
        H = early("H", [128, 3, D])
        R = early("R", [128, 3, D])
        TMP = early("TMP", [HT, 2, D])
        XN = early("XN", [128, 3, D])
        XT = early("XT", [HC + 1, 2, PAD + T])
        QS = early("QS", [HC, 2, T])
        QSb = early("QSb", [HC, 2, T], BF16)
        KT = early("KT", [HC + 1, 2, PAD + T])
        KTb = early("KTb", [HC, 2, PAD + T], BF16)
        QDb = early("QDb", [HC, HG, NBLK, 2, QB], BF16)
        VT = early("VT", [VTOK, 3, VD])
        V = early("V", [KW, NBLK, VD])
        M = early("M", [2 * QB, 80])
        mT = early("mT", [4 * UNITS, 2 * QB])
        PR = early("PR", [KW, 2, 2, HG * QB])
        ysb = early("ysb", [128, D])
        YT = early("YT", [HC + 1, 2, T])
        ROW = early("ROW", [128, 3, RW])
        XN2 = early("XN2", [128, 3, D])
        first_part.close()

        W1L = sb("W1L", [HC + 1, 2, EXPERTS, FF])
        W2L = sb("W2L", [128, EXPERTS, FCH, D])
        XMTH = sb("XMTH", [HC + 1, 2, 2, 128])
        XMTL = sb("XMTL", [HC, 2, 2, 128])
        XM = sb("XM", [128, 4, D])
        OT = sb("OT", [128, 4, D])
        HS = sb("HS", [128, FF])
        HTH = sb("HTH", [128, FCH, 128])
        HTL = sb("HTL", [128, FCH, 128])
        W1H = sb("W1H", [HC + 1, 2, EXPERTS, FF])
        W2H = sb("W2H", [128, EXPERTS, FCH, D])

        ST = ctx.enter_context(nc.psum_tensor("ST", [128, 4, 512], F32))
        Y = ctx.enter_context(nc.psum_tensor("Y", [128, 512], F32))
        G = ctx.enter_context(nc.psum_tensor("G", [128, 3, 512], F32))

        XS = nc.dram_tensor("dispatched", [DUMMY + 128, RW], F32, kind="Internal").ap()

        s_set = sem("s_set")
        s_tokw = sem("s_tokw")
        s_exp = sem("s_exp")
        s_img = sem("s_img")
        s_txt = sem("s_txt")
        s_qd = sem("s_qd")
        s_qdb = sem("s_qdb")
        s_v = sem("s_v")
        s_mrow = sem("s_mrow")
        s_scat = sem("s_scat")
        p_set = sem("p_set")
        p_tok = sem("p_tok")
        p_xt = sem("p_xt")
        p_qkv = sem("p_qkv")
        p_st = sem("p_st")
        p_pv = sem("p_pv")
        p_yt = sem("p_yt")
        p_proj = sem("p_proj")
        p_smax = sem("p_smax")
        p_lt = sem("p_lt")
        p_log = sem("p_log")
        p_mt = sem("p_mt")
        p_pref = sem("p_pref")
        p_cnt = sem("p_cnt")
        p_mx = sem("p_mx")
        p_l1 = sem("p_l1")
        p_ht = sem("p_ht")
        p_l2 = sem("p_l2")
        a_sq = sem("a_sq")
        a_xt = sem("a_xt")
        a_qk = sem("a_qk")
        a_v = sem("a_v")
        a_exp = sem("a_exp")
        a_yt = sem("a_yt")
        a_r = sem("a_r")
        a_lt = sem("a_lt")
        a_el = sem("a_el")
        a_mx = sem("a_mx")
        a_gelu = sem("a_gelu")
        a_split = sem("a_split")
        a_ht = sem("a_ht")
        d_set = sem("d_set")
        d_we = sem("d_we")
        d_sq = sem("d_sq")
        d_tvar = sem("d_tvar")
        d_tok = sem("d_tok")
        d_mv = sem("d_mv")
        d_xn = sem("d_xn")
        d_norm = sem("d_norm")
        d_h2 = sem("d_h2")
        d_mv2 = sem("d_mv2")
        d_xn2 = sem("d_xn2")
        d_max = sem("d_max")
        d_ls = sem("d_ls")
        d_log = sem("d_log")
        d_oh = sem("d_oh")
        d_mt = sem("d_mt")
        d_pref = sem("d_pref")
        d_row = sem("d_row")
        d_cn = sem("d_cn")
        d_tab = sem("d_tab")
        d_xm = sem("d_xm")
        d_xl = sem("d_xl")
        d_ht = sem("d_ht")
        d_out = sem("d_out")
        d_y = sem("d_y")
        c_set = sem("c_set")
        c_front = sem("c_front")
        c_back = sem("c_back")
        c_route = sem("c_route")
        c_srch = sem("c_srch")
        c_moe = sem("c_moe")
        g_set = sem("g_set")
        g_te = sem("g_te")
        g_trstd = sem("g_trstd")
        g_e1 = sem("g_e1")
        g_r1 = sem("g_r1")
        g_e2 = sem("g_e2")
        g_r2 = sem("g_r2")
        g_hold = sem("g_hold")
        g_split = sem("g_split")
        s_pad = sem("s_pad")
        s_row = [sem(f"s_row{u}") for u in range(4)]
        s_out = [sem(f"s_out{u}") for u in range(4)]

        parts = [(W1H[0:HC + c, c, e:e + 2, :], W1L[0:HC + c, c, e:e + 2, :], W1[0:HC + c, c, e:e + 2, :])
                 for c in range(2) for e in range(0, EXPERTS, 2)]
        parts += [(W2H[:, e, :, :], W2L[:, e, :, :], W2[:, e, :, :]) for e in range(EXPERTS)]

        block = ctx.enter_context(nc.Block())

        SET_LOADS = 13
        EXP_LOADS = 5

        @block.sync
        def _(sp):
            def load_txt(i):
                sp.dma_start(H[:, 2, :], txt[bass.ds(i, 1), :, :].rearrange("o t d -> t (o d)")).then_inc(s_txt, 16)

            def load_img(i):
                sp.dma_start(img[:, :, :], x[bass.ds(i, 1), :, :, :].rearrange("o p k n -> p (o k) n")).then_inc(
                    s_img, 16)

            sp.dma_start(cst[:, :], const[:, MASKS:MASKS + CW]).then_inc(s_set, 16)
            sp.dma_start(masks[:, :], const[:, 0:MASKS]).then_inc(s_set, 16)
            load_img(0)
            sp.dma_start(WS[:, :, :, :], wtok).then_inc(s_tokw, 16)
            sp.dma_start(GM[:, :, :], gam).then_inc(s_tokw, 16)
            sp.dma_start(BT[:, :, :], bet).then_inc(s_tokw, 16)
            sp.dma_start(btrow[:, :], btok.rearrange("(o d) -> o d", o=1)).then_inc(s_tokw, 16)
            sp.dma_start(WA[0:HC, :, :], wattn[:, 0:2 * D].rearrange("(c k) n -> k c n", c=2)).then_inc(s_set, 16)
            sp.dma_start(WA[HC:HC + 1, 1, :], battn[0:2 * D].rearrange("(o d) -> o d", o=1)).then_inc(s_set, 16)
            for c in range(2):
                sp.dma_start(WV[0:HC, c, :, 0:HD], wattn[c * HC:(c + 1) * HC, 2 * D:3 * D].rearrange(
                    "k (h d) -> k h d", d=HD)).then_inc(s_set, 16)
            sp.dma_start(WV[HC:HC + 1, 1, :, 0:HD], battn[2 * D:3 * D].rearrange("(o h d) -> o h d", o=1, d=HD)).then_inc(
                s_set, 16)
            sp.dma_start(WP[0:HC, :, :], wproj.rearrange("(c k) n -> k c n", c=2)).then_inc(s_set, 16)
            sp.dma_start(WP[HC:HC + 1, 1, :], bproj.rearrange("(o d) -> o d", o=1)).then_inc(s_set, 16)
            sp.dma_start(SW[0:HC, :, :], wsw.rearrange("(c k) n -> k c n", c=2)).then_inc(s_set, 16)
            sp.dma_start(SW[HC:HC + 1, 1, :], bsw.rearrange("(o d) -> o d", o=1)).then_inc(s_set, 16)
            sp.dma_start(B2[:, :, :], b2.partition_broadcast(128)).then_inc(s_set, 16)
            sp.wait_ge(d_set, 1)
            load_txt(0)
            sp.dma_start(W1[HC:HC + 1, 1, :, :], b1.rearrange("(o e) f -> o e f", o=1)).then_inc(s_set, 16)
            for e in range(0, EXPERTS, 4):
                for c in range(2):
                    sp.dma_start(W1[0:HC, c, e:e + 4, :],
                                 w1[e:e + 4, c * HC:(c + 1) * HC, :].rearrange("e k f -> k e f")).then_inc(s_exp, 16)
            sp.wait_ge(p_set, 2)
            sp.wait_ge(d_we, 1)
            sp.dma_start(W2[:, :, :, :].rearrange("p e f d -> p (e f) d"),
                         w2.rearrange("e (f p) d -> p (e f) d", p=128)).then_inc(s_exp, 16)

            def front(i, more):
                sp.wait_ge(p_tok, i + 1)
                if more:
                    sp.wait_ge(a_sq, i + 1)
                    load_img(i + 1)
                sp.wait_ge(a_qk, 4 * i + 2)
                for a in range(HG):
                    sp.dma_start(QDb[HD * a:HD * a + HD, 2 * (a % 3):2 * (a % 3) + 2, :, a // 3, :],
                                 QSb[HD * a:HD * a + HD, :, :].rearrange("p g (t q) -> p g t q", q=QB)).then_inc(
                                     s_qdb, 16)
                if not (isinstance(i, int) and i == 0):
                    sp.wait_ge(p_st, 6 * i)
                for a in range(HG):
                    sp.dma_start(QD[HD * a:HD * a + HD, 2 * a:2 * a + 2, :],
                                 QS[HD * a:HD * a + HD, :, :]).then_inc(s_qd, 16)
                if not (isinstance(i, int) and i == 0):
                    sp.wait_ge(p_pv, 6 * i)
                sp.wait_ge(a_v, 2 * i + 2)
                for par, rows, before in ((0, QB, PAD), (1, VTOK, KW - VTOK)):
                    win = V[:, :, :].rearrange("p (s w) d -> p w s d", w=2)
                    sp.dma_start(win[before:KW, par, :, :], VT[0:rows, :, :]).then_inc(s_v, 16)
                    sp.dma_start(win[0:before, par, 1:3, :], VT[VTOK - before:VTOK, 0:2, :]).then_inc(s_v, 16)
                if more:
                    sp.wait_ge(a_r, i + 1)
                    load_txt(i + 1)
                sp.wait_ge(d_mt, i + 1)
                for par in range(2):
                    sp.dma_start(QD[HC:HC + 1, HG * par:HG * par + HG, :], mT[:, QB * par:QB * par + QB]).then_inc(s_mrow, 16)

            front(0, NB > 1)
            if NB > 2:
                with sp.Fori(1, NB - 1) as i:
                    front(i, True)
            if NB > 1:
                front(NB - 1, False)

            sp.wait_ge(d_tab, 1)
            for e in range(EXPERTS):
                r = sp.value_load(CNTI[0:1, e:e + 1], min_val=0, max_val=N)
                sp.dma_start(XS[bass.ds(r + e * CAPR, 128), :], ZR[:, :]).then_inc(s_pad, 16)
            sp.dma_start(XS[DUMMY:DUMMY + 128, :], ZR[:, :]).then_inc(s_pad, 16)
            sp.wait_ge(s_pad, 16 * (EXPERTS + 1))
            sp.wait_ge(s_scat, 48 * NB)

            def load_rows(k, u, free):
                r = sp.value_load(TBI[0:1, 0, bass.ds(k, 1)], min_val=0, max_val=DUMMY)
                if free is not None:
                    sp.wait_ge(d_out, free)
                sp.dma_start(RT[:, u, :], XS[bass.ds(r, 128), :]).then_inc(s_row[u], 16)

            for k in range(4):
                load_rows(k, k, None)
            with sp.Fori(0, NT // 4) as it:
                for u in range(4):
                    k = it * 4 + u
                    load_rows(k + 4, u, k + 1)
            for u in range(4):
                sp.wait_ge(s_row[u], 16 * (NT // 4 + 1))

        @block.gpsimd
        def _(gp):
            nc.gpsimd.memset(neghalf[:, :], -0.5).then_inc(g_set, 1)
            nc.gpsimd.memset(epsc[:, :], EPS).then_inc(g_set, 1)
            nc.gpsimd.memset(QD[:, :, :], 0.0).then_inc(g_set, 1)
            nc.gpsimd.memset(QDb[:, :, :, :, :], 0.0).then_inc(g_set, 1)
            nc.gpsimd.memset(XT[:, :, :], 0.0).then_inc(g_set, 1)
            nc.gpsimd.memset(KT[:, :, :], 0.0).then_inc(g_set, 1)
            nc.gpsimd.memset(KTb[:, :, :], 0.0).then_inc(g_set, 1)
            nc.gpsimd.memset(V[:, :, :], 1.0).then_inc(g_set, 1)
            gp.wait_ge(g_set, 8)
            nc.gpsimd.memset(XT[HC:HC + 1, :, :], 1.0).then_inc(g_set, 1)
            nc.gpsimd.memset(KT[HC:HC + 1, :, :], 1.0).then_inc(g_set, 1)
            nc.gpsimd.memset(YT[HC:HC + 1, :, :], 1.0).then_inc(g_set, 1)
            nc.gpsimd.memset(XT2[HC:HC + 1, :, :], 1.0).then_inc(g_set, 1)
            gp.wait_ge(g_set, 12)

            def hold():
                return nc.gpsimd.tensor_tensor(gpause[:, :], neghalf[:, 0:1], neghalf[:, 0:1], ALU.add)

            def front(i):
                gp.wait_ge(d_tvar, i + 1)
                nc.gpsimd.tensor_tensor(tve[:, :, 0], tvar[:, :, 0], epsc[0:HT, 0:2], ALU.add).then_inc(g_te, 1)
                gp.wait_ge(g_te, i + 1)
                nc.gpsimd.tensor_tensor(trstd[:, :, 0], tve[:, :, 0], neghalf[0:HT, 0:2], ALU.pow).then_inc(g_trstd, 1)
                gp.wait_ge(d_mv, i + 1)
                nc.gpsimd.tensor_tensor(ve1[:, :], MV[:, :, 1], epsc[:, :], ALU.add).then_inc(g_e1, 1)
                gp.wait_ge(g_e1, i + 1)
                nc.gpsimd.tensor_tensor(rstd1[:, :], ve1[:, :], neghalf[:, :], ALU.pow).then_inc(g_r1, 1)

            def second(a):
                gp.wait_ge(d_mv2, a + 1)
                nc.gpsimd.tensor_tensor(ve2[:, :], ROW[:, :, D + 1], epsc[:, :], ALU.add).then_inc(g_e2, 1)
                gp.wait_ge(g_e2, a + 1)
                nc.gpsimd.tensor_tensor(ROW[:, :, D + 1], ve2[:, :], neghalf[:, :], ALU.pow).then_inc(g_r2, 1)

            def scatter(a):
                gp.wait_ge(d_row, a + 1)
                hold()
                for j in range(3):
                    gp.indirect_dma_start(XS[:, :], bass.IndirectOffsetOnAxis(ap=SLI[0:ROWS[j], j:j + 1], axis=0),
                                          ROW[0:ROWS[j], j, :], None, bounds_check=DUMMY - 1,
                                          oob_is_err=False).then_inc(s_scat, 16)

            front(0)
            front(1)
            second(0)
            with gp.Fori(2, NB) as i:
                front(i)
                scatter(i - 2)
                second(i - 1)
            scatter(NB - 2)
            second(NB - 1)
            scatter(NB - 1)

            for n, (high, low, weights) in enumerate(parts):
                gp.wait_ge(a_split, n + 1)
                nc.gpsimd.tensor_tensor(cut(low), weights, high, ALU.subtract).then_inc(g_split, 1)

            gp.wait_ge(g_r2, NB)
            nc.gpsimd.tensor_tensor(ve2[:, :], epsc[:, :], epsc[:, :], ALU.add).then_inc(g_hold, 1)
            with gp.Fori(0, NT // 4) as it:
                for u in range(4):
                    k = it * 4 + u
                    gp.wait_ge(g_hold, k + 1)
                    gp.wait_ge(d_out, k + 1)
                    hold().then_inc(g_hold, 1)
                    gp.indirect_dma_start(out, bass.IndirectOffsetOnAxis(ap=OI[:, u:u + 1], axis=0),
                                          OT[:, u, :], None, bounds_check=N - 1,
                                          oob_is_err=False).then_inc(s_out[u], 16)
            for u in range(4):
                gp.wait_ge(s_out[u], 16 * (NT // 4))

        @block.scalar
        def _(act):
            copy = nc.scalar.copy

            def square(i):
                act.wait_ge(s_img, 16 * (i + 1))
                if not (isinstance(i, int) and i == 0):
                    act.wait_ge(d_sq, i)
                nc.scalar.activation(sq[:, :, :], img[:, :, :], ACT.Square).then_inc(a_sq, 1)

            def exps(a, n):
                act.wait_ge(p_st, 6 * a + n + 1)
                if n >= 2 or not (isinstance(a, int) and a == 0):
                    act.wait_ge(p_pv, 6 * a + n - 1)
                nc.scalar.activation(PR[:, n % 2, :, :], ST[0:KW, 2 * (n % 2):2 * (n % 2) + 2, 0:HG * QB],
                                     ACT.Exp).then_inc(a_exp, 1)

            def y_turned(a, j, bank):
                act.wait_ge(p_yt, 3 * a + j + 1)
                if j == 0 and not (isinstance(a, int) and a == 0):
                    act.wait_ge(p_proj, 3 * a)
                for c in range(2):
                    last = copy(YT[0:HC, c, :].rearrange("p (s j q) -> p s j q", s=2, j=3)[:, :, j, :],
                                G[0:HC, bank, 128 * c:128 * c + 128].rearrange("p (s q) -> p s q", s=2)[:, :, 0:QB])
                last.then_inc(a_yt, 1)

            def x_turned(i):
                if not (isinstance(i, int) and i == 0):
                    act.wait_ge(p_qkv, 6 * i)
                for c in range(2):
                    act.wait_ge(p_xt, 2 * i + c + 1)
                    copy(XT[0:HC, c, PAD:PAD + T], G[0:HC, 2 * c, 0:T]).then_inc(a_xt, 1)

            def queries_keys(i):
                first = isinstance(i, int) and i == 0
                if not first:
                    act.wait_ge(s_qd, 16 * HG * i)
                    act.wait_ge(s_qdb, 16 * HG * i)
                for g in range(2):
                    act.wait_ge(p_qkv, 6 * i + g + 1)
                    bank = 2 - g
                    act.mul(QS[:, g, :], G[0:HC, bank, 0:T], HD ** -0.5)
                    act.mul(QSb[:, g, :], G[0:HC, bank, 0:T], HD ** -0.5).then_inc(a_qk, 1)
                for g in range(2):
                    act.wait_ge(p_qkv, 6 * i + g + 3)
                    if g == 0 and not first:
                        act.wait_ge(p_st, 6 * i)
                        act.wait_ge(p_smax, UNITS * i)
                    copy(KT[0:HC, g, PAD:PAD + T], G[0:HC, 2 * g, 0:T])
                    copy(KTb[:, g, PAD:PAD + T], G[0:HC, 2 * g, 0:T]).then_inc(a_qk, 1)

            def values(i):
                if not (isinstance(i, int) and i == 0):
                    act.wait_ge(s_v, 64 * i)
                for n, m0, m1 in ((0, 0, 2), (1, 2, 3)):
                    act.wait_ge(p_qkv, 6 * i + n + 5)
                    copy(VT[:, m0:m1, :], G[0:VTOK, 2 * n, 0:(m1 - m0) * VD].rearrange("p (m d) -> p m d", d=VD)).then_inc(
                        a_v, 1)

            def residual(i, back):
                if back:
                    act.wait_ge(d_h2, 3 * i)
                act.wait_ge(d_xn, i + 1)
                copy(R[:, :, :], H[:, :, :]).then_inc(a_r, 1)

            def router_turned(a):
                if not (isinstance(a, int) and a == 0):
                    act.wait_ge(p_log, a)
                for c in range(2):
                    act.wait_ge(p_lt, 2 * a + c + 1)
                    copy(XT2[0:HC, c, :], G[0:HC, 2 - 2 * c, 0:T]).then_inc(a_lt, 1)

            def router_exp(a):
                act.wait_ge(d_ls, a + 1)
                nc.scalar.activation(EL[:, :, :], LS[:, :, :], ACT.Exp).then_inc(a_el, 1)

            def body(i, front, back, route, more):
                b, c = i - 1, i - 2
                if back:
                    exps(b, 0)
                    exps(b, 1)
                if route:
                    router_turned(c)
                if back:
                    exps(b, 2)
                    exps(b, 3)
                    y_turned(b, 0, 2)
                    exps(b, 4)
                if route:
                    router_exp(c)
                if front:
                    x_turned(i)
                if back:
                    exps(b, 5)
                    y_turned(b, 1, 0)
                if more:
                    square(i + 1)
                if front:
                    queries_keys(i)
                if back:
                    y_turned(b, 2, 1)
                if front:
                    values(i)
                    residual(i, back)

            act.wait_ge(g_set, 12)
            act.wait_ge(d_set, 1)
            act.wait_ge(d_we, 1)
            square(0)
            body(0, True, False, False, True)
            body(1, True, True, False, True)
            body(2, True, True, True, True)
            with act.Fori(3, NB - 1) as i:
                body(i, True, True, True, True)
            body(NB - 1, True, True, True, False)
            body(NB, False, True, True, False)
            body(NB + 1, False, False, True, False)

            act.wait_ge(s_exp, 16 * EXP_LOADS)
            act.wait_ge(s_set, 16 * SET_LOADS)
            act.wait_ge(d_row, NB)
            act.wait_ge(s_scat, 48 * NB)
            for high, _, weights in parts:
                copy(cut(high), weights).then_inc(a_split, 1)

            def turned(k, v):
                act.wait_ge(p_mx, k + 1)
                if not (isinstance(k, int) and k < 2):
                    act.wait_ge(p_l1, k - 1)
                copy(cut(XMTH[0:HC, v, :, :]), G[0:HC, 2, 0:256].rearrange("p (c n) -> p c n", c=2)).then_inc(a_mx, 1)

            def gelu(k, v):
                act.wait_ge(p_l1, k + 1)
                if not (isinstance(k, int) and k == 0):
                    act.wait_ge(p_ht, k)
                nc.scalar.activation(HS[:, :].rearrange("p (b n) -> p b n", b=2), ST[:, 2 * v:2 * v + 2, 0:FF // 2],
                                     ACT.Gelu).then_inc(a_gelu, 1)

            turned(0, 0)
            turned(1, 1)
            gelu(0, 0)

            def hidden_turned(k):
                act.wait_ge(p_ht, k + 1)
                if not (isinstance(k, int) and k == 0):
                    act.wait_ge(p_l2, k)
                for b in range(2):
                    copy(cut(HTH[:, 3 * b:3 * b + 3, :]), G[:, b, 0:384].rearrange("p (f n) -> p f n", f=3)).then_inc(
                        a_ht, 1)

            def two(it):
                for v in range(2):
                    k = it * 2 + v
                    hidden_turned(k)
                    gelu(k + 1, 1 - v)
                    turned(k + 2, v)

            two(0)
            with act.Fori(1, NT // 2) as it:
                two(it)

        @block.tensor
        def _(pe):
            mm = nc.tensor.matmul

            def halves(o, lhs, rhs):
                mm(o, lhs(0, HC), rhs(0, HC), start=True, stop=False)
                return mm(o, lhs(1, HC + 1), rhs(1, HC + 1), start=False, stop=True)

            def tokens(i, back):
                pe.wait_ge(s_img, 16 * (i + 1))
                if isinstance(i, int) and i == 1:
                    pe.wait_ge(a_v, 1)
                elif not isinstance(i, int) or i > 1:
                    pe.wait_ge(d_h2, 3 * (i - 1))
                for j in range(2):
                    for k in range(PCH):
                        if j == 0 and k == PCH // 2 and back:
                            max_turn(i - 1)
                        mm(G[0:HT, j, 0:D + 1], img[:, k, HT * j:HT * j + HT], WE[:, k, 0:D + 1],
                           start=(k == 0), stop=(k == PCH - 1))
                pe.wait_ge(d_sq, i + 1)
                for j in range(2):
                    last = mm(G[0:HT, j, D + 2:D + 3], ssq[:, HT * j:HT * j + HT], cst[0:PIX, C_CNT:C_CNT + 1],
                              start=True, stop=True)
                last.then_inc(p_tok, 1)

            def x_turn(i, back, route):
                pe.wait_ge(d_tok, i + 1)
                pe.wait_ge(d_xn, i + 1)
                for c in range(2):
                    if c == 0 and route:
                        pe.wait_ge(a_lt, 2 * (i - 2) + 2)
                    if c == 1 and back:
                        pe.wait_ge(a_yt, 3 * (i - 1) + 1)
                    for j in range(3):
                        last = nc.tensor.transpose(G[0:HC, 2 * c, OFF[j]:OFF[j] + ROWS[j]],
                                                   XN[0:ROWS[j], j, c * HC:(c + 1) * HC],
                                                   ident[0:ROWS[j], 0:ROWS[j]])
                    last.then_inc(p_xt, 1)

            def project_qk(i, back, route):
                pe.wait_ge(a_xt, 2 * i + 2)
                for n in range(4):
                    bank = (2, 1, 0, 2)[n]
                    if n == 1 and route:
                        pe.wait_ge(d_pref, i - 1)
                    if n == 2 and back:
                        pe.wait_ge(a_yt, 3 * (i - 1) + 2)
                    if n == 3:
                        pe.wait_ge(a_qk, 4 * i + 1)
                    halves(G[0:HC, bank, 0:T], lambda c, r: WA[0:r, c, HC * n:HC * n + HC],
                           lambda c, r: XT[0:r, c, PAD:PAD + T]).then_inc(p_qkv, 1)

            def project_v(i):
                for n, m0, m1 in ((0, 0, 2), (1, 2, 3)):
                    pe.wait_ge(a_qk, 4 * i + 3 + n)
                    for m in range(m0, m1):
                        last = halves(G[0:VTOK, 2 * n, VD * (m - m0):VD * (m - m0) + VD],
                                      lambda c, r: XT[0:r, c, PAD + VTOK * m:PAD + VTOK * (m + 1)],
                                      lambda c, r: WV[0:r, c, :, :].rearrange("p h d -> p (h d)"))
                    last.then_inc(p_qkv, 1)

            def maxima(i, back):
                pe.wait_ge(s_qdb, 16 * HG * (i + 1))
                pe.wait_ge(a_qk, 4 * i + 4)
                if back:
                    pe.wait_ge(a_exp, 6 * i)
                for n in range(UNITS):
                    if n >= 4:
                        pe.wait_ge(d_max, UNITS * i + n - 3)
                    t0 = 4 * n % NBLK
                    mm(ST[0:2 * QB, n % 4, 0:4 * KW], identb[0:2 * QB, 0:2 * QB], mqb[:, t0:t0 + 4, :], start=True,
                       stop=True, skip_group_check=True)
                    for m in range(4):
                        p, t = (4 * n + m) // NBLK, (4 * n + m) % NBLK
                        last = mm(ST[0:2 * QB, n % 4, KW * m:KW * m + KW],
                                  QDb[:, p, t, :, :].rearrange("p w q -> p (w q)"),
                                  KTb[:, p % 2, QB * t:QB * t + KW], start=False, stop=True, skip_group_check=True)
                    last.then_inc(p_smax, 1)

            def max_turn(i):
                pe.wait_ge(d_max, UNITS * i + UNITS)
                nc.tensor.transpose(ST[0:80, 1, 0:2 * QB], M[:, :], ident[0:2 * QB, 0:2 * QB]).then_inc(p_mt, 1)

            def scores(a, n):
                t = ORDER[n]
                if n == 0:
                    pe.wait_ge(s_qd, 16 * HG * (a + 1))
                    pe.wait_ge(s_mrow, 32 * (a + 1))
                    pe.wait_ge(d_max, UNITS * a + UNITS)
                if n >= 2:
                    pe.wait_ge(a_exp, 6 * a + n - 1)
                for g in range(2):
                    bank = 2 * (n % 2) + g
                    mm(ST[0:KW, bank, 0:HG * QB], identb[0:KW, 0:KW],
                       mtb[0:KW, min(t, 2), :].unsqueeze(1).broadcast_to([KW, HG, QB]), start=True, stop=False)
                    last = mm(ST[0:KW, bank, 0:HG * QB], KT[:, g, QB * t:QB * t + KW],
                              QD[:, g:HEADS:2, QB * t:QB * t + QB],
                             start=False, stop=True)
                last.then_inc(p_st, 1)

            def weighted(a, n):
                t, s = ORDER[n], n % 2
                pe.wait_ge(a_exp, 6 * a + n + 1)
                if n == 0:
                    pe.wait_ge(s_v, 64 * (a + 1))
                if s == 0 and not (n == 0 and isinstance(a, int) and a == 0):
                    pe.wait_ge(d_norm, 3 * a + n // 2)
                for h in range(HEADS):
                    last = mm(Y[64 * s:64 * s + QB, (HD + 1) * h:(HD + 1) * (h + 1)],
                              PR[:, n % 2, h // HG, QB * (h % HG):QB * (h % HG) + QB],
                              V[:, t, (HD + 1) * h:(HD + 1) * (h + 1)],
                              start=True, stop=True)
                last.then_inc(p_pv, 1)

            def y_turn(a, j, bank):
                pe.wait_ge(d_norm, 3 * a + j + 1)
                for c in range(2):
                    last = nc.tensor.transpose(G[0:HC, bank, 128 * c:128 * c + 118], ysb[0:118, c * HC:(c + 1) * HC],
                                               ident[0:118, 0:118])
                last.then_inc(p_yt, 1)

            def project_out(a, front):
                pe.wait_ge(a_yt, 3 * a + 3)
                for j in range(3):
                    if j > 0 and front:
                        pe.wait_ge(a_v, 2 * (a + 1) + j)
                    halves(G[0:ROWS[j], (1, 0, 2)[j], 0:D], lambda c, r: YT[0:r, c, OFF[j]:OFF[j] + ROWS[j]],
                           lambda c, r: WP[0:r, c, :]).then_inc(p_proj, 1)

            def router_turn(a, front):
                pe.wait_ge(d_h2, 3 * a + 3)
                pe.wait_ge(d_xn2, a + 1)
                for c in range(2):
                    if c == 1 and front:
                        pe.wait_ge(d_tok, a + 3)
                    for j in range(3):
                        last = nc.tensor.transpose(G[0:HC, 2 - 2 * c, OFF[j]:OFF[j] + ROWS[j]],
                                                   XN2[0:ROWS[j], j, c * HC:(c + 1) * HC],
                                                   ident[0:ROWS[j], 0:ROWS[j]])
                    last.then_inc(p_lt, 1)

            def logits(a):
                pe.wait_ge(a_lt, 2 * a + 2)
                for j in range(3):
                    last = halves(G[0:ROWS[j], 1, 8 * j:8 * j + 8], lambda c, r: XT2[0:r, c, OFF[j]:OFF[j] + ROWS[j]],
                                  lambda c, r: SW[0:r, c, :])
                last.then_inc(p_log, 1)

            def prefixes(a):
                pe.wait_ge(d_oh, a + 1)
                for j in range(3):
                    for m in range(j):
                        mm(G[:, 1, 8 * j:8 * j + 8], onesb[0:ROWS[m], :], OHb[0:ROWS[m], m, :],
                           start=(m == 0), stop=False)
                    mm(G[:, 1, 8 * j:8 * j + 8], utrib[0:ROWS[j], :], OHb[0:ROWS[j], j, :], start=(j == 0), stop=True)
                for j in range(3):
                    last = mm(G[:, 1, 24:32], onesb[0:ROWS[j], :], OHb[0:ROWS[j], j, :], start=(j == 0), stop=(j == 2))
                last.then_inc(p_pref, 1)

            def body(i, front, back, route):
                b, c = i - 1, i - 2
                if front:
                    tokens(i, back)
                elif back:
                    max_turn(b)
                if back:
                    scores(b, 0)
                if route:
                    router_turn(c, front)
                if back:
                    scores(b, 1)
                    weighted(b, 0)
                    scores(b, 2)
                    weighted(b, 1)
                if route:
                    logits(c)
                if back:
                    scores(b, 3)
                    if route:
                        pe.wait_ge(a_lt, 2 * c + 1)
                    else:
                        pe.wait_ge(a_v, 2)
                    y_turn(b, 0, 2)
                    weighted(b, 2)
                    scores(b, 4)
                    weighted(b, 3)
                if front:
                    x_turn(i, back, route)
                if route:
                    prefixes(c)
                if back:
                    scores(b, 5)
                    if front:
                        pe.wait_ge(a_xt, 2 * i + 1)
                    else:
                        pe.wait_ge(a_lt, 2 * c + 2)
                    y_turn(b, 1, 0)
                    weighted(b, 4)
                    weighted(b, 5)
                if front:
                    project_qk(i, back, route)
                if back:
                    if front:
                        pe.wait_ge(a_qk, 4 * i + 2)
                    else:
                        pe.wait_ge(d_pref, c + 1)
                    y_turn(b, 2, 1)
                if front:
                    project_v(i)
                if back:
                    project_out(b, front)
                if front:
                    maxima(i, back)

            pe.wait_ge(s_tokw, 64)
            pe.wait_ge(d_set, 1)
            n = 0
            for s in range(5):
                for k in range(PCH):
                    mm(G[0:HT, 0, 0:D], BT[:, s, k:k + 1].broadcast_to([PIX, HT]), WS[:, s, k, :],
                       start=(n == 0), stop=False)
                    n += 1
            mm(G[0:HT, 0, 0:D], ones[0:1, 0:HT], btrow[:, :], start=False, stop=True).then_inc(p_set, 1)
            pe.wait_ge(d_we, 1)
            for k in range(PCH):
                last = mm(G[0:HT, 1, 0:D], ones[0:PIX, 0:HT], WE[:, k, 0:D], start=(k == 0), stop=(k == PCH - 1))
            last.then_inc(p_set, 1)

            pe.wait_ge(s_set, 16 * SET_LOADS)
            pe.wait_ge(g_set, 12)
            pe.wait_ge(d_set, 2)
            body(0, True, False, False)
            body(1, True, True, False)
            with pe.Fori(2, NB) as i:
                body(i, True, True, True)
            body(NB, False, True, True)
            body(NB + 1, False, False, True)

            with pe.Fori(0, TAU_STEPS + IDX_STEPS) as n:
                pe.wait_ge(d_cn, n + 1)
                mm(G[:, 0, 0:8], onesb[:, :], CNb[:, :], start=True, stop=True).then_inc(p_cnt, 1)

            def turn(k, u):
                pe.wait_ge(d_xm, k + 1)
                if not (isinstance(k, int) and k == 0):
                    pe.wait_ge(d_xl, k)
                for c in range(2):
                    last = nc.tensor.transpose(G[0:HC, 2, 128 * c:128 * c + 128],
                                               XM[:, u, c * HC:(c + 1) * HC], ident[:, :])
                last.then_inc(p_mx, 1)

            def layer1(k, v):
                e = pe.value_load(TBI[0:1, 1, bass.ds(k, 1)], min_val=0, max_val=EXPERTS - 1)
                pe.wait_ge(a_mx, k + 1)
                if not (isinstance(k, int) and k < 2):
                    pe.wait_ge(a_gelu, k - 1)
                for x, w, ones_row in ((XMTH, W1H, 1), (XMTH, W1L, 1), (XMTL, W1H, 0)):
                    if x is XMTL:
                        pe.wait_ge(d_xl, k + 1)
                    for half in range(2):
                        for c in range(2):
                            r = HC + c * ones_row
                            last = mm(ST[:, 2 * v + half, 0:FF // 2], cut(x[0:r, v, c, :]),
                                      cut(w[0:r, c, bass.ds(e, 1), half * (FF // 2):(half + 1) * (FF // 2)]),
                                      start=(c == 0 and w is W1H and x is XMTH), stop=(c == 1 and x is XMTL),
                                      skip_group_check=True)
                last.then_inc(p_l1, 1)

            def hidden_turn(k):
                pe.wait_ge(a_gelu, k + 1)
                if not (isinstance(k, int) and k == 0):
                    pe.wait_ge(d_ht, 2 * k)
                for f in range(FCH):
                    last = nc.tensor.transpose(G[:, f // 3, 128 * (f % 3):128 * (f % 3) + 128],
                                               HS[:, 128 * f:128 * f + 128], ident[:, :])
                last.then_inc(p_ht, 1)

            def layer2(k):
                e = pe.value_load(TBI[0:1, 1, bass.ds(k, 1)], min_val=0, max_val=EXPERTS - 1)
                pe.wait_ge(d_y, k + 1)
                for f in range(FCH):
                    if f % 3 == 0:
                        pe.wait_ge(a_ht, 2 * k + f // 3 + 1)
                    for w in (W2H, W2L):
                        mm(Y[:, 0:D], cut(HTH[:, f, :]), cut(w[:, bass.ds(e, 1), f, :]),
                           start=(f == 0 and w is W2H), stop=False)
                for f in range(FCH):
                    if f % 3 == 0:
                        pe.wait_ge(d_ht, 2 * k + f // 3 + 1)
                    last = mm(Y[:, 0:D], cut(HTL[:, f, :]), cut(W2H[:, bass.ds(e, 1), f, :]), start=False,
                              stop=(f == FCH - 1))
                last.then_inc(p_l2, 1)

            pe.wait_ge(g_split, len(parts))
            pe.wait_ge(d_tab, 1)
            turn(0, 0)
            turn(1, 1)
            layer1(0, 0)

            def four(it):
                for u in range(4):
                    k = it * 4 + u
                    hidden_turn(k)
                    layer1(k + 1, (u + 1) % 2)
                    turn(k + 2, (u + 2) % 4)
                    layer2(k)

            four(0)
            with pe.Fori(1, NT // 4) as it:
                four(it)

        @block.vector
        def _(dve):
            class Chain:

                def __init__(self, s, base=0):
                    self.s, self.base, self.n = s, base, 0

                def __call__(self, ins):
                    self.n += 1
                    ins.then_inc(self.s, 1)
                    dve.wait_ge(self.s, self.base + self.n)

            v = nc.vector
            FRONT, BACK, ROUTE = 4, 4, 11

            v.memset(H[:, :, :], 0.0)
            v.memset(M[:, :], 0.0)
            v.memset(ones[:, :], 1.0)
            v.memset(ROW[:, :, :], 0.0)
            v.memset(Y[:, :], 1.0)
            v.memset(BASE[:, :], 0.0)
            v.memset(G[:, :, :], 0.0)
            v.memset(onesb[:, :], 1.0)
            v.memset(WE[:, :, D:D + 2], 0.0)
            v.memset(WV[0:HC, :, :, HD], 0.0)
            v.memset(WV[HC:HC + 1, :, :, HD], 1.0)
            v.memset(PME[:, :, :], 0.0).then_inc(d_set, 1)
            dve.wait_ge(d_set, 1)
            link = Chain(c_set)
            dve.wait_ge(s_set, 16 * SET_LOADS)
            v.tensor_copy(identb[:, :], ident)
            v.tensor_copy(utrib[:, :], masks[:, M_UT:M_UT + 128])
            for t in range(NBLK + 2):
                v.tensor_copy(mqb[:, t, :], masks[0:2 * QB, M_MQ + KW * min(t % NBLK, 2):M_MQ + KW * min(t % NBLK, 2) + KW])
            v.tensor_copy(mtb[:, :, :], masks[:, M_MT:MASKS].rearrange("p (v k) -> p v k", v=3))
            v.tensor_copy(TK[:, :], cst[:, C_TOK:C_TOK + 3])
            v.memset(ZR[:, :], 0.0)
            link(v.tensor_copy(WE[:, :, D], cst[0:PIX, C_CNT:C_CNT + 1].broadcast_to([PIX, PCH])))
            link(v.memset(ZR[:, D + 3:D + 4], float(SKIP)))
            dve.wait_ge(s_tokw, 64)
            link(v.tensor_tensor(WE[:, :, 0:D], WS[:, 0, :, :], GM[:, 0, :].unsqueeze(2).broadcast_to([PIX, PCH, D]),
                                 ALU.mult))
            for s in range(1, 5):
                link(v.tensor_tensor(WTMP[:, :, :], WS[:, s, :, :],
                                     GM[:, s, :].unsqueeze(2).broadcast_to([PIX, PCH, D]), ALU.mult))
                link(v.tensor_tensor(WE[:, :, 0:D], WE[:, :, 0:D], WTMP[:, :, :], ALU.add))
            v.memset(MV[:, :, :], 0.0).then_inc(d_we, 1)
            SETUP = link.n
            dve.wait_ge(p_set, 1)
            v.tensor_copy(tbias[:, :], G[0:HT, 0, 0:D])
            dve.wait_ge(p_set, 2)
            v.tensor_copy(csum[:, :], G[0:HT, 1, 0:D]).then_inc(d_set, 1)
            dve.wait_ge(d_set, 2)

            def front(i):
                link = Chain(c_front, i * FRONT)
                first = isinstance(i, int) and i == 0
                dve.wait_ge(p_tok, i + 1)
                link(v.tensor_scalar(negmu[:, :, :], G[0:HT, 0:2, D:D + 1], -1.0 / PATCH_DIM, None, ALU.mult))
                link(v.tensor_tensor(msq[:, :, :], negmu[:, :, :], negmu[:, :, :], ALU.mult))
                v.scalar_tensor_tensor(tvar[:, :, :], G[0:HT, 0:2, D + 2:D + 3], 1.0 / PATCH_DIM, msq[:, :, :],
                                       ALU.mult, ALU.subtract).then_inc(d_tvar, 1)
                for j in range(2):
                    last = v.scalar_tensor_tensor(TMP[:, j, :], csum[:, :], negmu[:, j, :], G[0:HT, j, 0:D],
                                                  ALU.mult, ALU.add)
                last.then_inc(d_tok, 1)
                dve.wait_ge(d_tok, i + 1)
                dve.wait_ge(g_trstd, i + 1)
                if not first:
                    dve.wait_ge(a_r, i)
                for j in range(2):
                    last = v.scalar_tensor_tensor(H[0:HT, j, :], TMP[:, j, :], trstd[:, j, :], tbias[:, :],
                                                  ALU.mult, ALU.add)
                link(last)
                dve.wait_ge(s_txt, 16 * (i + 1))
                for j in range(3):
                    last = v.bn_stats(BN[:, j, :], H[:, j, :])
                link(last)
                v.memset(pause[:, :], 0.0)
                for j in range(3):
                    last = v.bn_aggr(MV[:, j, :], BN[:, j, :])
                last.then_inc(d_mv, 1)
                dve.wait_ge(d_mv, i + 1)
                dve.wait_ge(g_r1, i + 1)
                if not first:
                    dve.wait_ge(p_xt, 2 * i)
                for j in range(3):
                    last = v.tensor_scalar(XN[:, j, :], H[:, j, :], MV[:, j, 0:1], rstd1[:, j:j + 1],
                                           ALU.subtract, ALU.mult)
                last.then_inc(d_xn, 1)
                assert link.n == FRONT

            def squares(i):
                dve.wait_ge(a_sq, i + 1)
                if not (isinstance(i, int) and i == 0):
                    dve.wait_ge(p_tok, i)
                v.tensor_reduce(ssq[:, :], sq[:, :, :].rearrange("p k n -> p n k"), AX_X, ALU.add).then_inc(d_sq, 1)

            def maxima(i):
                first = isinstance(i, int) and i == 0
                if not first:
                    dve.wait_ge(p_mt, i)
                for n in range(UNITS):
                    dve.wait_ge(p_smax, UNITS * i + n + 1)
                    v.tensor_reduce(M[:, 4 * n:4 * n + 4], ST[0:2 * QB, n % 4, 0:4 * KW].rearrange("p (h k) -> p h k", h=4),
                                    AX_X, ALU.max, negate=True).then_inc(d_max, 1)

            def max_rows(i):
                dve.wait_ge(p_mt, i + 1)
                if not (isinstance(i, int) and i == 0):
                    dve.wait_ge(s_mrow, 32 * i)
                v.tensor_copy(mT[:, :], ST[0:4 * UNITS, 1, 0:2 * QB]).then_inc(d_mt, 1)

            def normalise(a, j, link):
                dve.wait_ge(p_pv, 6 * a + 2 * j + 2)
                if not (j == 0 and isinstance(a, int) and a == 0):
                    dve.wait_ge(p_yt, 3 * a + j)
                yv = Y[:, 0:HEADS * (HD + 1)].rearrange("p (h d) -> p h d", h=HEADS)
                link(v.reciprocal(rec[:, :], yv[:, :, HD]))
                v.tensor_tensor(ysb[:, :].rearrange("p (h d) -> p h d", h=HEADS), yv[:, :, 0:HD],
                                rec[:, :].unsqueeze(2).broadcast_to([128, HEADS, HD]), ALU.mult).then_inc(d_norm, 1)

            def second(a, link):
                first = isinstance(a, int) and a == 0
                if not first:
                    dve.wait_ge(s_scat, 48 * a)
                dve.wait_ge(a_r, a + 1)
                for j in range(3):
                    dve.wait_ge(p_proj, 3 * a + j + 1)
                    v.tensor_tensor(ROW[0:ROWS[j], j, 0:D], G[0:ROWS[j], (1, 0, 2)[j], 0:D], R[0:ROWS[j], j, :],
                                    ALU.add).then_inc(d_h2, 1)
                dve.wait_ge(d_h2, 3 * a + 3)
                for j in range(3):
                    last = v.bn_stats(BN2[:, j, :], ROW[:, j, 0:D])
                link(last)
                v.memset(pause[:, :], 0.0)
                for j in range(3):
                    last = v.bn_aggr(ROW[:, j, D:D + 2], BN2[:, j, :])
                last.then_inc(d_mv2, 1)

            def router_rows(a):
                first = isinstance(a, int) and a == 0
                dve.wait_ge(d_mv2, a + 1)
                dve.wait_ge(g_r2, a + 1)
                if not first:
                    dve.wait_ge(p_lt, 2 * a)
                for j in range(3):
                    last = v.tensor_scalar(XN2[:, j, :], ROW[:, j, 0:D], ROW[:, j, D:D + 1], ROW[:, j, D + 1:D + 2],
                                           ALU.subtract, ALU.mult)
                last.then_inc(d_xn2, 1)

            def wide(ap):
                return ap.unsqueeze(2).broadcast_to([128, 3, EXPERTS])

            def per_expert(ap):
                return ap.unsqueeze(1).broadcast_to([128, 3, EXPERTS])

            def route(a, link):
                dve.wait_ge(p_log, a + 1)
                lg = G[:, 1, 0:24].rearrange("p (j e) -> p j e", j=3)
                link(v.tensor_reduce(LM[:, :], lg, AX_X, ALU.max))
                if not (isinstance(a, int) and a == 0):
                    dve.wait_ge(a_el, a)
                v.tensor_tensor(LS[:, :, :], lg, wide(LM[:, :]), ALU.subtract).then_inc(d_ls, 1)
                v.tensor_tensor(EQ[:, :, :], lg, wide(LM[:, :]), ALU.is_equal).then_inc(d_log, 1)
                dve.wait_ge(d_log, a + 1)
                link(v.tensor_tensor(SC[:, :, :], EQ[:, :, :], per_expert(cst[:, C_W8:C_W8 + 8]), ALU.mult))
                link(v.tensor_reduce(MX[:, :], SC[:, :, :], AX_X, ALU.max))
                link(v.tensor_tensor(EQ[:, :, :], SC[:, :, :], wide(MX[:, :]), ALU.is_equal))
                if not (isinstance(a, int) and a == 0):
                    dve.wait_ge(p_pref, a)
                v.tensor_tensor(OH[:, :, :], EQ[:, :, :], wide(cst[:, C_VALID:C_VALID + 3]), ALU.mult)
                v.tensor_tensor(OHb[:, :, :], EQ[:, :, :], wide(cst[:, C_VALID:C_VALID + 3]), ALU.mult).then_inc(
                    d_oh, 1)
                dve.wait_ge(a_el, a + 1)
                link(v.tensor_reduce(ES[:, :], EL[:, :, :], AX_X, ALU.add))
                link(v.reciprocal(ROW[:, :, D + 2], ES[:, :]))

            def place(a, link):
                dve.wait_ge(p_pref, a + 1)
                dve.wait_ge(d_oh, a + 1)
                link(v.tensor_tensor(POS[:, :, :], G[:, 1, 0:24].rearrange("p (j e) -> p j e", j=3),
                                     per_expert(BASE[:, :]), ALU.add))
                v.tensor_tensor(BASE[:, :], BASE[:, :], G[:, 1, 24:32], ALU.add).then_inc(d_pref, 1)
                dve.wait_ge(d_pref, a + 1)
                link(v.tensor_tensor(POS[:, :, :], POS[:, :, :], per_expert(cst[:, C_EOFF:C_EOFF + 8]), ALU.add))
                link(v.tensor_tensor(POS[:, :, :], POS[:, :, :], OH[:, :, :], ALU.mult))
                link(v.tensor_reduce(SLF[:, :], POS[:, :, :], AX_X, ALU.add))
                v.tensor_copy(SLI[:, :], SLF[:, :])
                v.tensor_tensor(PME[:, bass.ds(3 * a, 3), :], OH[:, :, :], wide(ROW[:, :, D + 2]), ALU.mult)
                link(v.tensor_copy(ROW[:, :, D + 3], TK[:, :]))
                v.tensor_scalar(TK[:, :], TK[:, :], float(T), None, ALU.add).then_inc(d_row, 1)
                dve.wait_ge(d_row, a + 1)

            def body(i, do_front, back, do_route, more):
                b, c = i - 1, i - 2
                link, rlink = Chain(c_back, b * BACK), Chain(c_route, c * ROUTE)
                if do_front:
                    front(i)
                if back:
                    normalise(b, 0, link)
                if do_route:
                    route(c, rlink)
                if back:
                    normalise(b, 1, link)
                if do_route:
                    place(c, rlink)
                    assert rlink.n == ROUTE
                if back:
                    normalise(b, 2, link)
                if more:
                    squares(i + 1)
                if back:
                    second(b, link)
                    assert link.n == BACK
                if do_front:
                    maxima(i)
                if back:
                    router_rows(b)
                if do_front:
                    max_rows(i)

            squares(0)
            body(0, True, False, False, True)
            body(1, True, True, False, True)
            body(2, True, True, True, True)
            with dve.Fori(3, NB - 1) as i:
                body(i, True, True, True, True)
            body(NB - 1, True, True, True, False)
            body(NB, False, True, True, False)
            body(NB + 1, False, False, True, False)

            link = Chain(c_set, SETUP)
            link(v.tensor_scalar(NTE[:, :], BASE[:, :], 127.0, None, ALU.add))
            link(v.tensor_copy(CI[:, :], NTE[:, :]))
            v.tensor_copy(CNTI[:, :], BASE[:, :])
            link(v.tensor_scalar(CI2[:, :], CI[:, :], 7, None, ALU.arith_shift_right))
            link(v.tensor_copy(NTE[:, :], CI2[:, :]))
            link(v.tensor_tensor_scan(FI[:, :], ones[0:1, 0:8], NTE[0:1, :], 0.0, ALU.mult, ALU.add))
            link(v.tensor_tensor(FE[:, :], FI[:, :], NTE[0:1, :], ALU.subtract))
            link(v.tensor_scalar(AE[:, :], FE[:, :], -128.0, -float(DUMMY), ALU.mult, ALU.add))
            link(v.tensor_tensor(AE[:, :], AE[:, :], cst[0:1, C_EOFF:C_EOFF + 8], ALU.add))
            shape = [1, NTP, EXPERTS]
            kio = cst[0:1, C_KI:C_KI + NTP].unsqueeze(2).broadcast_to(shape)

            def each(ap):
                return ap.unsqueeze(1).broadcast_to(shape)

            v.tensor_tensor(IN1[:, :, :], kio, each(FE[:, :]), ALU.is_ge)
            link(v.tensor_tensor(IN2[:, :, :], kio, each(FI[:, :]), ALU.is_ge))
            link(v.tensor_tensor(IN1[:, :, :], IN1[:, :, :], IN2[:, :, :], ALU.subtract))
            link(v.scalar_tensor_tensor(IN2[:, :, :], kio, 128.0, each(AE[:, :]), ALU.mult, ALU.add))
            link(v.tensor_tensor(IN2[:, :, :], IN2[:, :, :], IN1[:, :, :], ALU.mult))
            link(v.tensor_tensor(IN3[:, :, :], IN1[:, :, :], each(cst[0:1, C_EI:C_EI + 8]), ALU.mult))
            link(v.tensor_reduce(TBF[:, 0, :], IN2[:, :, :], AX_X, ALU.add))
            link(v.tensor_reduce(TBF[:, 1, :], IN3[:, :, :], AX_X, ALU.add))
            link(v.tensor_scalar(TBF[:, 0, :], TBF[:, 0, :], float(DUMMY), None, ALU.add))
            v.tensor_copy(TBI[:, :, :], TBF[:, :, :]).then_inc(d_tab, 1)
            dve.wait_ge(d_tab, 1)

            link(v.memset(TIDX[:, :], 0.0))
            for j in range(3):
                link(v.tensor_tensor(TIDX[:, :].rearrange("p (b j) -> p b j", j=3)[:, :, j],
                                     cst[:, C_KI:C_KI + NB],
                                     TIDX[:, :].rearrange("p (b j) -> p b j", j=3)[:, :, j], ALU.add))
            link(v.tensor_scalar(TIDX[:, :], TIDX[:, :], float(T), None, ALU.mult))
            link(v.tensor_tensor(TIDX[:, :].rearrange("p (b j) -> p b j", j=3),
                                 TIDX[:, :].rearrange("p (b j) -> p b j", j=3),
                                 cst[:, C_TOK:C_TOK + 3].unsqueeze(1).broadcast_to([128, NB, 3]), ALU.add))

            tshape = [128, TILES, EXPERTS]

            def over(ap):
                return ap.unsqueeze(1).broadcast_to(tshape)

            SRCH = 6
            link(v.memset(TAU[:, :], 0.0625))
            link(v.memset(STEP[:, :], 0.5))

            def count_step(n, key, keep_op, bound, bound_op, value):
                s = Chain(c_srch, n * SRCH)
                s(v.tensor_tensor(MID[:, :], value[:, :], STEP[:, :], ALU.add))
                s(v.tensor_tensor(GE[:, :, :], key, over(MID[:, :]), keep_op))
                last = v.tensor_reduce(CN[:, :], GE[:, :, :].rearrange("p g e -> p e g"), AX_X, ALU.add)
                s(last)
                v.tensor_copy(CNb[:, :], CN[:, :]).then_inc(d_cn, 1)
                dve.wait_ge(p_cnt, n + 1)
                s(v.scalar_tensor_tensor(INC[:, :], G[:, 0, 0:8], bound, STEP[:, :], bound_op, ALU.mult))
                s(v.tensor_tensor(value[:, :], value[:, :], INC[:, :], ALU.add))
                s(v.tensor_scalar(STEP[:, :], STEP[:, :], 0.5, None, ALU.mult))
                assert s.n == SRCH

            with dve.Fori(0, TAU_STEPS) as n:
                count_step(n, PME[:, :, :], ALU.is_ge, float(CAP), ALU.is_ge, TAU)

            link(v.tensor_tensor(KEY[:, :, :], PME[:, :, :], over(TAU[:, :]), ALU.is_equal))
            link(v.tensor_scalar(GE[:, :, 0], TIDX[:, :], -float(SKIP), None, ALU.add))
            link(v.tensor_tensor(KEY[:, :, :], KEY[:, :, :], GE[:, :, 0].unsqueeze(2).broadcast_to(tshape), ALU.mult))
            link(v.tensor_tensor(GE[:, :, :], PME[:, :, :], over(TAU[:, :]), ALU.is_gt))
            link(v.scalar_tensor_tensor(KEY[:, :, :], GE[:, :, :], -float(SKIP) - 1.0, KEY[:, :, :],
                                        ALU.mult, ALU.add))
            link(v.tensor_scalar(KEY[:, :, :], KEY[:, :, :], float(SKIP), None, ALU.add))
            link(v.memset(IDX[:, :], 0.0))
            link(v.memset(STEP[:, :], float(1 << (IDX_STEPS - 1))))
            with dve.Fori(TAU_STEPS, TAU_STEPS + IDX_STEPS) as n:
                count_step(n, KEY[:, :, :], ALU.is_lt, float(CAP), ALU.is_le, IDX)

            MOE = 5

            def normal(k, u, r):
                dve.wait_ge(s_row[u], 16 * (r + 1))
                if not (isinstance(k, int) and k < 4):
                    dve.wait_ge(p_mx, k - 3)
                v.tensor_scalar(XM[:, u, :], RT[:, u, 0:D], RT[:, u, D:D + 1], RT[:, u, D + 1:D + 2],
                                ALU.subtract, ALU.mult).then_inc(d_xm, 1)

            def decide(k, u):
                s = Chain(c_moe, k * MOE)
                e = dve.value_load(TBI[0:1, 1, bass.ds(k, 1)], min_val=0, max_val=EXPERTS - 1)
                pm, tok = RT[:, u, D + 2:D + 3], RT[:, u, D + 3:D + 4]
                tau, idx = TAU[:, bass.ds(e, 1)], IDX[:, bass.ds(e, 1)]
                v.tensor_tensor(ceq[:, :], pm, tau, ALU.is_equal)
                v.tensor_tensor(clt[:, :], tok, idx, ALU.is_lt)
                s(v.tensor_tensor(ckp[:, :], pm, tau, ALU.is_gt))
                s(v.tensor_tensor(ceq[:, :], ceq[:, :], clt[:, :], ALU.mult))
                s(v.scalar_tensor_tensor(c1[:, :], ckp[:, :], ceq[:, 0:1], pm, ALU.add, ALU.mult))
                s(v.tensor_tensor(c2[:, :], pm, c1[:, :], ALU.subtract))
                s(v.scalar_tensor_tensor(Y2[:, :], XM[:, u, :], c2[:, 0:1], RT[:, u, 0:D], ALU.mult, ALU.add))
                assert s.n == MOE
                return e, tok

            def combine(k, u, it, e, tok):
                dve.wait_ge(p_l2, k + 1)
                v.tensor_tensor(Y1[:, :], Y[:, 0:D], B2[:, bass.ds(e, 1), :].rearrange("p o d -> p (o d)"),
                                ALU.add).then_inc(d_y, 1)
                dve.wait_ge(d_y, k + 2)
                if not isinstance(it, int):
                    dve.wait_ge(s_out[u], 16 * it)
                v.tensor_copy(OI[:, u:u + 1], tok)
                v.scalar_tensor_tensor(OT[:, u, :], Y1[:, :], c1[:, 0:1], Y2[:, :], ALU.mult, ALU.add).then_inc(
                    d_out, 1)

            link(v.tensor_copy(cut(XMTH[HC:HC + 1, :, :, :].rearrange("p v c n -> p (v c) n")),
                               ones[HC:HC + 1, :].unsqueeze(1).broadcast_to([1, 4, 128])))
            link(v.memset(ceq[:, :], 0.0))
            v.memset(c2[:, :], 0.0).then_inc(d_y, 1)
            for k in range(3):
                normal(k, k, 0)

            def low_parts(k, w):
                dve.wait_ge(a_mx, k + 1)
                if not (isinstance(k, int) and k < 2):
                    dve.wait_ge(p_l1, k - 1)
                v.tensor_tensor(cut(XMTL[:, w, :, :]), G[0:HC, 2, 0:256].rearrange("p (c n) -> p c n", c=2),
                                 XMTH[0:HC, w, :, :], ALU.subtract).then_inc(d_xl, 1)

            low_parts(0, 0)
            low_parts(1, 1)

            def four(it):
                for u in range(4):
                    k = it * 4 + u
                    if not (isinstance(k, int) and k == 0):
                        dve.wait_ge(p_l2, k)
                    for b in range(2):
                        dve.wait_ge(a_ht, 2 * k + b + 1)
                        v.tensor_tensor(cut(HTL[:, 3 * b:3 * b + 3, :]),
                                        G[:, b, 0:384].rearrange("p (f n) -> p f n", f=3),
                                        HTH[:, 3 * b:3 * b + 3, :], ALU.subtract).then_inc(d_ht, 1)
                    e, tok = decide(k, u)
                    low_parts(k + 2, u % 2)
                    normal(k + 3, (u + 3) % 4, it if u == 0 else it + 1)
                    combine(k, u, it, e, tok)

            four(0)
            with dve.Fori(1, NT // 4) as it:
                four(it)


_INS = ["x", "txt", "wtok", "gam", "bet", "btok", "wattn", "battn", "wproj", "bproj", "wsw", "bsw",
        "w1", "b1", "w2", "b2", "const"]


def _layout(np):
    pix = [(c, y, x) for c in range(3) for y in range(18) for x in range(18)
           if not (y in (0, 17) and x in (0, 17))]
    moves = [(1, 1), (1, 0), (1, 2), (0, 1), (2, 1)]
    often = [sum(0 <= y - dy < 16 and 0 <= x - dx < 16 for dy, dx in moves) for _, y, x in pix]
    groups = [[q for q, m in zip(pix, often) if m == times] for times in (5, 4, 3, 1)]
    times = [m for g, m in zip(groups, (5, 4, 3, 1)) for _ in range(-(-len(g) // PCH))]
    pix = [q for g in groups for q in g + [(3, 0, 0)] * (-len(g) % PCH)]
    rows = np.full((5, len(pix)), PATCH_DIM, np.int64)
    for s, (dy, dx) in enumerate(moves):
        for n, (c, y, x) in enumerate(pix):
            py, px = y - dy, x - dx
            if 0 <= py < 16 and 0 <= px < 16:
                rows[s, n] = (py * 16 + px) * 15 + 3 * s + c
    return pix, rows, times


def _constants(np, nb, times):
    n_tiles = tiles_of(nb * T) + 4
    m = np.zeros((128, MASKS), np.float32)
    c = np.zeros((128, C_KI + n_tiles), np.float32)
    p = np.arange(128)[:, None]
    c[:, C_ID:C_ID + 128] = np.eye(128)
    m[:, M_UT:M_UT + 128] = p < np.arange(128)[None, :]
    key = np.arange(KW)[None, :]
    for v in range(3):
        q = p % QB
        keep = (key >= q) & (key <= q + PAD) & (key >= PAD - QB * v)
        m[:, M_MQ + KW * v:M_MQ + KW * (v + 1)] = np.where(keep, 0, NEG)
        k, q = p, np.arange(QB)[None, :]
        keep = (k >= q) & (k <= q + PAD) & (k >= PAD - QB * v)
        m[:, M_MT + QB * v:M_MT + QB * (v + 1)] = np.where(keep, 0, NEG)
    for j in range(3):
        c[:, C_VALID + j] = p[:, 0] < ROWS[j]
        c[:, C_TOK + j] = p[:, 0] + OFF[j]
    e = np.arange(EXPERTS)
    c[:, C_EOFF:C_EOFF + EXPERTS] = e * (nb * T + 128)
    c[:, C_W8:C_W8 + EXPERTS] = EXPERTS - e
    c[:, C_EI:C_EI + EXPERTS] = e
    c[0:PIX, C_CNT] = times
    c[:, C_KI:] = np.arange(n_tiles)
    return np.concatenate([m, c], 1)


def kernel(**inputs):
    import numpy as np
    import concourse.bacc as bacc
    from concourse.bass_utils import run_bass_kernel_spmd

    a = {k: np.ascontiguousarray(v) for k, v in inputs.items()}
    nb = a["x"].shape[0]
    pix, rows, times = _layout(np)
    padded = np.pad(a["x"], ((0, 0), (0, 1), (1, 1), (1, 1)))
    side = 14
    cc = np.array([c for c, _, _ in pix])[:, None, None]
    yy = np.array([y for _, y, _ in pix])[:, None, None] + 16 * np.arange(side)[None, :, None]
    xx = np.array([x for _, _, x in pix])[:, None, None] + 16 * np.arange(side)[None, None, :]
    patches = padded[:, cc, yy, xx].reshape(nb, PIX, PCH, NPATCH)

    def shifted(w):
        w = np.concatenate([w, np.zeros((1,) + w.shape[1:], w.dtype)])
        return np.ascontiguousarray(np.moveaxis(w[rows].reshape((5, PIX, PCH) + w.shape[1:]), 0, 1))

    arrays = {
        "x": patches, "txt": a["txt"],
        "wtok": shifted(a["L0_tok_W"]), "gam": shifted(a["L0_tok_ln_gamma"]), "bet": shifted(a["L0_tok_ln_beta"]),
        "btok": a["L0_tok_b"], "wattn": a["L0_attn_W_attn"], "battn": a["L0_attn_b_attn"],
        "wproj": a["L0_attn_W_proj"], "bproj": a["L0_attn_b_proj"], "wsw": a["L0_ffn_switch_w"],
        "bsw": a["L0_ffn_switch_b"], "w1": a["L0_ffn_w1"], "b1": a["L0_ffn_b1"], "w2": a["L0_ffn_w2"],
        "b2": a["L0_ffn_b2"], "const": _constants(np, nb, times),
    }
    nc = bacc.Bacc("TRN2", target_bir_lowering=False, num_devices=1)
    args = [nc.dram_tensor("in_" + n, arrays[n].shape, mybir.dt.from_np(arrays[n].dtype), kind="ExternalInput").ap()
            for n in _INS]
    out = nc.dram_tensor("out_0_dram", (nb * T, D), F32, kind="ExternalOutput").ap()
    build(nc, *args, out)
    r = run_bass_kernel_spmd(nc, [{"in_" + n: arrays[n] for n in _INS}], core_ids=[0])
    return r.results[0]["out_0_dram"].reshape(nb, T, D)
```

```python
from contextlib import ExitStack

import concourse.bass as bass
from concourse import mybir

F32 = mybir.dt.float32
F32R = mybir.dt.float32r
BF16 = mybir.dt.bfloat16
I32 = mybir.dt.int32
ALU = mybir.AluOpType
ACT = mybir.ActivationFunctionType
AX_X = mybir.AxisListType.X

D = 192
HC = D // 2
HEADS, HD = 12, 16
HG = HEADS // 2
EXPERTS, FF = 8, 768
FCH = FF // 128
PIX, PCH = 121, 8
NPATCH, NTXT = 196, 128
T = NPATCH + NTXT
ROWS = [NPATCH // 2, NPATCH // 2, NTXT]
OFF = [0, ROWS[0], 2 * ROWS[0]]
HT = ROWS[0]
WIN = 64
QB = 54
NBLK = T // QB
KW = QB + WIN - 1
PAD = WIN - 1
VTOK = 2 * QB
VD = HEADS * (HD + 1)
ORDER = [0, 3, 1, 4, 2, 5]
UNITS = HG * NBLK // 4
PATCH_DIM = 16 * 16 * 15
EPS = 1e-5
NEG = -1e30
RW = D + 4
SKIP = 1000000
TAU_STEPS, IDX_STEPS = 27, 14
LANES = 128 // EXPERTS
SPAN = EXPERTS

C_ID = 0
C_BLK = C_ID + 128
C_VALID = C_BLK + 128
C_TOK = C_VALID + 3
C_EOFF = C_TOK + 3
C_W8 = C_EOFF + EXPERTS
C_EI = C_W8 + EXPERTS
C_CNT = C_EI + EXPERTS
C_KI = C_CNT + 1
M_UT = 0
M_MQ = M_UT + 128
M_MT = M_MQ + 3 * KW
MASKS = M_MT + 3 * QB


def cut(ap):
    return ap.bitcast(F32R)


def tiles_of(tokens):
    full = (tokens + EXPERTS * 127) // 128
    return -(-full // 4) * 4


def build(nc, x, txt, wtok, gam, bet, btok, wattn, battn, wproj, bproj, wsw, bsw, w1, b1, w2, b2, const, numbers, out):
    NB = x.shape[0]
    N = NB * T
    CAP = int(1.25 * N / EXPERTS)
    CAPR = N + 128
    DUMMY = EXPERTS * CAPR
    NT = tiles_of(N)
    NTP = NT + 4
    TILES = 3 * NB
    CW = C_KI + NTP

    with ExitStack() as ctx:
        def sb(name, shape, dt=F32):
            return ctx.enter_context(nc.sbuf_tensor(name, shape, dt))

        def sem(name):
            return ctx.enter_context(nc.semaphore(name))

        cst = sb("cst", [128, CW])
        ident = cst[:, C_ID:C_ID + 128]
        ones = sb("ones", [128, 128])
        onesb = sb("onesb", [128, 128], BF16)
        neghalf = sb("neghalf", [128, 3])
        epsc = sb("epsc", [128, 3])
        pause = sb("pause", [128, 1])
        gpause = sb("gpause", [128, 1])
        B2 = sb("B2", [128, EXPERTS, D])
        scratch = sb("scratch", [128, 4 * RW + 2 * D])
        btrow = sb("btrow", [1, D])
        SW = sb("SW", [HC + 1, 2, EXPERTS])

        negmu = sb("negmu", [HT, 2, 1])
        msq = sb("msq", [HT, 2, 1])
        tvar = sb("tvar", [HT, 2, 1])
        tve = sb("tve", [HT, 2, 1])
        trstd = sb("trstd", [HT, 2, 1])
        BN = sb("BN", [128, 3, 6])
        MV = sb("MV", [128, 3, 2])
        ve1 = sb("ve1", [128, 3])
        rstd1 = sb("rstd1", [128, 3])

        rec = sb("rec", [128, HEADS])
        BN2 = sb("BN2", [128, 3, 6])
        ve2 = sb("ve2", [128, 3])
        LM = sb("LM", [128, 3])
        LS = sb("LS", [128, 3, EXPERTS])
        EL = sb("EL", [128, 3, EXPERTS])
        ES = sb("ES", [128, 3])
        EQ = sb("EQ", [128, 3, EXPERTS])
        SC = sb("SC", [128, 3, EXPERTS])
        MX = sb("MX", [128, 3])
        OH = sb("OH", [128, 3, EXPERTS])
        OHb = sb("OHb", [128, 3, EXPERTS], BF16)
        POS = sb("POS", [128, 3, EXPERTS])
        SLF = sb("SLF", [128, 3])
        SLI = sb("SLI", [128, 3], I32)
        BASE = sb("BASE", [128, EXPERTS])
        TK = sb("TK", [128, 3])

        MID = sb("MID", [128, 1])
        STEP = sb("STEP", [128, 1])
        CN = sb("CN", [128, 1])
        INC = sb("INC", [128, 1])
        TAUL = sb("TAUL", [128, 1])
        IDXL = sb("IDXL", [128, 1])
        LIM = sb("LIM", [128, EXPERTS, 2])
        CI = sb("CI", [128, EXPERTS], I32)
        CI2 = sb("CI2", [128, EXPERTS], I32)
        CNTI = sb("CNTI", [128, EXPERTS], I32)
        NTE = sb("NTE", [128, EXPERTS])
        FI = sb("FI", [1, EXPERTS])
        FE = sb("FE", [1, EXPERTS])
        AE = sb("AE", [1, EXPERTS])
        IN3 = scratch[0:1, 0:NTP * EXPERTS].rearrange("p (n e) -> p n e", e=EXPERTS)
        TBF = sb("TBF", [1, 2, NTP])
        TBI = sb("TBI", [1, 2, NTP], I32)

        RT = scratch[:, 0:4 * RW].rearrange("p (u d) -> p u d", u=4)
        Y1 = scratch[:, 4 * RW:4 * RW + D]
        Y2 = scratch[:, 4 * RW + D:4 * RW + 2 * D]
        lim = sb("lim", [128, 4, 2])
        bias2 = sb("bias2", [128, 4, D])
        at = sb("at", [128, 4, 1])
        among = sb("among", [128, 4, 1])
        above = sb("above", [128, 4, 1])
        c1 = sb("c1", [128, 4])
        c2 = sb("c2", [128, 4])
        OI = sb("OI", [128, 4], I32)

        first_part = ExitStack()

        def early(name, shape, dt=F32):
            return first_part.enter_context(nc.sbuf_tensor(name, shape, dt))

        front_turn = ExitStack()

        def front(name, shape):
            return front_turn.enter_context(nc.sbuf_tensor(name, shape, F32))

        imgH = front("imgH", [PIX, PCH, NPATCH])
        imgL = front("imgL", [PIX, PCH, NPATCH])
        WEH = front("WEH", [PIX, PCH, D + 2])
        WEL = front("WEL", [PIX, PCH, D + 2])
        XTH = front("XTH", [HC + 1, 2, T])
        XTL = front("XTL", [HC, 2, T])
        WAH = front("WAH", [HC + 1, 2, 2 * D])
        WAL = front("WAL", [HC + 1, 2, 2 * D])
        WVH = front("WVH", [HC + 1, 2, VD])
        WVL = front("WVL", [HC + 1, 2, VD])
        front_turn.close()
        W1 = early("W1", [HC + 1, 2, EXPERTS, FF])

        batch_turn = ExitStack()

        def batch(name, shape, dt=F32):
            return batch_turn.enter_context(nc.sbuf_tensor(name, shape, dt))

        WS = batch("WS", [PIX, 5, PCH, D])
        masks = batch("masks", [128, MASKS])
        identb = batch("identb", [128, 128], BF16)
        utrib = batch("utrib", [128, 128], BF16)
        mqb = batch("mqb", [2 * QB, NBLK + 2, KW], BF16)
        mtb = batch("mtb", [128, 3, QB], BF16)
        GM = batch("GM", [PIX, 5, PCH])
        BT = batch("BT", [PIX, 5, PCH])
        WE = batch("WE", [PIX, PCH, D + 2])
        csum = batch("csum", [HT, D])
        tbias = batch("tbias", [HT, D])
        WA = batch("WA", [HC + 1, 2, 2 * D])
        WV = batch("WV", [HC + 1, 2, VD])
        WVV = WV[:, :, :].rearrange("k c (h d) -> k c h d", h=HEADS)
        WP = batch("WP", [HC + 1, 2, D])
        img = batch("img", [PIX, PCH, NPATCH])
        sq = batch("sq", [PIX, PCH, NPATCH])
        WTMP = sq[:, :, 0:D]
        WTM2 = batch("WTM2", [PIX, PCH, D])
        ssq = batch("ssq", [PIX, NPATCH])
        H = batch("H", [128, 3, D])
        R = batch("R", [128, 3, D])
        TMP = batch("TMP", [HT, 2, D])
        XN = batch("XN", [128, 3, D])
        QS = batch("QS", [HC, 2, T])
        QSb = batch("QSb", [HC, 2, T], BF16)
        KT = batch("KT", [HC + 1, 2, PAD + T])
        KTb = batch("KTb", [HC, 2, PAD + T], BF16)
        QDb = batch("QDb", [HC, HG, NBLK, 2, QB], BF16)
        VT = batch("VT", [VTOK, 3, VD])
        V = batch("V", [KW, NBLK, VD])
        M = batch("M", [2 * QB, 80])
        mT = batch("mT", [4 * UNITS, 2 * QB])
        PR = batch("PR", [KW, 2, 2, HG * QB])
        ysb = batch("ysb", [128, D])
        YT = batch("YT", [HC + 1, 2, T])
        ROW = batch("ROW", [128, 3, RW])
        XN2 = batch("XN2", [128, 3, D])
        PME = batch("PME", [128, EXPERTS, TILES])
        batch_turn.close()
        load_turn = ExitStack()
        W2 = load_turn.enter_context(nc.sbuf_tensor("W2", [128, EXPERTS, FCH, 2, D], F32))
        load_turn.close()
        early("W2_W1H_place", [128, 2 * EXPERTS * FCH * D + 2 * EXPERTS * FF])
        XT2 = early("XT2", [HC + 1, 2, T])
        arena = early("arena", [128, HEADS * T])
        WTM3 = arena[0:PIX, 0:PCH * D].rearrange("p (k d) -> p k d", k=PCH)
        QD = arena[0:HC + 1, :].rearrange("p (h t) -> p h t", h=HEADS)
        KEYS = max(TILES, NTP) * EXPERTS
        GE, KEY, PX, TX = (arena[:, n * KEYS:n * KEYS + TILES * SPAN] for n in range(4))
        IN1 = arena[0:1, 0:NTP * EXPERTS].rearrange("p (n e) -> p n e", e=EXPERTS)
        IN2 = arena[0:1, KEYS:KEYS + NTP * EXPERTS].rearrange("p (n e) -> p n e", e=EXPERTS)
        ZR = early("ZR", [128, RW])
        first_part.close()

        W1L = sb("W1L", [HC + 1, 2, EXPERTS, FF])
        W2HL = sb("W2HL", [128, EXPERTS, FCH, 2, D])
        W1H = sb("W1H", [HC + 1, 2, EXPERTS, FF])
        XMTH = sb("XMTH", [HC + 1, 2, 2, 128])
        XMTL = sb("XMTL", [HC, 2, 2, 128])
        XM = sb("XM", [128, 4, D])
        OT = sb("OT", [128, 4, D])
        HS = sb("HS", [128, FF])
        HTH = sb("HTH", [128, FCH, 128])
        HTL = sb("HTL", [128, FCH, 128])

        ST = ctx.enter_context(nc.psum_tensor("ST", [128, 4, 512], F32))
        Y = ctx.enter_context(nc.psum_tensor("Y", [128, 512], F32))
        G = ctx.enter_context(nc.psum_tensor("G", [128, 3, 512], F32))

        PD = nc.dram_tensor("probabilities", [EXPERTS, 128, TILES], F32, kind="Internal").ap()
        XS = nc.dram_tensor("dispatched", [DUMMY + 128, RW], F32, kind="Internal").ap()

        s_set = sem("s_set")
        s_cst = sem("s_cst")
        s_ws = [sem(f"s_ws{s}") for s in range(5)]
        s_exp = sem("s_exp")
        s_w2 = sem("s_w2")
        s_img = sem("s_img")
        s_txt = sem("s_txt")
        s_qd = sem("s_qd")
        s_qdb = sem("s_qdb")
        s_v = sem("s_v")
        s_mrow = sem("s_mrow")
        s_pd = sem("s_pd")
        s_px = sem("s_px")
        s_scat = sem("s_scat")
        p_set = sem("p_set")
        p_tok = sem("p_tok")
        p_xt = sem("p_xt")
        p_qkv = sem("p_qkv")
        p_st = sem("p_st")
        p_pv = sem("p_pv")
        p_yt = sem("p_yt")
        p_proj = sem("p_proj")
        p_smax = sem("p_smax")
        p_lt = sem("p_lt")
        p_log = sem("p_log")
        p_mt = sem("p_mt")
        p_pref = sem("p_pref")
        p_cnt = sem("p_cnt")
        p_mx = sem("p_mx")
        p_l1 = sem("p_l1")
        p_ht = sem("p_ht")
        p_l2 = sem("p_l2")
        a_sq = sem("a_sq")
        a_wh = sem("a_wh")
        a_ih = sem("a_ih")
        a_xt = sem("a_xt")
        a_qk = sem("a_qk")
        a_v = sem("a_v")
        a_exp = sem("a_exp")
        a_yt = sem("a_yt")
        a_r = sem("a_r")
        a_lt = sem("a_lt")
        a_el = sem("a_el")
        a_mx = sem("a_mx")
        a_gelu = sem("a_gelu")
        a_split = sem("a_split")
        a_ht = sem("a_ht")
        d_set = sem("d_set")
        d_we = sem("d_we")
        d_wl = sem("d_wl")
        d_xt = sem("d_xt")
        d_sq = sem("d_sq")
        d_tvar = sem("d_tvar")
        d_tok = sem("d_tok")
        d_mv = sem("d_mv")
        d_xn = sem("d_xn")
        d_norm = sem("d_norm")
        d_h2 = sem("d_h2")
        d_mv2 = sem("d_mv2")
        d_xn2 = sem("d_xn2")
        d_max = sem("d_max")
        d_ls = sem("d_ls")
        d_log = sem("d_log")
        d_oh = sem("d_oh")
        d_mt = sem("d_mt")
        d_pref = sem("d_pref")
        d_row = sem("d_row")
        d_cn = sem("d_cn")
        d_tab = sem("d_tab")
        d_xm = sem("d_xm")
        d_cmp = sem("d_cmp")
        d_lim = sem("d_lim")
        d_xl = sem("d_xl")
        d_ht = sem("d_ht")
        d_out = sem("d_out")
        d_y = sem("d_y")
        c_set = sem("c_set")
        c_front = sem("c_front")
        c_back = sem("c_back")
        c_route = sem("c_route")
        c_srch = sem("c_srch")
        c_moe = sem("c_moe")
        g_set = sem("g_set")
        g_we = sem("g_we")
        g_te = sem("g_te")
        g_il = sem("g_il")
        g_trstd = sem("g_trstd")
        g_e1 = sem("g_e1")
        g_r1 = sem("g_r1")
        g_e2 = sem("g_e2")
        g_r2 = sem("g_r2")
        g_hold = sem("g_hold")
        g_keep = sem("g_keep")
        g_fetch = sem("g_fetch")
        g_split = sem("g_split")
        s_pad = sem("s_pad")
        s_row = [sem(f"s_row{u}") for u in range(4)]
        s_out = [sem(f"s_out{u}") for u in range(4)]

        parts = [(W1H[0:HC + c, c, e:e + 2, :], W1L[0:HC + c, c, e:e + 2, :], W1[0:HC + c, c, e:e + 2, :])
                 for c in range(2) for e in range(0, EXPERTS, 2)]
        parts += [(W2HL[:, e, :, 0, :], W2HL[:, e, :, 1, :], W2[:, e, :, 1, :]) for e in range(EXPERTS)]

        block = ctx.enter_context(nc.Block())

        SET_LOADS = 10
        SHIFTS = [3, 4, 0, 1, 2]
        EXP_LOADS = 5
        KEEP = 4

        @block.sync
        def _(sp):
            def load_txt(i):
                sp.dma_start(H[:, 2, :], txt[bass.ds(i, 1), :, :].rearrange("o t d -> t (o d)")).then_inc(s_txt, 16)

            def load_img(i):
                sp.dma_start(img[:, :, :], x[bass.ds(i, 1), :, :, :].rearrange("o p k n -> p (o k) n")).then_inc(
                    s_img, 16)

            sp.dma_start(GM[:, :, :], gam).then_inc(s_cst, 16)
            sp.dma_start(BT[:, :, :], bet).then_inc(s_cst, 16)
            sp.dma_start(btrow[:, :], btok.rearrange("(o d) -> o d", o=1)).then_inc(s_cst, 16)
            sp.dma_start(cst[:, :], const[:, MASKS:MASKS + CW]).then_inc(s_cst, 16)
            sp.dma_start(masks[:, :], const[:, 0:MASKS]).then_inc(s_cst, 16)
            for s in SHIFTS:
                sp.dma_start(WS[:, s, :, :], wtok[:, s, :, :]).then_inc(s_ws[s], 16)
            load_img(0)
            sp.dma_start(WA[0:HC, :, :], wattn[:, 0:2 * D].rearrange("(c k) n -> k c n", c=2)).then_inc(s_set, 16)
            sp.dma_start(WA[HC:HC + 1, 1, :], battn[0:2 * D].rearrange("(o d) -> o d", o=1)).then_inc(s_set, 16)
            for c in range(2):
                sp.dma_start(WVV[0:HC, c, :, 0:HD], wattn[c * HC:(c + 1) * HC, 2 * D:3 * D].rearrange(
                    "k (h d) -> k h d", d=HD)).then_inc(s_set, 16)
            sp.dma_start(WVV[HC:HC + 1, 1, :, 0:HD],
                         battn[2 * D:3 * D].rearrange("(o h d) -> o h d", o=1, d=HD)).then_inc(s_set, 16)
            sp.dma_start(WP[0:HC, :, :], wproj.rearrange("(c k) n -> k c n", c=2)).then_inc(s_set, 16)
            sp.dma_start(WP[HC:HC + 1, 1, :], bproj.rearrange("(o d) -> o d", o=1)).then_inc(s_set, 16)
            sp.dma_start(SW[0:HC, :, :], wsw.rearrange("(c k) n -> k c n", c=2)).then_inc(s_set, 16)
            sp.dma_start(SW[HC:HC + 1, 1, :], bsw.rearrange("(o d) -> o d", o=1)).then_inc(s_set, 16)
            sp.dma_start(B2[:, :, :], b2.partition_broadcast(128)).then_inc(s_set, 16)
            sp.wait_ge(d_set, 1)
            load_txt(0)
            def front(i, more):
                if more:
                    sp.wait_ge(a_sq, i + 1)
                    sp.wait_ge(a_ih, i + 1)
                    sp.wait_ge(g_il, i + 1)
                    load_img(i + 1)
                sp.wait_ge(a_qk, 4 * i + 2)
                for a in range(HG):
                    sp.dma_start(QDb[HD * a:HD * a + HD, 2 * (a % 3):2 * (a % 3) + 2, :, a // 3, :],
                                 QSb[HD * a:HD * a + HD, :, :].rearrange("p g (t q) -> p g t q", q=QB)).then_inc(
                                     s_qdb, 16)
                if not (isinstance(i, int) and i == 0):
                    sp.wait_ge(p_st, 6 * i)
                for a in range(HG):
                    sp.dma_start(QD[HD * a:HD * a + HD, 2 * a:2 * a + 2, :],
                                 QS[HD * a:HD * a + HD, :, :]).then_inc(s_qd, 16)
                if not (isinstance(i, int) and i == 0):
                    sp.wait_ge(p_pv, 6 * i)
                sp.wait_ge(a_v, 2 * i + 2)
                for par, rows, before in ((0, QB, PAD), (1, VTOK, KW - VTOK)):
                    win = V[:, :, :].rearrange("p (s w) d -> p w s d", w=2)
                    sp.dma_start(win[before:KW, par, :, :], VT[0:rows, :, :]).then_inc(s_v, 16)
                    sp.dma_start(win[0:before, par, 1:3, :], VT[VTOK - before:VTOK, 0:2, :]).then_inc(s_v, 16)
                sp.wait_ge(d_mt, i + 1)
                for par in range(2):
                    sp.dma_start(QD[HC:HC + 1, HG * par:HG * par + HG, :],
                                 mT[:, QB * par:QB * par + QB]).then_inc(s_mrow, 16)
                if more:
                    sp.wait_ge(a_r, i + 1)
                    load_txt(i + 1)

            front(0, NB > 1)
            if NB > 2:
                with sp.Fori(1, NB - 1) as i:
                    front(i, True)
            if NB > 1:
                front(NB - 1, False)

            sp.wait_ge(d_row, NB)
            sp.dma_start(PD.rearrange("e p g -> p e g"), PME[:, :, :]).then_inc(s_pd, 16)
            sp.dma_start(TX, numbers).then_inc(s_px, 16)
            sp.wait_ge(s_pd, 16)
            sp.dma_start(PX, PD.rearrange("e (a b) g -> (e a) (b g)", b=SPAN)).then_inc(s_px, 16)
            for e in range(0, EXPERTS, 4):
                for c in range(2):
                    sp.dma_start(W1[0:HC, c, e:e + 4, :],
                                 w1[e:e + 4, c * HC:(c + 1) * HC, :].rearrange("e k f -> k e f")).then_inc(s_exp, 16)
            sp.dma_start(W1[HC:HC + 1, 1, :, :], b1.rearrange("(o e) f -> o e f", o=1)).then_inc(s_exp, 16)
            for e in range(EXPERTS):
                sp.dma_start(W2[:, e, :, 1, :], w2[e].rearrange("(f p) d -> p f d", p=128)).then_inc(s_w2, 16)

            sp.wait_ge(d_tab, 1)
            for e in range(EXPERTS):
                r = sp.value_load(CNTI[0:1, e:e + 1], min_val=0, max_val=N)
                sp.dma_start(XS[bass.ds(r + e * CAPR, 128), :], ZR[:, :]).then_inc(s_pad, 16)
            sp.dma_start(XS[DUMMY:DUMMY + 128, :], ZR[:, :]).then_inc(s_pad, 16)
            sp.wait_ge(s_pad, 16 * (EXPERTS + 1))
            sp.wait_ge(s_scat, 48 * NB)

            def load_rows(k, u, free):
                r = sp.value_load(TBI[0:1, 0, bass.ds(k, 1)], min_val=0, max_val=DUMMY)
                if free is not None:
                    sp.wait_ge(d_out, free)
                sp.dma_start(RT[:, u, :], XS[bass.ds(r, 128), :]).then_inc(s_row[u], 16)

            for k in range(4):
                load_rows(k, k, None)
            with sp.Fori(0, NT // 4) as it:
                for u in range(4):
                    k = it * 4 + u
                    load_rows(k + 4, u, k + 1)
            for u in range(4):
                sp.wait_ge(s_row[u], 16 * (NT // 4 + 1))

        @block.gpsimd
        def _(gp):
            nc.gpsimd.memset(neghalf[:, :], -0.5).then_inc(g_set, 1)
            nc.gpsimd.memset(epsc[:, :], EPS).then_inc(g_set, 1)
            nc.gpsimd.memset(QDb[:, :, :, :, :], 0.0).then_inc(g_set, 1)
            nc.gpsimd.memset(KT[:, :, :], 0.0).then_inc(g_set, 1)
            nc.gpsimd.memset(KTb[:, :, :], 0.0).then_inc(g_set, 1)
            nc.gpsimd.memset(V[:, :, :], 1.0).then_inc(g_set, 1)
            gp.wait_ge(s_cst, 16 * 5)
            for s, place in ((3, WTM2), (4, WTM3)):
                gp.wait_ge(s_ws[s], 16)
                nc.gpsimd.tensor_tensor(place[:, :, :], WS[:, s, :, :], GM[:, s, :].unsqueeze(2).broadcast_to(
                    [PIX, PCH, D]), ALU.mult).then_inc(g_we, 1)
            gp.wait_ge(g_we, 2)
            nc.gpsimd.tensor_tensor(WTM2[:, :, :], WTM2[:, :, :], WTM3[:, :, :], ALU.add).then_inc(g_we, 1)
            gp.wait_ge(g_we, 3)
            nc.gpsimd.memset(QD[:, :, :], 0.0).then_inc(g_set, 1)
            gp.wait_ge(g_set, 7)
            nc.gpsimd.memset(KT[HC:HC + 1, :, :], 1.0).then_inc(g_set, 1)
            nc.gpsimd.memset(YT[HC:HC + 1, :, :], 1.0).then_inc(g_set, 1)
            nc.gpsimd.memset(XT2[HC:HC + 1, :, :], 1.0).then_inc(g_set, 1)
            gp.wait_ge(g_set, 10)

            def hold():
                return nc.gpsimd.tensor_tensor(gpause[:, :], neghalf[:, 0:1], neghalf[:, 0:1], ALU.add)

            def front(i):
                gp.wait_ge(d_tvar, i + 1)
                nc.gpsimd.tensor_tensor(tve[:, :, 0], tvar[:, :, 0], epsc[0:HT, 0:2], ALU.add).then_inc(g_te, 1)
                gp.wait_ge(g_te, i + 1)
                nc.gpsimd.tensor_tensor(trstd[:, :, 0], tve[:, :, 0], neghalf[0:HT, 0:2], ALU.pow).then_inc(g_trstd, 1)
                gp.wait_ge(d_mv, i + 1)
                nc.gpsimd.tensor_tensor(ve1[:, :], MV[:, :, 1], epsc[:, :], ALU.add).then_inc(g_e1, 1)
                gp.wait_ge(g_e1, i + 1)
                nc.gpsimd.tensor_tensor(rstd1[:, :], ve1[:, :], neghalf[:, :], ALU.pow).then_inc(g_r1, 1)

            def second(a):
                gp.wait_ge(d_mv2, a + 1)
                nc.gpsimd.tensor_tensor(ve2[:, :], ROW[:, :, D + 1], epsc[:, :], ALU.add).then_inc(g_e2, 1)
                gp.wait_ge(g_e2, a + 1)
                nc.gpsimd.tensor_tensor(ROW[:, :, D + 1], ve2[:, :], neghalf[:, :], ALU.pow).then_inc(g_r2, 1)

            def scatter(a):
                gp.wait_ge(d_row, a + 1)
                hold()
                for j in range(3):
                    gp.indirect_dma_start(XS[:, :], bass.IndirectOffsetOnAxis(ap=SLI[0:ROWS[j], j:j + 1], axis=0),
                                          ROW[0:ROWS[j], j, :], None, bounds_check=DUMMY - 1,
                                          oob_is_err=False).then_inc(s_scat, 16)

            def image_low(i):
                gp.wait_ge(a_ih, i + 1)
                if not (isinstance(i, int) and i == 0):
                    gp.wait_ge(p_tok, i)
                nc.gpsimd.tensor_tensor(cut(imgL[:, :, :]), img[:, :, :], imgH[:, :, :], ALU.subtract).then_inc(g_il, 1)

            image_low(0)
            front(0)
            image_low(1)
            front(1)
            image_low(2)
            second(0)
            with gp.Fori(2, NB - 1) as i:
                front(i)
                scatter(i - 2)
                image_low(i + 1)
                second(i - 1)
            front(NB - 1)
            scatter(NB - 3)
            second(NB - 2)
            scatter(NB - 2)
            second(NB - 1)
            scatter(NB - 1)

            for n, (high, low, weights) in enumerate(parts):
                gp.wait_ge(a_split, n + 1)
                nc.gpsimd.tensor_tensor(cut(low), weights, high, ALU.subtract).then_inc(g_split, 1)

            def factors(k, u):
                pm, base = RT[:, u, D + 2:D + 3], k * KEEP
                gp.wait_ge(d_cmp, k + 1)
                nc.gpsimd.tensor_tensor(at[:, u, :], at[:, u, :], among[:, u, :], ALU.mult).then_inc(g_keep, 1)
                gp.wait_ge(g_keep, base + 1)
                nc.gpsimd.tensor_tensor(above[:, u, :], above[:, u, :], at[:, u, :], ALU.add).then_inc(g_keep, 1)
                gp.wait_ge(g_keep, base + 2)
                nc.gpsimd.tensor_tensor(c1[:, u:u + 1], above[:, u, :], pm, ALU.mult).then_inc(g_keep, 1)
                gp.wait_ge(g_keep, base + 3)
                nc.gpsimd.tensor_tensor(c2[:, u:u + 1], pm, c1[:, u:u + 1], ALU.subtract).then_inc(g_keep, 1)

            def fetch(k, u):
                e = gp.value_load(TBI[0:1, 1, bass.ds(k, 1)], min_val=0, max_val=EXPERTS - 1)
                nc.gpsimd.tensor_copy(lim[:, u:u + 1, :], LIM[:, bass.ds(e, 1), :])
                nc.gpsimd.tensor_copy(bias2[:, u:u + 1, :], B2[:, bass.ds(e, 1), :]).then_inc(g_fetch, 1)

            gp.wait_ge(d_lim, 1)
            fetch(0, 0)
            fetch(1, 1)
            factors(0, 0)
            gp.wait_ge(g_r2, NB)
            nc.gpsimd.tensor_tensor(ve2[:, :], epsc[:, :], epsc[:, :], ALU.add).then_inc(g_hold, 1)
            with gp.Fori(0, NT // 4) as it:
                for u in range(4):
                    k = it * 4 + u
                    fetch(k + 2, (u + 2) % 4)
                    factors(k + 1, (u + 1) % 4)
                    gp.wait_ge(g_hold, k + 1)
                    gp.wait_ge(d_out, k + 1)
                    hold().then_inc(g_hold, 1)
                    gp.indirect_dma_start(out, bass.IndirectOffsetOnAxis(ap=OI[:, u:u + 1], axis=0),
                                          OT[:, u, :], None, bounds_check=N - 1,
                                          oob_is_err=False).then_inc(s_out[u], 16)
            for u in range(4):
                gp.wait_ge(s_out[u], 16 * (NT // 4))

        @block.scalar
        def _(act):
            copy = nc.scalar.copy

            def square(i):
                act.wait_ge(s_img, 16 * (i + 1))
                if not (isinstance(i, int) and i == 0):
                    act.wait_ge(d_sq, i)
                nc.scalar.activation(sq[:, :, :], img[:, :, :], ACT.Square).then_inc(a_sq, 1)

            def image_high(i):
                if not (isinstance(i, int) and i == 0):
                    act.wait_ge(p_tok, i)
                copy(cut(imgH[:, :, :]), img[:, :, :]).then_inc(a_ih, 1)

            def exps(a, n):
                act.wait_ge(p_st, 6 * a + n + 1)
                if n >= 2 or not (isinstance(a, int) and a == 0):
                    act.wait_ge(p_pv, 6 * a + n - 1)
                nc.scalar.activation(PR[:, n % 2, :, :], ST[0:KW, 2 * (n % 2):2 * (n % 2) + 2, 0:HG * QB],
                                     ACT.Exp).then_inc(a_exp, 1)

            def y_turned(a, j, bank):
                act.wait_ge(p_yt, 3 * a + j + 1)
                if j == 0 and not (isinstance(a, int) and a == 0):
                    act.wait_ge(p_proj, 3 * a)
                for c in range(2):
                    last = copy(YT[0:HC, c, :].rearrange("p (s j q) -> p s j q", s=2, j=3)[:, :, j, :],
                                G[0:HC, bank, 128 * c:128 * c + 128].rearrange("p (s q) -> p s q", s=2)[:, :, 0:QB])
                last.then_inc(a_yt, 1)

            def x_turned(i):
                if not (isinstance(i, int) and i == 0):
                    act.wait_ge(p_qkv, 6 * i)
                for c in range(2):
                    act.wait_ge(p_xt, 2 * i + c + 1)
                    copy(cut(XTH[0:HC, c, :]), G[0:HC, 2 * c, 0:T]).then_inc(a_xt, 1)

            def queries_keys(i):
                first = isinstance(i, int) and i == 0
                if not first:
                    act.wait_ge(s_qd, 16 * HG * i)
                    act.wait_ge(s_qdb, 16 * HG * i)
                for g in range(2):
                    act.wait_ge(p_qkv, 6 * i + g + 1)
                    bank = 2 - g
                    act.mul(QS[:, g, :], G[0:HC, bank, 0:T], HD ** -0.5)
                    act.mul(QSb[:, g, :], G[0:HC, bank, 0:T], HD ** -0.5).then_inc(a_qk, 1)
                for g in range(2):
                    act.wait_ge(p_qkv, 6 * i + g + 3)
                    if g == 0 and not first:
                        act.wait_ge(p_st, 6 * i)
                        act.wait_ge(p_smax, UNITS * i)
                    copy(KT[0:HC, g, PAD:PAD + T], G[0:HC, 2 * g, 0:T])
                    copy(KTb[:, g, PAD:PAD + T], G[0:HC, 2 * g, 0:T]).then_inc(a_qk, 1)

            def values(i):
                if not (isinstance(i, int) and i == 0):
                    act.wait_ge(s_v, 64 * i)
                for n, m0, m1 in ((0, 0, 2), (1, 2, 3)):
                    act.wait_ge(p_qkv, 6 * i + n + 5)
                    copy(VT[:, m0:m1, :], G[0:VTOK, 2 - n, 0:(m1 - m0) * VD].rearrange("p (m d) -> p m d", d=VD)).then_inc(
                        a_v, 1)

            def residual(i, back):
                if back:
                    act.wait_ge(d_h2, 3 * i)
                act.wait_ge(d_xn, i + 1)
                copy(R[:, :, :], H[:, :, :]).then_inc(a_r, 1)

            def router_turned(a):
                if not (isinstance(a, int) and a == 0):
                    act.wait_ge(p_log, a)
                for c in range(2):
                    act.wait_ge(p_lt, 2 * a + c + 1)
                    copy(XT2[0:HC, c, :], G[0:HC, 2 - 2 * c, 0:T]).then_inc(a_lt, 1)

            def router_exp(a):
                act.wait_ge(d_ls, a + 1)
                nc.scalar.activation(EL[:, :, :], LS[:, :, :], ACT.Exp).then_inc(a_el, 1)

            def body(i, front, back, route, more):
                b, c = i - 1, i - 2
                if back:
                    exps(b, 0)
                    exps(b, 1)
                if route:
                    router_turned(c)
                if back:
                    exps(b, 2)
                if more and back:
                    square(i + 1)
                if back:
                    exps(b, 3)
                    y_turned(b, 0, 2)
                if more and back:
                    image_high(i + 1)
                if back:
                    exps(b, 4)
                if route:
                    router_exp(c)
                if front:
                    x_turned(i)
                if back:
                    exps(b, 5)
                if front:
                    queries_keys(i)
                if more and not back:
                    square(i + 1)
                    image_high(i + 1)
                if back:
                    y_turned(b, 1, 1)
                    y_turned(b, 2, 0)
                if front:
                    values(i)
                    residual(i, back)

            act.wait_ge(s_img, 16)
            image_high(0)
            act.wait_ge(d_set, 1)
            act.wait_ge(s_set, 16 * SET_LOADS)
            for high, weights in ((WAH, WA), (WVH, WV)):
                for c in range(2):
                    copy(cut(high[0:HC + c, c, :]), weights[0:HC + c, c, :]).then_inc(a_wh, 1)
            act.wait_ge(d_we, 1)
            copy(cut(WEH[:, :, :]), WE[:, :, :]).then_inc(a_wh, 1)
            act.wait_ge(g_set, 10)
            square(0)
            body(0, True, False, False, True)
            body(1, True, True, False, True)
            body(2, True, True, True, True)
            with act.Fori(3, NB - 1) as i:
                body(i, True, True, True, True)
            body(NB - 1, True, True, True, False)
            body(NB, False, True, True, False)
            body(NB + 1, False, False, True, False)

            act.wait_ge(s_exp, 16 * EXP_LOADS)
            act.wait_ge(s_set, 16 * SET_LOADS)
            act.wait_ge(d_row, NB)
            act.wait_ge(s_scat, 48 * NB)
            for n, (high, _, weights) in enumerate(parts):
                if n == len(parts) - EXPERTS:
                    act.wait_ge(s_w2, 16 * EXPERTS)
                copy(cut(high), weights).then_inc(a_split, 1)

            def turned(k, v):
                act.wait_ge(p_mx, k + 1)
                if not (isinstance(k, int) and k < 2):
                    act.wait_ge(p_l1, k - 1)
                copy(cut(XMTH[0:HC, v, :, :]), G[0:HC, 2, 0:256].rearrange("p (c n) -> p c n", c=2)).then_inc(a_mx, 1)

            def gelu(k, v):
                act.wait_ge(p_l1, k + 1)
                if not (isinstance(k, int) and k == 0):
                    act.wait_ge(p_ht, k)
                nc.scalar.activation(HS[:, :].rearrange("p (b n) -> p b n", b=2), ST[:, 2 * v:2 * v + 2, 0:FF // 2],
                                     ACT.Gelu).then_inc(a_gelu, 1)

            turned(0, 0)
            turned(1, 1)
            gelu(0, 0)

            def hidden_turned(k):
                act.wait_ge(p_ht, k + 1)
                if not (isinstance(k, int) and k == 0):
                    act.wait_ge(p_l2, k)
                for b in range(2):
                    copy(cut(HTH[:, 3 * b:3 * b + 3, :]), G[:, b, 0:384].rearrange("p (f n) -> p f n", f=3)).then_inc(
                        a_ht, 1)

            def two(it):
                for v in range(2):
                    k = it * 2 + v
                    hidden_turned(k)
                    gelu(k + 1, 1 - v)
                    turned(k + 2, v)

            two(0)
            with act.Fori(1, NT // 2) as it:
                two(it)

        @block.tensor
        def _(pe):
            mm = nc.tensor.matmul

            def halves(o, lhs, rhs):
                mm(o, lhs(0, HC), rhs(0, HC), start=True, stop=False)
                return mm(o, lhs(1, HC + 1), rhs(1, HC + 1), start=False, stop=True)

            def tokens(i, back):
                pe.wait_ge(g_il, i + 1)
                if isinstance(i, int) and i == 1:
                    pe.wait_ge(a_v, 2)
                elif not isinstance(i, int) or i > 1:
                    pe.wait_ge(d_h2, 3 * (i - 1) - 1)
                for j in range(2):
                    if j == 1 and not (isinstance(i, int) and i < 2):
                        pe.wait_ge(d_h2, 3 * (i - 1))
                    for k in range(PCH):
                        if j == 0 and k == PCH // 2 and back:
                            max_turn(i - 1)
                        for a, w in ((imgH, WEH), (imgH, WEL), (imgL, WEH)):
                            mm(G[0:HT, j, 0:D + 2], cut(a[:, k, HT * j:HT * j + HT]), cut(w[:, k, :]),
                               start=(k == 0 and a is imgH and w is WEH), stop=(k == PCH - 1 and a is imgL))
                pe.wait_ge(d_sq, i + 1)
                for j in range(2):
                    last = mm(G[0:HT, j, D + 2:D + 3], ssq[:, HT * j:HT * j + HT], cst[0:PIX, C_CNT:C_CNT + 1],
                              start=True, stop=True)
                last.then_inc(p_tok, 1)

            def x_turn(i, back, route):
                pe.wait_ge(d_tok, i + 1)
                pe.wait_ge(d_xn, i + 1)
                for c in range(2):
                    if c == 0 and route:
                        pe.wait_ge(a_lt, 2 * (i - 2) + 2)
                    if c == 1 and back:
                        pe.wait_ge(a_yt, 3 * (i - 1) + 1)
                    for j in range(3):
                        last = nc.tensor.transpose(G[0:HC, 2 * c, OFF[j]:OFF[j] + ROWS[j]],
                                                   XN[0:ROWS[j], j, c * HC:(c + 1) * HC],
                                                   ident[0:ROWS[j], 0:ROWS[j]])
                    last.then_inc(p_xt, 1)

            SPLIT = [(XTH, 0, c, HC + c) for c in range(2)] + [(XTH, 1, c, HC + c) for c in range(2)] + [
                (XTL, 0, c, HC) for c in range(2)]

            def project_qk(i, route):
                pe.wait_ge(d_xt, 2 * i + 2)
                for n in range(4):
                    bank = (2, 1, 0, 2)[n]
                    if n == 1 and route:
                        pe.wait_ge(d_pref, i - 1)
                    if n == 3:
                        pe.wait_ge(a_qk, 4 * i + 1)
                    for m, (xs, part, c, r) in enumerate(SPLIT):
                        last = mm(G[0:HC, bank, 0:T], cut((WAH, WAL)[part][0:r, c, HC * n:HC * n + HC]),
                                  cut(xs[0:r, c, :]), start=(m == 0), stop=(m == len(SPLIT) - 1))
                    last.then_inc(p_qkv, 1)

            def project_v(i, n, back):
                m0, m1 = ((0, 2), (2, 3))[n]
                if n == 0:
                    pe.wait_ge(a_qk, 4 * i + 4)
                elif back:
                    pe.wait_ge(a_yt, 3 * (i - 1) + 2)
                for m in range(m0, m1):
                    for k, (xs, part, c, r) in enumerate(SPLIT):
                        last = mm(G[0:VTOK, 2 - n, VD * (m - m0):VD * (m - m0) + VD],
                                  cut(xs[0:r, c, VTOK * m:VTOK * (m + 1)]), cut((WVH, WVL)[part][0:r, c, :]),
                                  start=(k == 0), stop=(k == len(SPLIT) - 1))
                last.then_inc(p_qkv, 1)

            def maxima(i, back):
                pe.wait_ge(s_qdb, 16 * HG * (i + 1))
                pe.wait_ge(a_qk, 4 * i + 4)
                if back:
                    pe.wait_ge(a_exp, 6 * i)
                for n in range(UNITS):
                    if n >= 4:
                        pe.wait_ge(d_max, UNITS * i + n - 3)
                    t0 = 4 * n % NBLK
                    mm(ST[0:2 * QB, n % 4, 0:4 * KW], identb[0:2 * QB, 0:2 * QB], mqb[:, t0:t0 + 4, :], start=True,
                       stop=True, skip_group_check=True)
                    for m in range(4):
                        p, t = (4 * n + m) // NBLK, (4 * n + m) % NBLK
                        last = mm(ST[0:2 * QB, n % 4, KW * m:KW * m + KW],
                                  QDb[:, p, t, :, :].rearrange("p w q -> p (w q)"),
                                  KTb[:, p % 2, QB * t:QB * t + KW], start=False, stop=True, skip_group_check=True)
                    last.then_inc(p_smax, 1)

            def max_turn(i):
                pe.wait_ge(d_max, UNITS * i + UNITS)
                nc.tensor.transpose(ST[0:80, 1, 0:2 * QB], M[:, :], ident[0:2 * QB, 0:2 * QB]).then_inc(p_mt, 1)

            def scores(a, n):
                t = ORDER[n]
                if n == 0:
                    pe.wait_ge(s_qd, 16 * HG * (a + 1))
                    pe.wait_ge(s_mrow, 32 * (a + 1))
                    pe.wait_ge(d_max, UNITS * a + UNITS)
                if n >= 2:
                    pe.wait_ge(a_exp, 6 * a + n - 1)
                for g in range(2):
                    bank = 2 * (n % 2) + g
                    mm(ST[0:KW, bank, 0:HG * QB], identb[0:KW, 0:KW],
                       mtb[0:KW, min(t, 2), :].unsqueeze(1).broadcast_to([KW, HG, QB]), start=True, stop=False)
                    last = mm(ST[0:KW, bank, 0:HG * QB], KT[:, g, QB * t:QB * t + KW],
                              QD[:, g:HEADS:2, QB * t:QB * t + QB],
                             start=False, stop=True)
                last.then_inc(p_st, 1)

            def weighted(a, n):
                t, s = ORDER[n], n % 2
                pe.wait_ge(a_exp, 6 * a + n + 1)
                if n == 0:
                    pe.wait_ge(s_v, 64 * (a + 1))
                if s == 0 and not (n == 0 and isinstance(a, int) and a == 0):
                    pe.wait_ge(d_norm, 3 * a + n // 2)
                for h in range(HEADS):
                    last = mm(Y[64 * s:64 * s + QB, (HD + 1) * h:(HD + 1) * (h + 1)],
                              PR[:, n % 2, h // HG, QB * (h % HG):QB * (h % HG) + QB],
                              V[:, t, (HD + 1) * h:(HD + 1) * (h + 1)],
                              start=True, stop=True)
                last.then_inc(p_pv, 1)

            def y_turn(a, j, bank):
                pe.wait_ge(d_norm, 3 * a + j + 1)
                for c in range(2):
                    last = nc.tensor.transpose(G[0:HC, bank, 128 * c:128 * c + 118], ysb[0:118, c * HC:(c + 1) * HC],
                                               ident[0:118, 0:118])
                last.then_inc(p_yt, 1)

            def project_out(a, tiles, front):
                pe.wait_ge(a_yt, 3 * a + 3)
                for j in tiles:
                    if j > 0 and front:
                        pe.wait_ge(a_v, 2 * (a + 1) + j)
                    halves(G[0:ROWS[j], (0, 2, 1)[j], 0:D], lambda c, r: YT[0:r, c, OFF[j]:OFF[j] + ROWS[j]],
                           lambda c, r: WP[0:r, c, :]).then_inc(p_proj, 1)

            def router_turn(a, front):
                pe.wait_ge(d_h2, 3 * a + 3)
                pe.wait_ge(d_xn2, a + 1)
                for c in range(2):
                    if c == 1 and front:
                        pe.wait_ge(d_tok, a + 3)
                    for j in range(3):
                        last = nc.tensor.transpose(G[0:HC, 2 - 2 * c, OFF[j]:OFF[j] + ROWS[j]],
                                                   XN2[0:ROWS[j], j, c * HC:(c + 1) * HC],
                                                   ident[0:ROWS[j], 0:ROWS[j]])
                    last.then_inc(p_lt, 1)

            def logits(a):
                pe.wait_ge(a_lt, 2 * a + 2)
                for j in range(3):
                    last = halves(G[0:ROWS[j], 1, 8 * j:8 * j + 8], lambda c, r: XT2[0:r, c, OFF[j]:OFF[j] + ROWS[j]],
                                  lambda c, r: SW[0:r, c, :])
                last.then_inc(p_log, 1)

            def prefixes(a):
                pe.wait_ge(d_oh, a + 1)
                for j in range(3):
                    for m in range(j):
                        mm(G[:, 1, 8 * j:8 * j + 8], onesb[0:ROWS[m], :], OHb[0:ROWS[m], m, :],
                           start=(m == 0), stop=False)
                    mm(G[:, 1, 8 * j:8 * j + 8], utrib[0:ROWS[j], :], OHb[0:ROWS[j], j, :], start=(j == 0), stop=True)
                for j in range(3):
                    last = mm(G[:, 1, 24:32], onesb[0:ROWS[j], :], OHb[0:ROWS[j], j, :], start=(j == 0), stop=(j == 2))
                last.then_inc(p_pref, 1)

            def body(i, front, back, route):
                b, c = i - 1, i - 2
                if front:
                    tokens(i, back)
                elif back:
                    max_turn(b)
                if back:
                    scores(b, 0)
                if route:
                    router_turn(c, front)
                if back:
                    scores(b, 1)
                    weighted(b, 0)
                    scores(b, 2)
                    weighted(b, 1)
                if route:
                    logits(c)
                if back:
                    scores(b, 3)
                    if route:
                        pe.wait_ge(a_lt, 2 * c + 1)
                    else:
                        pe.wait_ge(a_v, 2)
                    y_turn(b, 0, 2)
                    weighted(b, 2)
                    scores(b, 4)
                if front:
                    x_turn(i, back, route)
                if back:
                    weighted(b, 3)
                if route:
                    prefixes(c)
                if back:
                    scores(b, 5)
                if front:
                    project_qk(i, route)
                if back:
                    if front:
                        pe.wait_ge(a_qk, 4 * i + 2)
                    else:
                        pe.wait_ge(d_pref, c + 1)
                    y_turn(b, 1, 1)
                    weighted(b, 4)
                    weighted(b, 5)
                if front:
                    project_v(i, 0, back)
                if back:
                    if front:
                        pe.wait_ge(a_qk, 4 * i + 3)
                    else:
                        pe.wait_ge(a_lt, 2 * c + 2)
                    y_turn(b, 2, 0)
                if front:
                    project_v(i, 1, back)
                if back:
                    project_out(b, (0, 1), front)
                if front:
                    maxima(i, back)
                if back:
                    project_out(b, (2,), front)

            pe.wait_ge(s_cst, 16 * 5)
            pe.wait_ge(d_set, 1)
            n = 0
            for s in SHIFTS:
                pe.wait_ge(s_ws[s], 16)
                for k in range(PCH):
                    mm(G[0:HT, 0, 0:D], BT[:, s, k:k + 1].broadcast_to([PIX, HT]), WS[:, s, k, :],
                       start=(n == 0), stop=False)
                    n += 1
            mm(G[0:HT, 0, 0:D], ones[0:1, 0:HT], btrow[:, :], start=False, stop=True).then_inc(p_set, 1)
            pe.wait_ge(d_we, 1)
            for k in range(PCH):
                last = mm(G[0:HT, 1, 0:D], ones[0:PIX, 0:HT], WE[:, k, 0:D], start=(k == 0), stop=(k == PCH - 1))
            last.then_inc(p_set, 1)

            pe.wait_ge(s_set, 16 * SET_LOADS)
            pe.wait_ge(g_set, 10)
            pe.wait_ge(d_set, 2)
            pe.wait_ge(d_wl, 2)
            body(0, True, False, False)
            body(1, True, True, False)
            with pe.Fori(2, NB) as i:
                body(i, True, True, True)
            body(NB, False, True, True)
            body(NB + 1, False, False, True)

            with pe.Fori(0, TAU_STEPS + IDX_STEPS) as n:
                pe.wait_ge(d_cn, n + 1)
                mm(G[:, 0, 0:1], cst[:, C_BLK:C_BLK + 128], CN[:, :], start=True, stop=True).then_inc(p_cnt, 1)
            steps = TAU_STEPS + IDX_STEPS
            pe.wait_ge(d_cn, steps + 1)
            for n, found in enumerate((TAUL, IDXL)):
                last = mm(G[:, 0, 8 * n:8 * n + 8], found[:, 0:1].broadcast_to([128, 128]), ident[:, 0:128:LANES],
                          start=True, stop=True)
            last.then_inc(p_cnt, 1)

            def turn(k, u):
                pe.wait_ge(d_xm, k + 1)
                if not (isinstance(k, int) and k == 0):
                    pe.wait_ge(d_xl, k)
                for c in range(2):
                    last = nc.tensor.transpose(G[0:HC, 2, 128 * c:128 * c + 128],
                                               XM[:, u, c * HC:(c + 1) * HC], ident[:, :])
                last.then_inc(p_mx, 1)

            def layer1(k, v):
                e = pe.value_load(TBI[0:1, 1, bass.ds(k, 1)], min_val=0, max_val=EXPERTS - 1)
                pe.wait_ge(a_mx, k + 1)
                if not (isinstance(k, int) and k < 2):
                    pe.wait_ge(a_gelu, k - 1)
                for x, w, ones_row in ((XMTH, W1H, 1), (XMTH, W1L, 1), (XMTL, W1H, 0)):
                    if x is XMTL:
                        pe.wait_ge(d_xl, k + 1)
                    for half in range(2):
                        for c in range(2):
                            r = HC + c * ones_row
                            last = mm(ST[:, 2 * v + half, 0:FF // 2], cut(x[0:r, v, c, :]),
                                      cut(w[0:r, c, bass.ds(e, 1), half * (FF // 2):(half + 1) * (FF // 2)]),
                                      start=(c == 0 and w is W1H and x is XMTH), stop=(c == 1 and x is XMTL),
                                      skip_group_check=True)
                last.then_inc(p_l1, 1)

            def hidden_turn(k):
                pe.wait_ge(a_gelu, k + 1)
                if not (isinstance(k, int) and k == 0):
                    pe.wait_ge(d_ht, 2 * k)
                for f in range(FCH):
                    last = nc.tensor.transpose(G[:, f // 3, 128 * (f % 3):128 * (f % 3) + 128],
                                               HS[:, 128 * f:128 * f + 128], ident[:, :])
                last.then_inc(p_ht, 1)

            def layer2(k):
                e = pe.value_load(TBI[0:1, 1, bass.ds(k, 1)], min_val=0, max_val=EXPERTS - 1)
                if not (isinstance(k, int) and k == 0):
                    pe.wait_ge(d_out, k)
                for f in range(FCH):
                    if f % 3 == 0:
                        pe.wait_ge(a_ht, 2 * k + f // 3 + 1)
                    mm(Y[:, 0:2 * D], cut(HTH[:, f, :]),
                       cut(W2HL[:, bass.ds(e, 1), f, :, :].rearrange("p o s d -> p (o s d)")),
                       start=(f == 0), stop=(f == FCH - 1), skip_group_check=True)
                for f in range(FCH):
                    if f % 3 == 0:
                        pe.wait_ge(d_ht, 2 * k + f // 3 + 1)
                    last = mm(Y[:, 0:D], cut(HTL[:, f, :]),
                              cut(W2HL[:, bass.ds(e, 1), f, 0:1, :].rearrange("p o s d -> p (o s d)")),
                              start=False, stop=(f == FCH - 1), skip_group_check=True)
                last.then_inc(p_l2, 1)

            pe.wait_ge(g_split, len(parts))
            pe.wait_ge(d_tab, 1)
            turn(0, 0)
            turn(1, 1)
            layer1(0, 0)

            def four(it):
                for u in range(4):
                    k = it * 4 + u
                    hidden_turn(k)
                    layer1(k + 1, (u + 1) % 2)
                    turn(k + 2, (u + 2) % 4)
                    layer2(k)

            four(0)
            with pe.Fori(1, NT // 4) as it:
                four(it)

        @block.vector
        def _(dve):
            class Chain:

                def __init__(self, s, base=0):
                    self.s, self.base, self.n = s, base, 0

                def __call__(self, ins):
                    self.n += 1
                    ins.then_inc(self.s, 1)
                    dve.wait_ge(self.s, self.base + self.n)

            v = nc.vector
            FRONT, BACK, ROUTE = 4, 4, 11

            v.memset(H[:, :, :], 0.0)
            v.memset(M[:, :], 0.0)
            v.memset(ones[:, :], 1.0)
            v.memset(ROW[:, :, :], 0.0)
            v.memset(Y[:, :], 1.0)
            v.memset(BASE[:, :], 0.0)
            v.memset(G[:, :, :], 0.0)
            v.memset(onesb[:, :], 1.0)
            v.memset(WE[:, :, D:D + 2], 0.0)
            v.memset(WVV[0:HC, :, :, HD], 0.0)
            v.memset(WVV[HC:HC + 1, :, :, HD], 1.0)
            v.memset(PME[:, :, :], 0.0).then_inc(d_set, 1)
            dve.wait_ge(d_set, 1)
            link = Chain(c_set)
            dve.wait_ge(s_cst, 16 * 5)
            v.tensor_copy(identb[:, :], ident)
            v.tensor_copy(utrib[:, :], masks[:, M_UT:M_UT + 128])
            for t in range(NBLK + 2):
                at_mask = M_MQ + KW * min(t % NBLK, 2)
                v.tensor_copy(mqb[:, t, :], masks[0:2 * QB, at_mask:at_mask + KW])
            v.tensor_copy(mtb[:, :, :], masks[:, M_MT:MASKS].rearrange("p (v k) -> p v k", v=3))
            v.tensor_copy(TK[:, :], cst[:, C_TOK:C_TOK + 3])
            v.memset(ZR[:, :], 0.0)
            link(v.tensor_copy(WE[:, :, D], cst[0:PIX, C_CNT:C_CNT + 1].broadcast_to([PIX, PCH])))
            link(v.memset(ZR[:, D + 3:D + 4], float(SKIP)))
            dve.wait_ge(s_ws[0], 16)
            link(v.tensor_tensor(WE[:, :, 0:D], WS[:, 0, :, :], GM[:, 0, :].unsqueeze(2).broadcast_to([PIX, PCH, D]),
                                 ALU.mult))
            for s in range(1, 3):
                dve.wait_ge(s_ws[s], 16)
                link(v.tensor_tensor(WTMP[:, :, :], WS[:, s, :, :],
                                     GM[:, s, :].unsqueeze(2).broadcast_to([PIX, PCH, D]), ALU.mult))
                link(v.tensor_tensor(WE[:, :, 0:D], WE[:, :, 0:D], WTMP[:, :, :], ALU.add))
            dve.wait_ge(g_we, 3)
            link(v.tensor_tensor(WE[:, :, 0:D], WE[:, :, 0:D], WTM2[:, :, :], ALU.add))
            v.memset(MV[:, :, :], 0.0).then_inc(d_we, 1)
            SETUP = link.n
            dve.wait_ge(a_wh, 4)
            for high, low, weights in ((WAH, WAL, WA), (WVH, WVL, WV)):
                for c in range(2):
                    v.tensor_tensor(cut(low[0:HC + c, c, :]), weights[0:HC + c, c, :], high[0:HC + c, c, :], ALU.subtract)
            v.tensor_copy(cut(XTH[HC:HC + 1, :, :].rearrange("p c t -> p (c t)")),
                          ones[HC:HC + 1, 0:1].broadcast_to([1, 2 * T])).then_inc(d_wl, 1)
            dve.wait_ge(a_wh, 5)
            v.tensor_tensor(cut(WEL[:, :, :]), WE[:, :, :], WEH[:, :, :], ALU.subtract).then_inc(d_wl, 1)
            dve.wait_ge(p_set, 1)
            v.tensor_copy(tbias[:, :], G[0:HT, 0, 0:D])
            dve.wait_ge(p_set, 2)
            v.tensor_copy(csum[:, :], G[0:HT, 1, 0:D]).then_inc(d_set, 1)
            dve.wait_ge(d_set, 2)

            def front(i):
                link = Chain(c_front, i * FRONT)
                first = isinstance(i, int) and i == 0
                dve.wait_ge(p_tok, i + 1)
                link(v.tensor_scalar(negmu[:, :, :], G[0:HT, 0:2, D:D + 1], -1.0 / PATCH_DIM, None, ALU.mult))
                link(v.tensor_tensor(msq[:, :, :], negmu[:, :, :], negmu[:, :, :], ALU.mult))
                v.scalar_tensor_tensor(tvar[:, :, :], G[0:HT, 0:2, D + 2:D + 3], 1.0 / PATCH_DIM, msq[:, :, :],
                                       ALU.mult, ALU.subtract).then_inc(d_tvar, 1)
                for j in range(2):
                    last = v.scalar_tensor_tensor(TMP[:, j, :], csum[:, :], negmu[:, j, :], G[0:HT, j, 0:D],
                                                  ALU.mult, ALU.add)
                last.then_inc(d_tok, 1)
                dve.wait_ge(d_tok, i + 1)
                dve.wait_ge(g_trstd, i + 1)
                if not first:
                    dve.wait_ge(a_r, i)
                for j in range(2):
                    last = v.scalar_tensor_tensor(H[0:HT, j, :], TMP[:, j, :], trstd[:, j, :], tbias[:, :],
                                                  ALU.mult, ALU.add)
                link(last)
                dve.wait_ge(s_txt, 16 * (i + 1))
                for j in range(3):
                    last = v.bn_stats(BN[:, j, :], H[:, j, :])
                link(last)
                v.memset(pause[:, :], 0.0)
                for j in range(3):
                    last = v.bn_aggr(MV[:, j, :], BN[:, j, :])
                last.then_inc(d_mv, 1)
                dve.wait_ge(d_mv, i + 1)
                dve.wait_ge(g_r1, i + 1)
                if not first:
                    dve.wait_ge(p_xt, 2 * i)
                for j in range(3):
                    last = v.tensor_scalar(XN[:, j, :], H[:, j, :], MV[:, j, 0:1], rstd1[:, j:j + 1],
                                           ALU.subtract, ALU.mult)
                last.then_inc(d_xn, 1)
                assert link.n == FRONT

            def squares(i):
                dve.wait_ge(a_sq, i + 1)
                if not (isinstance(i, int) and i == 0):
                    dve.wait_ge(p_tok, i)
                v.tensor_reduce(ssq[:, :], sq[:, :, :].rearrange("p k n -> p n k"), AX_X, ALU.add).then_inc(d_sq, 1)

            def maxima(i):
                first = isinstance(i, int) and i == 0
                if not first:
                    dve.wait_ge(p_mt, i)
                for n in range(UNITS):
                    dve.wait_ge(p_smax, UNITS * i + n + 1)
                    v.tensor_reduce(M[:, 4 * n:4 * n + 4], ST[0:2 * QB, n % 4, 0:4 * KW].rearrange("p (h k) -> p h k", h=4),
                                    AX_X, ALU.max, negate=True).then_inc(d_max, 1)

            def max_rows(i):
                dve.wait_ge(p_mt, i + 1)
                if not (isinstance(i, int) and i == 0):
                    dve.wait_ge(s_mrow, 32 * i)
                v.tensor_copy(mT[:, :], ST[0:4 * UNITS, 1, 0:2 * QB]).then_inc(d_mt, 1)

            def normalise(a, j, link):
                dve.wait_ge(p_pv, 6 * a + 2 * j + 2)
                if not (j == 0 and isinstance(a, int) and a == 0):
                    dve.wait_ge(p_yt, 3 * a + j)
                yv = Y[:, 0:HEADS * (HD + 1)].rearrange("p (h d) -> p h d", h=HEADS)
                link(v.reciprocal(rec[:, :], yv[:, :, HD]))
                v.tensor_tensor(ysb[:, :].rearrange("p (h d) -> p h d", h=HEADS), yv[:, :, 0:HD],
                                rec[:, :].unsqueeze(2).broadcast_to([128, HEADS, HD]), ALU.mult).then_inc(d_norm, 1)

            def second(a, tiles):
                first = isinstance(a, int) and a == 0
                if 0 in tiles:
                    if not first:
                        dve.wait_ge(s_scat, 48 * a)
                    dve.wait_ge(a_r, a + 1)
                for j in tiles:
                    dve.wait_ge(p_proj, 3 * a + j + 1)
                    v.tensor_tensor(ROW[0:ROWS[j], j, 0:D], G[0:ROWS[j], (0, 2, 1)[j], 0:D], R[0:ROWS[j], j, :],
                                    ALU.add).then_inc(d_h2, 1)

            def second_statistics(a, link):
                dve.wait_ge(d_h2, 3 * a + 3)
                for j in range(3):
                    last = v.bn_stats(BN2[:, j, :], ROW[:, j, 0:D])
                link(last)
                v.memset(pause[:, :], 0.0)
                for j in range(3):
                    last = v.bn_aggr(ROW[:, j, D:D + 2], BN2[:, j, :])
                last.then_inc(d_mv2, 1)

            def router_rows(a):
                first = isinstance(a, int) and a == 0
                dve.wait_ge(d_mv2, a + 1)
                dve.wait_ge(g_r2, a + 1)
                if not first:
                    dve.wait_ge(p_lt, 2 * a)
                for j in range(3):
                    last = v.tensor_scalar(XN2[:, j, :], ROW[:, j, 0:D], ROW[:, j, D:D + 1], ROW[:, j, D + 1:D + 2],
                                           ALU.subtract, ALU.mult)
                last.then_inc(d_xn2, 1)

            def wide(ap):
                return ap.unsqueeze(2).broadcast_to([128, 3, EXPERTS])

            def per_expert(ap):
                return ap.unsqueeze(1).broadcast_to([128, 3, EXPERTS])

            def route(a, link):
                dve.wait_ge(p_log, a + 1)
                lg = G[:, 1, 0:24].rearrange("p (j e) -> p j e", j=3)
                link(v.tensor_reduce(LM[:, :], lg, AX_X, ALU.max))
                if not (isinstance(a, int) and a == 0):
                    dve.wait_ge(a_el, a)
                v.tensor_tensor(LS[:, :, :], lg, wide(LM[:, :]), ALU.subtract).then_inc(d_ls, 1)
                v.tensor_tensor(EQ[:, :, :], lg, wide(LM[:, :]), ALU.is_equal).then_inc(d_log, 1)
                dve.wait_ge(d_log, a + 1)
                link(v.tensor_tensor(SC[:, :, :], EQ[:, :, :], per_expert(cst[:, C_W8:C_W8 + 8]), ALU.mult))
                link(v.tensor_reduce(MX[:, :], SC[:, :, :], AX_X, ALU.max))
                link(v.tensor_tensor(EQ[:, :, :], SC[:, :, :], wide(MX[:, :]), ALU.is_equal))
                if not (isinstance(a, int) and a == 0):
                    dve.wait_ge(p_pref, a)
                v.tensor_tensor(OH[:, :, :], EQ[:, :, :], wide(cst[:, C_VALID:C_VALID + 3]), ALU.mult)
                v.tensor_tensor(OHb[:, :, :], EQ[:, :, :], wide(cst[:, C_VALID:C_VALID + 3]), ALU.mult).then_inc(
                    d_oh, 1)
                dve.wait_ge(a_el, a + 1)
                link(v.tensor_reduce(ES[:, :], EL[:, :, :], AX_X, ALU.add))
                link(v.reciprocal(ROW[:, :, D + 2], ES[:, :]))

            def place(a, link):
                dve.wait_ge(p_pref, a + 1)
                dve.wait_ge(d_oh, a + 1)
                link(v.tensor_tensor(POS[:, :, :], G[:, 1, 0:24].rearrange("p (j e) -> p j e", j=3),
                                     per_expert(BASE[:, :]), ALU.add))
                v.tensor_tensor(BASE[:, :], BASE[:, :], G[:, 1, 24:32], ALU.add).then_inc(d_pref, 1)
                dve.wait_ge(d_pref, a + 1)
                link(v.tensor_tensor(POS[:, :, :], POS[:, :, :], per_expert(cst[:, C_EOFF:C_EOFF + 8]), ALU.add))
                link(v.tensor_tensor(POS[:, :, :], POS[:, :, :], OH[:, :, :], ALU.mult))
                link(v.tensor_reduce(SLF[:, :], POS[:, :, :], AX_X, ALU.add))
                v.tensor_copy(SLI[:, :], SLF[:, :])
                v.tensor_tensor(PME[:, :, bass.ds(3 * a, 3)].rearrange("p e j -> p j e"), OH[:, :, :],
                                wide(ROW[:, :, D + 2]), ALU.mult)
                link(v.tensor_copy(ROW[:, :, D + 3], TK[:, :]))
                v.tensor_scalar(TK[:, :], TK[:, :], float(T), None, ALU.add).then_inc(d_row, 1)
                dve.wait_ge(d_row, a + 1)

            def body(i, do_front, back, do_route, more):
                b, c = i - 1, i - 2
                link, rlink = Chain(c_back, b * BACK), Chain(c_route, c * ROUTE)
                if do_front:
                    front(i)
                if back:
                    normalise(b, 0, link)
                if do_route:
                    route(c, rlink)
                if do_front:
                    x_low(i)
                if back:
                    normalise(b, 1, link)
                if do_route:
                    place(c, rlink)
                    assert rlink.n == ROUTE
                if more:
                    squares(i + 1)
                if back:
                    normalise(b, 2, link)
                    second(b, (0, 1))
                if do_front:
                    maxima(i)
                if back:
                    second(b, (2,))
                if do_front:
                    max_rows(i)
                if back:
                    second_statistics(b, link)
                    assert link.n == BACK
                    router_rows(b)

            def x_low(i):
                for c in range(2):
                    dve.wait_ge(a_xt, 2 * i + c + 1)
                    if c == 0 and not (isinstance(i, int) and i == 0):
                        dve.wait_ge(p_qkv, 6 * i)
                    v.tensor_tensor(cut(XTL[:, c, :]), G[0:HC, 2 * c, 0:T], XTH[0:HC, c, :], ALU.subtract).then_inc(
                        d_xt, 1)

            squares(0)
            body(0, True, False, False, True)
            body(1, True, True, False, True)
            body(2, True, True, True, True)
            with dve.Fori(3, NB - 1) as i:
                body(i, True, True, True, True)
            body(NB - 1, True, True, True, False)
            body(NB, False, True, True, False)
            body(NB + 1, False, False, True, False)

            link = Chain(c_set, SETUP)
            link(v.tensor_scalar(NTE[:, :], BASE[:, :], 127.0, None, ALU.add))
            link(v.tensor_copy(CI[:, :], NTE[:, :]))
            v.tensor_copy(CNTI[:, :], BASE[:, :])
            link(v.tensor_scalar(CI2[:, :], CI[:, :], 7, None, ALU.arith_shift_right))
            link(v.tensor_copy(NTE[:, :], CI2[:, :]))
            link(v.tensor_tensor_scan(FI[:, :], ones[0:1, 0:8], NTE[0:1, :], 0.0, ALU.mult, ALU.add))
            link(v.tensor_tensor(FE[:, :], FI[:, :], NTE[0:1, :], ALU.subtract))
            link(v.tensor_scalar(AE[:, :], FE[:, :], -128.0, -float(DUMMY), ALU.mult, ALU.add))
            link(v.tensor_tensor(AE[:, :], AE[:, :], cst[0:1, C_EOFF:C_EOFF + 8], ALU.add))
            shape = [1, NTP, EXPERTS]
            kio = cst[0:1, C_KI:C_KI + NTP].unsqueeze(2).broadcast_to(shape)

            def each(ap):
                return ap.unsqueeze(1).broadcast_to(shape)

            v.tensor_tensor(IN1[:, :, :], kio, each(FE[:, :]), ALU.is_ge)
            link(v.tensor_tensor(IN2[:, :, :], kio, each(FI[:, :]), ALU.is_ge))
            link(v.tensor_tensor(IN1[:, :, :], IN1[:, :, :], IN2[:, :, :], ALU.subtract))
            link(v.scalar_tensor_tensor(IN2[:, :, :], kio, 128.0, each(AE[:, :]), ALU.mult, ALU.add))
            link(v.tensor_tensor(IN2[:, :, :], IN2[:, :, :], IN1[:, :, :], ALU.mult))
            link(v.tensor_tensor(IN3[:, :, :], IN1[:, :, :], each(cst[0:1, C_EI:C_EI + 8]), ALU.mult))
            link(v.tensor_reduce(TBF[:, 0, :], IN2[:, :, :], AX_X, ALU.add))
            link(v.tensor_reduce(TBF[:, 1, :], IN3[:, :, :], AX_X, ALU.add))
            link(v.tensor_scalar(TBF[:, 0, :], TBF[:, 0, :], float(DUMMY), None, ALU.add))
            v.tensor_copy(TBI[:, :, :], TBF[:, :, :]).then_inc(d_tab, 1)
            dve.wait_ge(d_tab, 1)

            SRCH = 2
            v.memset(TAUL[:, :], 0.0625)
            v.memset(STEP[:, :], 0.5)
            link(v.memset(MID[:, :], 0.5625))

            def count_step(n, key, keep_op, bound_op, value):
                s = Chain(c_srch, n * SRCH)
                v.tensor_scalar(GE, key, MID[:, 0:1], 0.0, keep_op, ALU.add, accum_out=CN[:, :]).then_inc(d_cn, 1)
                dve.wait_ge(p_cnt, n + 1)
                v.scalar_tensor_tensor(INC[:, :], G[:, 0, 0:1], float(CAP), STEP[:, :], bound_op, ALU.mult)
                s(v.tensor_scalar(STEP[:, :], STEP[:, :], 0.5, None, ALU.mult))
                v.scalar_tensor_tensor(MID[:, :], value[:, :], INC[:, 0:1], STEP[:, :], ALU.add, ALU.add)
                s(v.tensor_tensor(value[:, :], value[:, :], INC[:, :], ALU.add))
                assert s.n == SRCH

            dve.wait_ge(s_px, 32)
            with dve.Fori(0, TAU_STEPS // 9) as n:
                for m in range(9):
                    count_step(n * 9 + m, PX, ALU.is_ge, ALU.is_ge, TAUL)

            v.tensor_scalar(GE, PX, TAUL[:, 0:1], -float(SKIP) - 1.0, ALU.is_gt, ALU.mult)
            link(v.scalar_tensor_tensor(KEY, PX, TAUL[:, 0:1], TX, ALU.is_equal, ALU.mult))
            v.memset(IDXL[:, :], 0.0)
            v.memset(STEP[:, :], float(1 << (IDX_STEPS - 1)))
            v.memset(MID[:, :], float(1 << (IDX_STEPS - 1)))
            link(v.scalar_tensor_tensor(KEY, KEY, float(SKIP), GE, ALU.add, ALU.add))
            with dve.Fori(0, IDX_STEPS // 7) as n:
                for m in range(7):
                    count_step(n * 7 + (TAU_STEPS + m), KEY, ALU.is_lt, ALU.is_le, IDXL)
            v.memset(pause[:, :], 0.0).then_inc(d_cn, 1)
            dve.wait_ge(p_cnt, TAU_STEPS + IDX_STEPS + 1)
            v.tensor_copy(LIM[:, :, :], G[:, 0, 0:16].rearrange("p (s e) -> p e s", s=2)).then_inc(d_lim, 1)

            MOE = 2

            def normal(k, u, r):
                dve.wait_ge(s_row[u], 16 * (r + 1))
                if not (isinstance(k, int) and k < 4):
                    dve.wait_ge(p_mx, k - 3)
                v.tensor_scalar(XM[:, u, :], RT[:, u, 0:D], RT[:, u, D:D + 1], RT[:, u, D + 1:D + 2],
                                ALU.subtract, ALU.mult).then_inc(d_xm, 1)

            def compare(k, u):
                dve.wait_ge(g_fetch, k + 1)
                pm, tok = RT[:, u, D + 2:D + 3], RT[:, u, D + 3:D + 4]
                tau, idx = lim[:, u, 0:1], lim[:, u, 1:2]
                v.tensor_tensor(at[:, u, :], pm, tau, ALU.is_equal)
                v.tensor_tensor(above[:, u, :], pm, tau, ALU.is_gt)
                v.tensor_tensor(among[:, u, :], tok, idx, ALU.is_lt).then_inc(d_cmp, 1)

            def residual_part(k, u):
                s = Chain(c_moe, k * MOE)
                dve.wait_ge(g_keep, k * KEEP + KEEP)
                s(v.scalar_tensor_tensor(Y2[:, :], XM[:, u, :], c2[:, u:u + 1], RT[:, u, 0:D], ALU.mult, ALU.add))
                s(v.scalar_tensor_tensor(Y2[:, :], bias2[:, u, :],
                                         c1[:, u:u + 1], Y2[:, :], ALU.mult, ALU.add))
                assert s.n == MOE

            def combine(k, u, it):
                dve.wait_ge(p_l2, k + 1)
                v.scalar_tensor_tensor(Y1[:, :], Y[:, 0:D], c1[:, u:u + 1], Y2[:, :], ALU.mult, ALU.add).then_inc(
                    d_y, 1)
                dve.wait_ge(d_y, k + 2)
                if not isinstance(it, int):
                    dve.wait_ge(s_out[u], 16 * it)
                v.tensor_copy(OI[:, u:u + 1], RT[:, u, D + 3:D + 4])
                v.scalar_tensor_tensor(OT[:, u, :], Y[:, D:2 * D], c1[:, u:u + 1], Y1[:, :], ALU.mult, ALU.add).then_inc(
                    d_out, 1)

            link(v.tensor_copy(cut(XMTH[HC:HC + 1, :, :, :].rearrange("p v c n -> p (v c) n")),
                               ones[HC:HC + 1, :].unsqueeze(1).broadcast_to([1, 4, 128])))
            v.memset(pause[:, :], 0.0).then_inc(d_y, 1)
            for k in range(3):
                normal(k, k, 0)
            compare(0, 0)

            def low_parts(k, w):
                dve.wait_ge(a_mx, k + 1)
                if not (isinstance(k, int) and k < 2):
                    dve.wait_ge(p_l1, k - 1)
                v.tensor_tensor(cut(XMTL[:, w, :, :]), G[0:HC, 2, 0:256].rearrange("p (c n) -> p c n", c=2),
                                 XMTH[0:HC, w, :, :], ALU.subtract).then_inc(d_xl, 1)

            low_parts(0, 0)
            low_parts(1, 1)

            def four(it):
                for u in range(4):
                    k = it * 4 + u
                    if not (isinstance(k, int) and k == 0):
                        dve.wait_ge(p_l2, k)
                    for b in range(2):
                        dve.wait_ge(a_ht, 2 * k + b + 1)
                        v.tensor_tensor(cut(HTL[:, 3 * b:3 * b + 3, :]),
                                        G[:, b, 0:384].rearrange("p (f n) -> p f n", f=3),
                                        HTH[:, 3 * b:3 * b + 3, :], ALU.subtract).then_inc(d_ht, 1)
                    residual_part(k, u)
                    compare(k + 1, (u + 1) % 4)
                    normal(k + 3, (u + 3) % 4, it if u == 0 else it + 1)
                    low_parts(k + 2, u % 2)
                    combine(k, u, it)

            four(0)
            with dve.Fori(1, NT // 4) as it:
                four(it)


_INS = ["x", "txt", "wtok", "gam", "bet", "btok", "wattn", "battn", "wproj", "bproj", "wsw", "bsw",
        "w1", "b1", "w2", "b2", "const", "numbers"]


def _layout(np):
    pix = [(c, y, x) for c in range(3) for y in range(18) for x in range(18)
           if not (y in (0, 17) and x in (0, 17))]
    moves = [(1, 1), (1, 0), (1, 2), (0, 1), (2, 1)]
    often = [sum(0 <= y - dy < 16 and 0 <= x - dx < 16 for dy, dx in moves) for _, y, x in pix]
    groups = [[q for q, m in zip(pix, often) if m == times] for times in (5, 4, 3, 1)]
    times = [m for g, m in zip(groups, (5, 4, 3, 1)) for _ in range(-(-len(g) // PCH))]
    pix = [q for g in groups for q in g + [(3, 0, 0)] * (-len(g) % PCH)]
    rows = np.full((5, len(pix)), PATCH_DIM, np.int64)
    for s, (dy, dx) in enumerate(moves):
        for n, (c, y, x) in enumerate(pix):
            py, px = y - dy, x - dx
            if 0 <= py < 16 and 0 <= px < 16:
                rows[s, n] = (py * 16 + px) * 15 + 3 * s + c
    return pix, rows, times


def _constants(np, nb, times):
    n_tiles = tiles_of(nb * T) + 4
    m = np.zeros((128, MASKS), np.float32)
    c = np.zeros((128, C_KI + n_tiles), np.float32)
    p = np.arange(128)[:, None]
    c[:, C_ID:C_ID + 128] = np.eye(128)
    c[:, C_BLK:C_BLK + 128] = p // LANES == np.arange(128)[None, :] // LANES
    m[:, M_UT:M_UT + 128] = p < np.arange(128)[None, :]
    key = np.arange(KW)[None, :]
    for v in range(3):
        q = p % QB
        keep = (key >= q) & (key <= q + PAD) & (key >= PAD - QB * v)
        m[:, M_MQ + KW * v:M_MQ + KW * (v + 1)] = np.where(keep, 0, NEG)
        k, q = p, np.arange(QB)[None, :]
        keep = (k >= q) & (k <= q + PAD) & (k >= PAD - QB * v)
        m[:, M_MT + QB * v:M_MT + QB * (v + 1)] = np.where(keep, 0, NEG)
    for j in range(3):
        c[:, C_VALID + j] = p[:, 0] < ROWS[j]
        c[:, C_TOK + j] = p[:, 0] + OFF[j]
    e = np.arange(EXPERTS)
    c[:, C_EOFF:C_EOFF + EXPERTS] = e * (nb * T + 128)
    c[:, C_W8:C_W8 + EXPERTS] = EXPERTS - e
    c[:, C_EI:C_EI + EXPERTS] = e
    c[0:PIX, C_CNT] = times
    c[:, C_KI:] = np.arange(n_tiles)
    return np.concatenate([m, c], 1)


def _numbers(np, nb):
    p, g = np.arange(128)[:, None], np.arange(3 * nb)[None, :]
    n = (g // 3 * T + np.array(OFF)[g % 3] + p - SKIP).astype(np.float32)
    return np.tile(n.reshape(LANES, SPAN * 3 * nb), (EXPERTS, 1))


def kernel(**inputs):
    import numpy as np
    import concourse.bacc as bacc
    from concourse.bass_utils import run_bass_kernel_spmd

    a = {k: np.ascontiguousarray(v) for k, v in inputs.items()}
    nb = a["x"].shape[0]
    pix, rows, times = _layout(np)
    padded = np.pad(a["x"], ((0, 0), (0, 1), (1, 1), (1, 1)))
    side = 14
    cc = np.array([c for c, _, _ in pix])[:, None, None]
    yy = np.array([y for _, y, _ in pix])[:, None, None] + 16 * np.arange(side)[None, :, None]
    xx = np.array([x for _, _, x in pix])[:, None, None] + 16 * np.arange(side)[None, None, :]
    patches = padded[:, cc, yy, xx].reshape(nb, PIX, PCH, NPATCH)

    def shifted(w):
        w = np.concatenate([w, np.zeros((1,) + w.shape[1:], w.dtype)])
        return np.ascontiguousarray(np.moveaxis(w[rows].reshape((5, PIX, PCH) + w.shape[1:]), 0, 1))

    arrays = {
        "x": patches, "txt": a["txt"],
        "wtok": shifted(a["L0_tok_W"]), "gam": shifted(a["L0_tok_ln_gamma"]), "bet": shifted(a["L0_tok_ln_beta"]),
        "btok": a["L0_tok_b"], "wattn": a["L0_attn_W_attn"], "battn": a["L0_attn_b_attn"],
        "wproj": a["L0_attn_W_proj"], "bproj": a["L0_attn_b_proj"], "wsw": a["L0_ffn_switch_w"],
        "bsw": a["L0_ffn_switch_b"], "w1": a["L0_ffn_w1"], "b1": a["L0_ffn_b1"], "w2": a["L0_ffn_w2"],
        "b2": a["L0_ffn_b2"], "const": _constants(np, nb, times), "numbers": _numbers(np, nb),
    }
    nc = bacc.Bacc("TRN2", target_bir_lowering=False, num_devices=1)
    args = [nc.dram_tensor("in_" + n, arrays[n].shape, mybir.dt.from_np(arrays[n].dtype), kind="ExternalInput").ap()
            for n in _INS]
    out = nc.dram_tensor("out_0_dram", (nb * T, D), F32, kind="ExternalOutput").ap()
    build(nc, *args, out)
    r = run_bass_kernel_spmd(nc, [{"in_" + n: arrays[n] for n in _INS}], core_ids=[0])
    return r.results[0]["out_0_dram"].reshape(nb, T, D)
```
